# Optimizing a Trainium2 kernel written in Bass

```python
import numpy as np
import jax
import jax.numpy as jnp

def _softmax(x, axis=-1):
    return jax.nn.softmax(x, axis=axis)

def _gelu(x):
    return jax.nn.gelu(x, approximate=True)

def _silu(x):
    return jax.nn.silu(x)

def _sigmoid(x):
    return jax.nn.sigmoid(x)

def _layernorm(x, axis=-1, eps=1e-05):
    m = jnp.mean(x, axis=axis, keepdims=True)
    v = jnp.var(x, axis=axis, keepdims=True)
    return (x - m) / jnp.sqrt(v + eps)

def _scatter_add(tgt, idx, src, axis=0):
    return tgt.at[idx].add(src)

def _segment_sum(src, seg, n):
    return jax.ops.segment_sum(src, seg, n)
kernel_name = 'mk_decoder_postln_d1_seqx_r4_3dcf20'

def setup_inputs(seed: int=0):
    np.random.seed(seed)
    _w = jnp.asarray

    def _rec_inputs():
        import jax
        import jax.numpy as jnp
        _rk = jax.random.key(seed)
        x = 7.22e-05 + 1 * jax.random.normal(jax.random.fold_in(_rk, 1), (128, 128, 256), jnp.float32)
        _lenS = 128 - jax.random.randint(jax.random.fold_in(_rk, 7), (128,), 0, max(1, 128 // 4) + 1, jnp.int32)
        _lenS2 = 128 - jax.random.randint(jax.random.fold_in(_rk, 8), (128,), 0, max(1, 128 // 4) + 1, jnp.int32)
        _ctx_768P = jax.random.normal(jax.random.fold_in(_rk, 11), (128, 16, 192), jnp.float32)
        _ctx_768c = jax.random.dirichlet(jax.random.fold_in(_rk, 511), 0.3 * jnp.ones((16,), jnp.float32), (128, 128))
        _ctx_768t = jnp.einsum('bsk,bkd->bsd', _ctx_768c, _ctx_768P)
        _ctx_768t = _ctx_768t * jax.lax.rsqrt(jnp.mean(jnp.square(_ctx_768t)) + 1e-12) * 0.953939
        ctx_768 = 3.88148e-05 + 0.999967 * (_ctx_768t + 0.3 * jax.random.normal(jax.random.fold_in(_rk, 611), (128, 128, 192), jnp.float32))
        _validS = jnp.arange(128)[None, :] < _lenS[:, None]
        _validS2 = jnp.arange(128)[None, :] < _lenS2[:, None]
        _causal = jnp.tril(jnp.ones((128, 128), dtype=bool))
        mask_BxS_bf1 = jnp.ones((128, 128), dtype=bool)
        mask_BxS2_bf1 = jnp.ones((128, 128), dtype=bool)
        return (x, ctx_768, mask_BxS_bf1, mask_BxS2_bf1)
    x, ctx_768, mask_BxS_bf1, mask_BxS2_bf1 = _rec_inputs()

    def _L0_attn_setup():
        import jax, jax.numpy as jnp
        import numpy as np
        from jax import lax
        B, L, D_MODEL = (2, 256, 256)
        D_INNER, D_STATE, D_CONV = (512, 16, 4)
        DT_RANK = 64
        key = jax.random.key(seed)
        ks = jax.random.split(key, 10)
        s = lambda k, shp, sc=0.02: jax.random.normal(k, shp, jnp.float32) * sc
        A = jnp.tile(jnp.arange(1, D_STATE + 1, dtype=jnp.float32), (D_INNER, 1))
        return {'x': s(ks[0], (B, L, D_MODEL), 1.0), 'in_proj_w': s(ks[1], (2 * D_INNER, D_MODEL)), 'conv_w': s(ks[2], (D_INNER, 1, D_CONV), 0.1), 'conv_b': s(ks[3], (D_INNER,), 0.1), 'x_proj_w': s(ks[4], (DT_RANK + 2 * D_STATE, D_INNER)), 'dt_proj_w': s(ks[5], (D_INNER, DT_RANK), 0.1), 'dt_proj_b': s(ks[6], (D_INNER,), 0.1), 'A_log': jnp.log(A), 'D': jnp.ones((D_INNER,), jnp.float32), 'out_proj_w': s(ks[7], (D_MODEL, D_INNER))}
    _L0_attn_all = _L0_attn_setup()
    _L0_attn_in = {k: v for k, v in _L0_attn_all.items() if k in ('in_proj_w', 'conv_w', 'conv_b', 'x_proj_w', 'dt_proj_w', 'dt_proj_b', 'A_log', 'D', 'out_proj_w')}
    del _L0_attn_all

    def _L0_xattn_setup():
        import jax, jax.numpy as jnp
        import numpy as np
        B, T, DT, G, DV = (16, 128, 256, 144, 192)
        H, DH = (4, 32)
        INNER = H * DH
        HID = 4 * DT
        N_STATE = 64
        K_TOP = 32

        def layernorm(x, g, b, eps=1e-05):
            m = x.mean(-1, keepdims=True)
            v = x.var(-1, keepdims=True)
            return (x - m) * jax.lax.rsqrt(v + eps) * g + b

        def s4d(x, log_dt, A_re, A_im, C_re, C_im, D_skip):
            Bb, L, D = x.shape
            dt = jnp.exp(log_dt)
            A = A_re + 1j * A_im
            C = C_re + 1j * C_im
            dtA = dt[:, None] * A
            dC = C * (jnp.exp(dtA) - 1.0) / A
            powers = jnp.exp(dtA[:, :, None] * jnp.arange(L))
            K = 2.0 * jnp.einsum('dn,dnl->dl', dC, powers).real
            n = 2 * L
            Kf = jnp.fft.rfft(K, n=n, axis=-1)
            xf = jnp.fft.rfft(x, n=n, axis=1)
            y = jnp.fft.irfft(xf * Kf.T[None], n=n, axis=1)[:, :L]
            return y + x * D_skip
        key = jax.random.key(seed)
        ks = jax.random.split(key, 16)
        s = 0.02
        inp = {'x_text': jax.random.normal(ks[0], (B, T, DT), jnp.float32), 'x_vision': jax.random.normal(ks[1], (B, G, DV), jnp.float32), 'text_mask': jnp.ones((B, T), bool), 'vision_mask': jnp.ones((B, G), bool), 'Wq': jax.random.normal(ks[2], (DT, INNER), jnp.float32) * s, 'Wk': jax.random.normal(ks[3], (DV, INNER), jnp.float32) * s, 'Wv': jax.random.normal(ks[4], (DV, DT), jnp.float32) * s, 'W_film_in': jax.random.normal(ks[5], (DT, 2 * DT), jnp.float32) * s, 'b_film_in': jnp.zeros((2 * DT,), jnp.float32), 'W_film_out': jax.random.normal(ks[6], (DT, 2 * DT), jnp.float32) * s, 'b_film_out': jnp.zeros((2 * DT,), jnp.float32), 'g_norm_in': jnp.ones((DT,), jnp.float32), 'b_norm_in': jnp.zeros((DT,), jnp.float32), 'g_norm_out': jnp.ones((DT,), jnp.float32), 'b_norm_out': jnp.zeros((DT,), jnp.float32), 'g_ffn': jnp.ones((DT,), jnp.float32), 'b_ffn': jnp.zeros((DT,), jnp.float32), 'W1': jax.random.normal(ks[7], (DT, HID), jnp.float32) * s, 'b1': jnp.zeros((HID,), jnp.float32), 'W2': jax.random.normal(ks[8], (HID, DT), jnp.float32) * s, 'b2': jnp.zeros((DT,), jnp.float32), 'log_dt': jnp.log(0.001) + jax.random.uniform(ks[9], (DT,), jnp.float32) * (jnp.log(0.1) - jnp.log(0.001)), 'A_re': -0.5 * jnp.ones((DT, N_STATE), jnp.float32), 'A_im': jnp.tile(jnp.pi * jnp.arange(N_STATE, dtype=jnp.float32), (DT, 1)), 'C_re': jax.random.normal(ks[10], (DT, N_STATE), jnp.float32) * 0.5 ** 0.5, 'C_im': jax.random.normal(ks[11], (DT, N_STATE), jnp.float32) * 0.5 ** 0.5, 'D_skip': jax.random.normal(ks[12], (DT,), jnp.float32), 'mod_gate': jnp.array(0.5, jnp.float32)}
        return inp
    _L0_xattn_all = _L0_xattn_setup()
    _L0_xattn_in = {k: v for k, v in _L0_xattn_all.items() if k in ('Wq', 'Wk', 'Wv', 'W_film_in', 'b_film_in', 'W_film_out', 'b_film_out', 'g_norm_in', 'b_norm_in', 'g_norm_out', 'b_norm_out', 'g_ffn', 'b_ffn', 'W1', 'b1', 'W2', 'b2', 'log_dt', 'A_re', 'A_im', 'C_re', 'C_im', 'D_skip', 'mod_gate')}
    del _L0_xattn_all

    def _L0_ffn_setup():
        import jax, jax.numpy as jnp
        import numpy as np
        B, S, D = (4, 512, 256)
        P = 9
        DM = D // 4
        EPS = 1e-05

        def _mix(x, mix_kernel):
            xp = jnp.pad(x, ((0, 0), (1, 1), (0, 0)))
            return mix_kernel[0] * xp[:, :-2] + mix_kernel[1] * xp[:, 1:-1] + mix_kernel[2] * xp[:, 2:]

        def _layernorm(h, gamma, beta):
            mu = jnp.mean(h, axis=-1, keepdims=True)
            var = jnp.var(h, axis=-1, keepdims=True)
            return (h - mu) * jax.lax.rsqrt(var + EPS) * gamma + beta
        key = jax.random.key(seed)
        ks = jax.random.split(key, 12)
        sc_in = 1.0 / np.sqrt(D)
        sc_mid = 1.0 / np.sqrt(DM)
        return {'x': jax.random.normal(ks[0], (B, S, D), dtype=jnp.float32), 'mix_kernel': jax.random.normal(ks[1], (3, D), dtype=jnp.float32) * 0.5, 'W1': jax.random.normal(ks[2], (P, D, DM), dtype=jnp.float32) * sc_in, 'b1': jnp.zeros((P, DM), dtype=jnp.float32), 'W2': jax.random.normal(ks[3], (P, DM, D), dtype=jnp.float32) * sc_mid, 'b2': jnp.zeros((P, D), dtype=jnp.float32), 'Wo1': jax.random.normal(ks[4], (D, DM), dtype=jnp.float32) * sc_in, 'bo1': jnp.zeros((DM,), dtype=jnp.float32), 'Wo2': jax.random.normal(ks[5], (DM, P), dtype=jnp.float32) * sc_mid, 'bo2': jnp.zeros((P,), dtype=jnp.float32), 'gamma': jnp.ones((D,), dtype=jnp.float32), 'beta': jnp.zeros((D,), dtype=jnp.float32)}
    _L0_ffn_all = _L0_ffn_setup()
    _L0_ffn_in = {k: v for k, v in _L0_ffn_all.items() if k in ('mix_kernel', 'W1', 'b1', 'W2', 'b2', 'Wo1', 'bo1', 'Wo2', 'bo2', 'gamma', 'beta')}
    del _L0_ffn_all
    return {'x': x, 'ctx_768': ctx_768, 'mask_BxS_bf1': mask_BxS_bf1, 'mask_BxS2_bf1': mask_BxS2_bf1, 'L0_attn_in_proj_w': _L0_attn_in['in_proj_w'], 'L0_attn_conv_w': _L0_attn_in['conv_w'], 'L0_attn_conv_b': _L0_attn_in['conv_b'], 'L0_attn_x_proj_w': _L0_attn_in['x_proj_w'], 'L0_attn_dt_proj_w': _L0_attn_in['dt_proj_w'], 'L0_attn_dt_proj_b': _L0_attn_in['dt_proj_b'], 'L0_attn_A_log': _L0_attn_in['A_log'], 'L0_attn_D': _L0_attn_in['D'], 'L0_attn_out_proj_w': _L0_attn_in['out_proj_w'], 'L0_xattn_Wq': _L0_xattn_in['Wq'], 'L0_xattn_Wk': _L0_xattn_in['Wk'], 'L0_xattn_Wv': _L0_xattn_in['Wv'], 'L0_xattn_W_film_in': _L0_xattn_in['W_film_in'], 'L0_xattn_b_film_in': _L0_xattn_in['b_film_in'], 'L0_xattn_W_film_out': _L0_xattn_in['W_film_out'], 'L0_xattn_b_film_out': _L0_xattn_in['b_film_out'], 'L0_xattn_g_norm_in': _L0_xattn_in['g_norm_in'], 'L0_xattn_b_norm_in': _L0_xattn_in['b_norm_in'], 'L0_xattn_g_norm_out': _L0_xattn_in['g_norm_out'], 'L0_xattn_b_norm_out': _L0_xattn_in['b_norm_out'], 'L0_xattn_g_ffn': _L0_xattn_in['g_ffn'], 'L0_xattn_b_ffn': _L0_xattn_in['b_ffn'], 'L0_xattn_W1': _L0_xattn_in['W1'], 'L0_xattn_b1': _L0_xattn_in['b1'], 'L0_xattn_W2': _L0_xattn_in['W2'], 'L0_xattn_b2': _L0_xattn_in['b2'], 'L0_xattn_log_dt': _L0_xattn_in['log_dt'], 'L0_xattn_A_re': _L0_xattn_in['A_re'], 'L0_xattn_A_im': _L0_xattn_in['A_im'], 'L0_xattn_C_re': _L0_xattn_in['C_re'], 'L0_xattn_C_im': _L0_xattn_in['C_im'], 'L0_xattn_D_skip': _L0_xattn_in['D_skip'], 'L0_xattn_mod_gate': _L0_xattn_in['mod_gate'], 'L0_ffn_mix_kernel': _L0_ffn_in['mix_kernel'], 'L0_ffn_W1': _L0_ffn_in['W1'], 'L0_ffn_b1': _L0_ffn_in['b1'], 'L0_ffn_W2': _L0_ffn_in['W2'], 'L0_ffn_b2': _L0_ffn_in['b2'], 'L0_ffn_Wo1': _L0_ffn_in['Wo1'], 'L0_ffn_bo1': _L0_ffn_in['bo1'], 'L0_ffn_Wo2': _L0_ffn_in['Wo2'], 'L0_ffn_bo2': _L0_ffn_in['bo2'], 'L0_ffn_gamma': _L0_ffn_in['gamma'], 'L0_ffn_beta': _L0_ffn_in['beta']}

def reference(x, ctx_768, mask_BxS_bf1, mask_BxS2_bf1, L0_attn_in_proj_w, L0_attn_conv_w, L0_attn_conv_b, L0_attn_x_proj_w, L0_attn_dt_proj_w, L0_attn_dt_proj_b, L0_attn_A_log, L0_attn_D, L0_attn_out_proj_w, L0_xattn_Wq, L0_xattn_Wk, L0_xattn_Wv, L0_xattn_W_film_in, L0_xattn_b_film_in, L0_xattn_W_film_out, L0_xattn_b_film_out, L0_xattn_g_norm_in, L0_xattn_b_norm_in, L0_xattn_g_norm_out, L0_xattn_b_norm_out, L0_xattn_g_ffn, L0_xattn_b_ffn, L0_xattn_W1, L0_xattn_b1, L0_xattn_W2, L0_xattn_b2, L0_xattn_log_dt, L0_xattn_A_re, L0_xattn_A_im, L0_xattn_C_re, L0_xattn_C_im, L0_xattn_D_skip, L0_xattn_mod_gate, L0_ffn_mix_kernel, L0_ffn_W1, L0_ffn_b1, L0_ffn_W2, L0_ffn_b2, L0_ffn_Wo1, L0_ffn_bo1, L0_ffn_Wo2, L0_ffn_bo2, L0_ffn_gamma, L0_ffn_beta):
    import jax
    import jax.numpy as jnp

    def _L0_attn_ref(x, in_proj_w, conv_w, conv_b, x_proj_w, dt_proj_w, dt_proj_b, A_log, D, out_proj_w):
        import jax, jax.numpy as jnp
        import numpy as np
        from jax import lax
        B, L, D_MODEL = (2, 256, 256)
        D_INNER, D_STATE, D_CONV = (512, 16, 4)
        DT_RANK = 64
        b, l, _ = x.shape
        d_inner, d_state = A_log.shape
        dt_rank = dt_proj_w.shape[1]
        d_conv = conv_w.shape[-1]
        xz = jnp.einsum('bld,ed->ble', x, in_proj_w)
        xc, z = jnp.split(xz, 2, axis=-1)
        xt = xc.transpose(0, 2, 1)
        xt = lax.conv_general_dilated(xt, conv_w, window_strides=(1,), padding=[(d_conv - 1, 0)], feature_group_count=d_inner, dimension_numbers=('NCH', 'OIH', 'NCH'))
        xt = xt + conv_b[None, :, None]
        xs = jax.nn.silu(xt.transpose(0, 2, 1))
        x_dbl = jnp.einsum('bld,rd->blr', xs, x_proj_w)
        dt, Bm, Cm = jnp.split(x_dbl, [dt_rank, dt_rank + d_state], axis=-1)
        dt = jax.nn.softplus(jnp.einsum('blr,dr->bld', dt, dt_proj_w) + dt_proj_b)
        A = -jnp.exp(A_log)
        deltaA = jnp.exp(dt[..., None] * A)
        deltaBx = dt[..., None] * Bm[:, :, None, :] * xs[..., None]

        def step(h, inputs):
            dA, dBx, c = inputs
            h = dA * h + dBx
            y = jnp.einsum('bdn,bn->bd', h, c)
            return (h, y)
        h0 = jnp.zeros((b, d_inner, d_state), xs.dtype)
        _, ys = lax.scan(step, h0, (deltaA.transpose(1, 0, 2, 3), deltaBx.transpose(1, 0, 2, 3), Cm.transpose(1, 0, 2)))
        y = ys.transpose(1, 0, 2) + D * xs
        y = y * jax.nn.silu(z)
        return jnp.einsum('bld,ed->ble', y, out_proj_w)

    def _L0_xattn_ref(x_text, x_vision, text_mask, vision_mask, Wq, Wk, Wv, W_film_in, b_film_in, W_film_out, b_film_out, g_norm_in, b_norm_in, g_norm_out, b_norm_out, g_ffn, b_ffn, W1, b1, W2, b2, log_dt, A_re, A_im, C_re, C_im, D_skip, mod_gate):
        import jax, jax.numpy as jnp
        import numpy as np
        B, T, DT, G, DV = (16, 128, 256, 144, 192)
        H, DH = (4, 32)
        INNER = H * DH
        HID = 4 * DT
        N_STATE = 64
        K_TOP = 32

        def layernorm(x, g, b, eps=1e-05):
            m = x.mean(-1, keepdims=True)
            v = x.var(-1, keepdims=True)
            return (x - m) * jax.lax.rsqrt(v + eps) * g + b

        def s4d(x, log_dt, A_re, A_im, C_re, C_im, D_skip):
            Bb, L, D = x.shape
            dt = jnp.exp(log_dt)
            A = A_re + 1j * A_im
            C = C_re + 1j * C_im
            dtA = dt[:, None] * A
            dC = C * (jnp.exp(dtA) - 1.0) / A
            powers = jnp.exp(dtA[:, :, None] * jnp.arange(L))
            K = 2.0 * jnp.einsum('dn,dnl->dl', dC, powers).real
            n = 2 * L
            Kf = jnp.fft.rfft(K, n=n, axis=-1)
            xf = jnp.fft.rfft(x, n=n, axis=1)
            y = jnp.fft.irfft(xf * Kf.T[None], n=n, axis=1)[:, :L]
            return y + x * D_skip
        Bb, Tt, D = x_text.shape
        Gg = x_vision.shape[1]
        Q = (x_text @ Wq).reshape(Bb, Tt, H, DH)
        K = (x_vision @ Wk).reshape(Bb, Gg, H, DH)
        scores = jnp.einsum('bthd,bghd->bhtg', Q, K) / np.sqrt(DH).astype(np.float32)
        scores = jnp.where(vision_mask[:, None, None, :], scores, -jnp.inf)
        topv, topi = jax.lax.top_k(scores, K_TOP)
        probs = jax.nn.softmax(topv, axis=-1)
        bi = jnp.arange(Bb)[:, None, None, None]
        hi = jnp.arange(H)[None, :, None, None]
        ti = jnp.arange(Tt)[None, None, :, None]
        attn = jnp.zeros_like(scores).at[bi, hi, ti, topi].set(probs)
        attn_mean = attn.mean(axis=1)
        V = x_vision @ Wv
        c_t = jnp.einsum('btg,bgd->btd', attn_mean, V)
        c_t = c_t * text_mask[..., None]
        x = layernorm(x_text, g_norm_in, b_norm_in)
        scale_in, shift_in = jnp.split(c_t @ W_film_in + b_film_in, 2, axis=-1)
        x = x * (1.0 + mod_gate * scale_in) + mod_gate * shift_in
        y = s4d(x, log_dt, A_re, A_im, C_re, C_im, D_skip)
        scale_out, shift_out = jnp.split(c_t @ W_film_out + b_film_out, 2, axis=-1)
        y = y * (1.0 + mod_gate * scale_out) + mod_gate * shift_out
        xt = x_text + y
        h = layernorm(xt, g_ffn, b_ffn)
        h = jax.nn.gelu(h @ W1 + b1, approximate=False) @ W2 + b2
        xt = xt + h
        return layernorm(xt, g_norm_out, b_norm_out)

    def _L0_ffn_ref(x, mix_kernel, W1, b1, W2, b2, Wo1, bo1, Wo2, bo2, gamma, beta):
        import jax, jax.numpy as jnp
        import numpy as np
        B, S, D = (4, 512, 256)
        P = 9
        DM = D // 4
        EPS = 1e-05

        def _mix(x, mix_kernel):
            xp = jnp.pad(x, ((0, 0), (1, 1), (0, 0)))
            return mix_kernel[0] * xp[:, :-2] + mix_kernel[1] * xp[:, 1:-1] + mix_kernel[2] * xp[:, 2:]

        def _layernorm(h, gamma, beta):
            mu = jnp.mean(h, axis=-1, keepdims=True)
            var = jnp.var(h, axis=-1, keepdims=True)
            return (h - mu) * jax.lax.rsqrt(var + EPS) * gamma + beta
        x_mixed = _mix(x, mix_kernel)
        h = jnp.einsum('bsd,pdm->bspm', x_mixed, W1) + b1
        stacked_paths = jnp.einsum('bspm,pmd->bspd', h, W2) + b2
        scores = jnp.tanh(x_mixed @ Wo1 + bo1) @ Wo2 + bo2
        idx = jnp.argmax(scores, axis=-1)
        weights = jax.nn.one_hot(idx, P, dtype=stacked_paths.dtype)
        collapsed = jnp.einsum('bspd,bsp->bsd', stacked_paths, weights)
        return _layernorm(x + collapsed, gamma, beta)
    x = _layernorm(x + _L0_attn_ref(x, L0_attn_in_proj_w, L0_attn_conv_w, L0_attn_conv_b, L0_attn_x_proj_w, L0_attn_dt_proj_w, L0_attn_dt_proj_b, L0_attn_A_log, L0_attn_D, L0_attn_out_proj_w), axis=-1)
    x = _layernorm(x + _L0_xattn_ref(x, ctx_768, mask_BxS_bf1, mask_BxS2_bf1, L0_xattn_Wq, L0_xattn_Wk, L0_xattn_Wv, L0_xattn_W_film_in, L0_xattn_b_film_in, L0_xattn_W_film_out, L0_xattn_b_film_out, L0_xattn_g_norm_in, L0_xattn_b_norm_in, L0_xattn_g_norm_out, L0_xattn_b_norm_out, L0_xattn_g_ffn, L0_xattn_b_ffn, L0_xattn_W1, L0_xattn_b1, L0_xattn_W2, L0_xattn_b2, L0_xattn_log_dt, L0_xattn_A_re, L0_xattn_A_im, L0_xattn_C_re, L0_xattn_C_im, L0_xattn_D_skip, L0_xattn_mod_gate), axis=-1)
    x = _layernorm(x + _L0_ffn_ref(x, L0_ffn_mix_kernel, L0_ffn_W1, L0_ffn_b1, L0_ffn_W2, L0_ffn_b2, L0_ffn_Wo1, L0_ffn_bo1, L0_ffn_Wo2, L0_ffn_bo2, L0_ffn_gamma, L0_ffn_beta), axis=-1)
    return x

_drawn_inputs = setup_inputs


def setup_inputs(seed=0):
    import zlib

    import numpy as np

    out = dict(_drawn_inputs(seed))
    spreads = {'L0_attn_D': (1.0, 0.6),
     'L0_xattn_b_film_in': (0.0, 0.1),
     'L0_xattn_b_film_out': (0.0, 0.1),
     'L0_xattn_g_norm_in': (1.0, 0.2),
     'L0_xattn_b_norm_in': (0.0, 0.1),
     'L0_xattn_g_norm_out': (1.0, 0.2),
     'L0_xattn_b_norm_out': (0.0, 0.1),
     'L0_xattn_g_ffn': (1.0, 0.2),
     'L0_xattn_b_ffn': (0.0, 0.275),
     'L0_xattn_b1': (0.0, 0.1),
     'L0_xattn_b2': (0.0, 0.1),
     'L0_xattn_A_re': (-0.5, 0.2),
     'L0_ffn_b1': (0.0, 0.1),
     'L0_ffn_b2': (0.0, 0.1),
     'L0_ffn_bo1': (0.0, 0.1),
     'L0_ffn_bo2': (0.0, 0.1),
     'L0_ffn_gamma': (1.0, 0.2),
     'L0_ffn_beta': (0.0, 0.1)}
    factors = {'L0_attn_conv_w': 2.868,
     'L0_attn_x_proj_w': 8.0,
     'L0_attn_dt_proj_w': 8.0,
     'L0_attn_dt_proj_b': 23.041,
     'L0_attn_A_log': 28.393}
    for name, (base, spread) in spreads.items():
        noise = np.random.default_rng([zlib.crc32(name.encode()), seed]).standard_normal(out[name].shape)
        drawn = base * np.exp(spread * noise) if base else spread * noise
        out[name] = jnp.asarray(drawn.astype(out[name].dtype))
    for name, factor in factors.items():
        out[name] = (out[name] * factor).astype(out[name].dtype)
    return out
```

```python
from contextlib import ExitStack

import concourse.bass as bass
from concourse import mybir

ALU = mybir.AluOpType
ACT = mybir.ActivationFunctionType
AX = mybir.AxisListType
F32 = mybir.dt.float32
BF16 = mybir.dt.bfloat16
U8 = mybir.dt.uint8

P = 128
L = 128
D = 256
DH = D // P
DI = 512
C = DI // P
NS = 16
R = 64
G = 4
T = G * L
CTX = 192
CT2 = CTX - P
H = 4
HD = 32
TOPK = 32
KR = TOPK // 8
MOD = 1024
EPS = 1e-5
SM = 64
HID = 1024
NP_ = 9
DM = D // 4
RING = 8
NEG = -3.0e38
OFF = -1.0e30

V_CONVW, V_CONVB, V_DTB, V_D, V_ALOG = 0, 16, 20, 24, 28
V_B1, V_MIX, V_FB1, V_BO1, NV = 92, 100, 106, 111, 112
W_GIN, W_BIN, W_GFFN, W_BFFN, W_B2, W_GOUT, W_BOUT, W_GAM, W_BET = range(9)
NW = 9 * D + 1

PER = dict(
    ld_xT=16, ld_x=16, ld_ctxT=32, ld_ctx=16, ld_mask=32, st_x1=16, st_xa=32, st_xin=32,
    in_mm=8, xp_mm=1, dt_mm=4, conv0=4, tap=8, conv=4, xth=4, xs=4, zhalf=4, zth=4, zs=4,
    dtr=1, bc_hi=1, bc_r1=1, bc_mid=1, bc_cp=1, bcp=1, vabs=4, vrelu=4, vexp=4, vln=4,
    cor1=4, cor2=4, cor3=4, dt=4, u=4,
    bb_mm=16, bb_sb=16, cb_mm=64, decay=64, bx=64, scan=64, hc=64, nsum=64, y=4, yg=4,
    o_mm=2, res=2, st1=4, mv1=1, ve1=1, rs1=1, x1=4, st2=4, mv2=1, ve2=1, rs2=1, xn0=4,
    xn1=1, xn2=1, tmb=1, xt_mm=2, x1T=2, q_mm=1, k_mm=1, qT=1, kT=1, maskb=1, s_mm=16, smask=4,
    v8=4 * KR, took=4 * KR, nmax=4, ex=4, em=4, rinv=4, rq=4, diag=4, at_mm=4, atT=4,
    xa_mm=2, xaT0=1, xaT1=1, film_mm=4, film_mul=4, film=4,
)

FRONT = ["xc0", "xc1", "xc2", "xc3", "z0", "z1", "z2", "z3", "xp", "dt0", "dt1", "dt2", "dt3", "ln",
         "sp0", "sp1", "sp2", "sp3"]
BACK = (["y3", "oproj", "ln1", "mask", "x1", "x1T", "qk", "xn"]
        + [s + str(b) for b in range(G) for s in ("sc", "tka", "tkb", "tkc", "tkd", "sm", "at")]
        + ["xa", "film0", "film1", "film2", "film3"])
PE_AT = dict(xc0=0, xc1=1, xc2=3, xc3=4, oproj=7, z0=9, z1=10, z2=11, z3=12, x1T=14, qk=16,
             sc0=18, xp=19, dt0=21, dt1=22, dt2=23, dt3=24, at0=27, sc1=27, at1=35, sc2=35,
             at2=43, sc3=43, at3=51, xa=53, film0=55, film1=56, film2=58, film3=60)
ACT_AT = dict(xc0=1, xc1=2, xc2=4, xc3=5, z0=10, z1=11, z2=12, z3=13, x1T=15, qk=17,
              xp=20, dt0=22, dt1=23, dt2=24, sm0=24, dt3=25, at0=28, ln=29, sm1=33, at1=36,
              sm2=41, at2=44, sm3=49, at3=52, xa=54)
DVE_AT = dict(y3=1, xc0=2, xc1=3, xc2=5, xc3=6, ln1=8, x1=10, z0=12, z1=13, z2=14, z3=15, xn=17,
              sc0=19, tka0=20, xp=20, tkb0=21, tkc0=22, tkd0=23, sm0=25,
              sc1=28, tka1=29, tkb1=30, tkc1=31, tkd1=32, sm1=34,
              sc2=36, tka2=37, tkb2=38, tkc2=39, tkd2=40, sm2=42,
              sc3=44, tka3=45, tkb3=46, tkc3=47, tkd3=48, sm3=50,
              film0=56, film1=57, film2=59, film3=61)
POOL_AT = dict(y3=1, ln1=9, x1=11, mask=12, xn=18, sm0=26, sp0=28, sp1=31, sm1=34, sp2=37, sm2=42,
               sp3=44, sm3=50)


def steps_at(table, u, which):
    return [s for s, at in table.items() if at == u and s in which]


LAST_READ = dict(
    xc0=("conv", 1), xc1=("conv", 2), xc2=("conv", 3), xc3=("conv", 4),
    z0=("zth", 1), z1=("zth", 2), z2=("zth", 3), z3=("zth", 4), xp=("bc_r1", 1),
    dt0=("vrelu", 1), dt1=("vrelu", 2), dt2=("vrelu", 3), dt3=("vrelu", 4),
    o0=("res", 1), o1=("res", 2), t0=("x1T", 1), t1=("x1T", 2), q=("qT", 1), k=("kT", 1),
    s0=("smask", 1), s1=("smask", 2), s2=("smask", 3), s3=("smask", 4),
    a0=("atT", 1), a1=("atT", 2), a2=("atT", 3), a3=("atT", 4), xa0=("xaT0", 1), xa1=("xaT1", 1),
    f0=("film", 1), f1=("film", 2), f2=("film", 3), f3=("film", 4),
)
TILES = dict(oproj=["o0", "o1"], x1T=["t0", "t1"], qk=["q", "k"], xa=["xa0", "xa1"],
             **{f"sc{b}": [f"s{b}"] for b in range(G)}, **{f"at{b}": [f"a{b}"] for b in range(G)},
             **{f"film{b}": [f"f{b}"] for b in range(G)})
ORDER = [t for s in PE_AT for t in TILES.get(s, [s])]
BANK = {t: n % 2 for n, t in enumerate(ORDER)}


def is_front(tile):
    return tile in FRONT


def bank_before(tile, which):
    held = None
    for t in ORDER:
        if t == tile:
            return held
        if BANK[t] == BANK[tile] and is_front(t) in which:
            held = t
    return None


class Carve:

    def __init__(self, arena, start=0):
        self.arena, self.at = arena, start

    def f32(self, cols, rows=P):
        v = self.arena[0:rows, self.at:self.at + cols]
        self.at += cols
        assert self.at <= self.arena.shape[1], self.at
        return v

    def bf16(self, cols, rows=P):
        return self.f32((cols + 1) // 2, rows).bitcast(BF16)

    def u8(self, cols, rows=P):
        return self.f32((cols + 3) // 4, rows).bitcast(U8)


class Semaphores:

    def __init__(self, nc):
        self.nc, self.held = nc, []

    def named(self, name):
        self.held.append(self.nc.alloc_semaphore(name))
        return self.held[-1]

    def clear(self):
        self.nc.all_engine_barrier()
        self.nc.clear_and_free_semaphores(self.held)
        self.nc.all_engine_barrier()
        self.held = []


def decoder_layer(nc, i_, out, NB):
    B = NB * G
    x1_d = nc.dram_tensor("x1_scratch", [L, B, D], F32).ap()
    xa_d = nc.dram_tensor("xa_scratch", [CTX, B * L], F32).ap()
    xin_d = nc.dram_tensor("xin_scratch", [DH, L, B, P], F32).ap()
    y_d = nc.dram_tensor("y_scratch", [L, B, D], F32).ap()
    kr_d = nc.dram_tensor("kernel_scratch", [D, 2 * L], F32).ap()
    wf_d = nc.dram_tensor("film_scratch", [CTX + 1, MOD], F32).ap()
    with ExitStack() as ctx:
        arena = ctx.enter_context(nc.sbuf_tensor("arena", [P, 53200], F32))
        psum = ctx.enter_context(nc.psum_tensor("psum", [P, 8, 512], F32))
        sems = Semaphores(nc)
        setup(nc, sems, i_, arena, psum, kr_d, wf_d)
        sems.clear()
        pass1(nc, sems, i_, arena, psum, x1_d, xa_d, xin_d, wf_d, NB)
        sems.clear()
        pass2(nc, sems, arena, psum, xin_d, y_d, kr_d, B)
        sems.clear()
        pass3(nc, sems, i_, arena, psum, x1_d, xa_d, y_d, wf_d, out, NB)


def all_blocks(eng, iteration, NB):
    iteration(0, 0, True, False)
    if NB > 2:
        iteration(1, 1, True, True)
        if NB > 4:
            with eng.Fori(0, (NB - 4) // 2, 1) as q:
                iteration(q * 2 + 2, 0, True, True)
                iteration(q * 2 + 3, 1, True, True)
        iteration(NB - 2, 0, True, True)
    iteration(NB - 1, 1, False, True)


def identity(nc, eng, ident, sem):
    eng.memset(ident, 0.0).then_inc(sem, 1)
    eng.wait_ge(sem, 1)
    eng.affine_select(out=ident, in_=ident, compare_op=ALU.not_equal, fill=1.0, base=0,
                      pattern=[[-1, P]], channel_multiplier=1).then_inc(sem, 1)


def setup(nc, sems, i_, arena, psum, kr_d, wf_d):
    NE, NR, NG = 35, 16, 8
    TWO_PI = 6.283185307179586
    MAGIC = 12582912.0
    C1 = 6.28125
    C2 = 0.0019340515136718750
    C3 = TWO_PI - C1 - C2
    PI = 3.1415925
    with ExitStack() as ctx:
        def sem(n):
            return sems.named(n)
        loaded, film_mm, film_sb, film_st = sem("loaded"), sem("film_folded"), sem("film_gated"), sem("film_stored")
        consts, dve_step, dt_ready, mag_a = sem("s_consts"), sem("dve_step"), sem("dt_ready"), sem("mag_a")
        angles, sines, mags, tables, kmm, ksb, kst = (sem(n) for n in (
            "angles", "sines", "mags", "tables", "kernel_mm", "kernel_sb", "kernel_stored"))
        zero_st, bias_row, tanh_a = sem("zeros_ready"), sem("bias_row"), sem("tanh_a")
        cv = Carve(arena)
        wv = cv.f32(DH * CTX).rearrange("p (k c) -> p k c", k=DH)
        wf = cv.f32(DH * MOD).rearrange("p (k c) -> p k c", k=DH)
        fold0, fold1 = cv.f32(MOD), cv.f32(MOD, CT2)
        brow = cv.f32(MOD, 1)
        gate = cv.f32(1)
        s4 = cv.f32(4 * D).rearrange("p (a d) -> p a d", a=4)
        are, aim, cre, cim = (s4[:, k] for k in range(4))
        dt = cv.f32(D)
        a, b = cv.f32(D), cv.f32(D)
        tab = cv.f32(NE * D).rearrange("p (e d) -> p e d", e=NE)
        turns = cv.f32(NE * D).rearrange("p (e d) -> p e d", e=NE)
        mag = cv.f32((NR + NG) * D).rearrange("p (e d) -> p e d", e=NR + NG)
        tmp = [cv.f32(D) for _ in range(8)]
        ph = cv.f32(5)
        drow = cv.f32(16 * D, 1).rearrange("p (d j) -> p d j", j=16)
        last8 = cv.f32(8, 1)
        ksbuf = cv.f32(16 * D, 8)
        zeros = cv.f32(2 * L)
        dsk = cv.f32(D, 1)
        block = ctx.enter_context(nc.Block())

        @block.sync
        def _(sp):
            for dst, src in (
                (wv, i_["wv"]), (wf, i_["wf"]), (brow, i_["film_b"]),
                (gate, i_["wide"][0:1, NW - 1:NW].to_broadcast([P, 1])),
                (s4[0:SM], i_["s4"]), (s4[SM:P], i_["s4"]), (dt, i_["log_dt"].to_broadcast([P, D])), (dsk, i_["d_skip"]),
            ):
                sp.dma_start(dst, src).then_inc(loaded, 16)
            sp.wait_ge(film_sb, 4)
            sp.dma_start(wf_d[0:P], fold0).then_inc(film_st, 16)
            sp.dma_start(wf_d[P:CTX], fold1).then_inc(film_st, 16)
            sp.wait_ge(bias_row, 3)
            sp.dma_start(wf_d[CTX:CTX + 1], brow).then_inc(film_st, 16)
            sp.wait_ge(zero_st, 1)
            sp.dma_start(kr_d.rearrange("(h p) j -> p h j", p=P)[:, :, L:2 * L],
                         zeros.rearrange("p (h j) -> p h j", h=DH)).then_inc(kst, 16)
            sp.wait_ge(ksb, 8)
            for k in range(NG):
                sp.dma_start(kr_d[:, 16 * k:16 * k + 16][None], ksbuf[k:k + 1].rearrange("p (d j) -> p d j", j=16))\
                  .then_inc(kst, 16)
            sp.wait_ge(film_st, 48)
            sp.wait_ge(kst, 16 * (NG + 1))

        @block.gpsimd
        def _(pool):
            pool.memset(zeros, 0.0).then_inc(zero_st, 1)
        @block.tensor
        def _(pe):
            pe.wait_ge(loaded, 128)
            for n, (lo, hi) in enumerate(((0, P), (P, CTX))):
                for half in range(2):
                    for k in range(DH):
                        mm = pe.matmul(psum[0:hi - lo, 2 * n + half], wv[:, k, lo:hi],
                                       wf[:, k, half * 512:(half + 1) * 512], start=k == 0, stop=k == DH - 1)
                    mm.then_inc(film_mm, 1)
            pe.wait_ge(film_sb, 4)
            pe.wait_ge(consts, 14)
            pe.wait_ge(tables, 1)
            for q in range(8):
                for dd in range(32):
                    d = 32 * q + dd
                    o = psum[0:8, q, 16 * dd:16 * dd + 16]
                    pe.matmul(o, tab[:, NR:NR + NG, d], tab[:, 0:NR, d], start=True, stop=False)
                    mm = pe.matmul(o, last8, drow[:, d], start=False, stop=True)
                mm.then_inc(kmm, 1)

        @block.scalar
        def _(act):
            act.wait_ge(loaded, 128)
            act.activation(dt, dt, ACT.Exp).then_inc(dt_ready, 1)
            act.wait_ge(mag_a, 1)
            for e in range(NR):
                act.activation(mag[:, e], a, ACT.Exp, scale=float(NR - 1 - e)).then_inc(mags, 1)
            for e in range(NG):
                act.activation(mag[:, NR + e], a, ACT.Exp, scale=float(16 * (NG - 1 - e))).then_inc(mags, 1)
            act.activation(tmp[0], a, ACT.Tanh, scale=0.5).then_inc(tanh_a, 1)
            for n in range(4):
                rows, dst = (P, fold0) if n < 2 else (CT2, fold1)
                act.wait_ge(film_mm, n + 1)
                act.activation(dst[0:rows, (n % 2) * 512:(n % 2) * 512 + 512], psum[0:rows, n], ACT.Identity,
                               scale=gate[0:rows]).then_inc(film_sb, 1)
            act.activation(brow, brow, ACT.Identity, scale=gate[0:1]).then_inc(bias_row, 1)
            for half in range(2):
                act.wait_ge(bias_row, half + 1)
                act.activation(brow[:, half * 512:half * 512 + D], brow[:, half * 512:half * 512 + D],
                               ACT.Identity, bias=1.0).then_inc(bias_row, 1)
            act.wait_ge(angles, 1)
            act.activation(tab, tab, ACT.Sin).then_inc(sines, 1)
            for q in range(8):
                act.wait_ge(kmm, q + 1)
                act.copy(ksbuf[:, 512 * q:512 * q + 512], psum[0:8, q]).then_inc(ksb, 1)

        @block.vector
        def _(dve):
            count = [0]

            def link(ins):
                ins.then_inc(dve_step, 1)
                count[0] += 1
                dve.wait_ge(dve_step, count[0])

            def tt(o, x, y, op):
                link(dve.tensor_tensor(o, x, y, op))

            dve.memset(ph[0:SM, 0:1], TWO_PI / 4).then_inc(consts, 1)
            dve.memset(ph[SM:P, 0:1], 0.0).then_inc(consts, 1)
            dve.memset(ph[0:SM, 1:2], 0.0).then_inc(consts, 1)
            dve.memset(ph[SM:P, 1:2], TWO_PI / 4).then_inc(consts, 1)
            dve.memset(ph[0:SM, 2:3], 0.25).then_inc(consts, 1)
            dve.memset(ph[SM:P, 2:3], 0.0).then_inc(consts, 1)
            dve.memset(ph[0:SM, 3:4], 0.0).then_inc(consts, 1)
            dve.memset(ph[SM:P, 3:4], 0.25).then_inc(consts, 1)
            dve.memset(ph[0:SM, 4:5], 2.0).then_inc(consts, 1)
            dve.memset(ph[SM:P, 4:5], -2.0).then_inc(consts, 1)
            dve.memset(drow, 0.0).then_inc(consts, 1)
            dve.memset(last8, 0.0).then_inc(consts, 1)
            dve.wait_ge(consts, 12)
            dve.memset(last8[:, 7:8], 1.0).then_inc(consts, 1)
            dve.wait_ge(loaded, 128)
            dve.tensor_copy(drow[:, :, 15], dsk).then_inc(consts, 1)
            dve.wait_ge(dt_ready, 1)
            dve.tensor_tensor(a, are, dt, ALU.mult).then_inc(mag_a, 1)
            tt(b, aim, dt, ALU.mult)
            exps = [NR - 1 - e for e in range(NR)] + [16 * (NG - 1 - e) for e in range(NG)] * 2 + [1, 1, 0.5]
            for e, x in enumerate(exps):
                last = dve.tensor_scalar(tab[:, e], b, float(x), None, ALU.mult)
            link(last)
            dve.wait_ge(consts, 14)
            groups = ((0, NR + NG, ph[:, 2:3], ph[:, 0:1]), (NR + NG, NR + 2 * NG, ph[:, 3:4], ph[:, 1:2]),
                      (NE - 3, NE - 2, 0.25, TWO_PI / 4), (NE - 2, NE, 0.0, 0.0))
            for lo, hi, turn, _ in groups:
                last = dve.tensor_scalar(turns[:, lo:hi], tab[:, lo:hi], 1 / TWO_PI, turn, ALU.mult, ALU.add)
            link(last)
            link(dve.tensor_scalar(turns, turns, MAGIC, -MAGIC, ALU.add, ALU.add))
            for part in (C1, C2, C3):
                flat = tab.rearrange("p e d -> p (e d)")
                link(dve.scalar_tensor_tensor(out=flat, in0=turns.rearrange("p e d -> p (e d)"), scalar=-part,
                                              in1=flat, op0=ALU.mult, op1=ALU.add))
            for lo, hi, _, phase in groups:
                last = dve.tensor_scalar(tab[:, lo:hi], tab[:, lo:hi], phase, PI, ALU.add, ALU.min)
            link(last)
            dve.tensor_scalar(tab, tab, -PI, None, ALU.max).then_inc(angles, 1)
            t, em, den, er, ei, x, qr, qi = tmp
            dve.wait_ge(tanh_a, 1)
            link(dve.tensor_scalar(em, t, -0.5, 0.5, ALU.mult, ALU.add))
            link(dve.reciprocal(em, em))
            tt(em, em, t, ALU.mult)
            tt(den, are, are, ALU.mult)
            tt(x, aim, aim, ALU.mult)
            tt(den, den, x, ALU.add)
            link(dve.reciprocal(den, den))
            dve.wait_ge(sines, 1)
            tt(x, tab[:, NE - 1], tab[:, NE - 1], ALU.mult)
            tt(er, em, tab[:, NE - 3], ALU.mult)
            link(dve.scalar_tensor_tensor(out=er, in0=x, scalar=-2.0, in1=er, op0=ALU.mult, op1=ALU.add))
            link(dve.scalar_tensor_tensor(out=ei, in0=em, scalar=1.0, in1=tab[:, NE - 2], op0=ALU.add, op1=ALU.mult))
            tt(qr, er, are, ALU.mult)
            tt(x, ei, aim, ALU.mult)
            tt(qr, qr, x, ALU.add)
            tt(qr, qr, den, ALU.mult)
            tt(qi, ei, are, ALU.mult)
            tt(x, er, aim, ALU.mult)
            tt(qi, qi, x, ALU.subtract)
            tt(qi, qi, den, ALU.mult)
            tt(er, cre, qr, ALU.mult)
            tt(x, cim, qi, ALU.mult)
            tt(er, er, x, ALU.subtract)
            tt(ei, cre, qi, ALU.mult)
            tt(x, cim, qr, ALU.mult)
            tt(ei, ei, x, ALU.add)
            link(dve.tensor_scalar(er, er, ph[:, 4:5], None, ALU.mult))
            link(dve.tensor_scalar(ei, ei, -2.0, None, ALU.mult))
            g0, g1 = tab[:, NR:NR + NG], tab[:, NR + NG:NR + 2 * NG]
            tt(g0, g0, er[:, None, :].to_broadcast([P, NG, D]), ALU.mult)
            tt(g1, g1, ei[:, None, :].to_broadcast([P, NG, D]), ALU.mult)
            tt(g0, g0, g1, ALU.add)
            dve.wait_ge(mags, NR + NG)
            tt(tab[:, 0:NR + NG], tab[:, 0:NR + NG], mag, ALU.mult)
            dve.memset(turns[:, 0, 0:1], 0.0).then_inc(tables, 1)

def pass1(nc, sems, i_, arena, psum, x1_d, xa_d, xin_d, wf_d, NB):
    with ExitStack() as ctx:
        S = {n: sems.named(n) for n in PER}
        w_ld = sems.named("w_ld")
        pool_step = sems.named("pool_step")
        bias_one = sems.named("bias_one")
        zeroed = sems.named("zeroed")
        alog_exp = sems.named("alog_exp")
        halved = sems.named("halved")

        cv = Carve(arena)
        win = cv.f32(DH * 2 * DI).rearrange("p (k e) -> p k e", k=DH)
        wxp = cv.f32(C * 96).rearrange("p (c r) -> p c r", c=C)
        wdt = cv.f32(DI, R)
        wout = cv.f32(C * D).rearrange("p (c d) -> p c d", c=C)
        wq = cv.f32(DH * P).rearrange("p (k e) -> p k e", k=DH)
        wk0, wk1 = cv.f32(P), cv.f32(P, CT2)
        wf0, wf1 = cv.f32(2 * D), cv.f32(2 * D, CT2 + 1)
        vec = cv.f32(NV)
        gb = cv.f32(2 * D)
        ident = cv.f32(P)
        sel3 = cv.bf16(2 * NS)
        negA = cv.f32(C * NS).rearrange("p (c n) -> p c n", c=C)
        half_w = cv.f32(20)
        nhalf = cv.f32(G)

        xT = cv.f32(DH * T).rearrange("p (k t) -> p k t", k=DH)
        x1 = cv.f32(G * D).rearrange("p (b d) -> p b d", b=G)
        ctxT0, ctxT1 = cv.f32(T), cv.f32(T, CT2)
        ctxn = cv.f32(G * CTX).rearrange("p (b d) -> p b d", b=G)
        mask8 = cv.u8(T)
        tmask8, tmb = cv.u8(G), cv.f32(G)
        maskb = cv.bf16(T).rearrange("p (b g) -> p b g", b=G)
        xs = [cv.f32(C * T).rearrange("p (c t) -> p c t", c=C) for _ in range(2)]
        zs = [cv.f32(C * T).rearrange("p (c t) -> p c t", c=C) for _ in range(2)]
        dt = [cv.f32(C * T).rearrange("p (c t) -> p c t", c=C) for _ in range(2)]
        uu = [cv.f32(C * T).rearrange("p (c t) -> p c t", c=C) for _ in range(2)]
        tmpA = cv.f32(C * T).rearrange("p (c t) -> p c t", c=C)
        tmpB = cv.f32(C * T).rearrange("p (c t) -> p c t", c=C)
        dtr_r1 = cv.f32(T)
        dtr, r1 = dtr_r1[0:R], dtr_r1[R:R + 2 * NS]
        mid = cv.bf16(T)[R:R + 2 * NS]
        bcp = [cv.bf16(T, 96) for _ in range(2)]
        Bb = cv.f32(NS * T).rearrange("p (n t) -> p n t", n=NS)
        ring = cv.f32(RING * T).rearrange("p (s t) -> p s t", s=RING)
        yg = cv.f32(C * T).rearrange("p (c t) -> p c t", c=C)
        xn = cv.f32(G * D).rearrange("p (b d) -> p b d", b=G)
        x1T = cv.f32(DH * T).rearrange("p (k t) -> p k t", k=DH)
        qT, kT = cv.f32(T), cv.f32(T)
        sc = cv.f32(H * P).rearrange("p (h g) -> p h g", h=H)
        left = cv.f32(H * P).rearrange("p (h g) -> p h g", h=H)
        diag = cv.f32(H * P).rearrange("p (h g) -> p h g", h=H)
        at = cv.f32(T).rearrange("p (b t) -> p b t", b=G)
        xa0, xa1 = cv.f32(T), cv.f32(T, CT2 + 1)
        stats = cv.f32(G * 6).rearrange("p (b s) -> p b s", b=G)
        mv = cv.f32(G * 2).rearrange("p (b s) -> p b s", b=G)
        ve, rs = cv.f32(G), cv.f32(G)
        v8 = cv.f32(KR * H * 8).rearrange("p (r h s) -> p r h s", r=KR, h=H)
        nmax, esum, rinv, rq = cv.f32(H), cv.f32(H), cv.f32(H), cv.f32(H)

        decay_ps, cb_ps = psum[:, 0:2], psum[:, 2:4]
        y_ps, bb_ps, side = psum[:, 4], psum[:, 5], psum[:, 6:8]

        def tile_ps(name):
            return side[:, BANK[name]]

        def seqs(v):
            return v.rearrange("p (b t) -> p b t", b=G)

        def need(eng, name, i, k):
            count = i * PER[name] + k
            if not isinstance(count, int) or count > 0:
                eng.wait_ge(S[name], count)

        def need_apart(eng, *what):
            counts = [(name, i * PER[name] + k) for name, i, k in what]
            counts = [(name, n if isinstance(n, int) else eng.to_reg(n)) for name, n in counts]
            eng.wait_ge(w_ld, 16 * N_W)
            for name, count in counts:
                if not isinstance(count, int) or count > 0:
                    eng.wait_ge(S[name], count)

        def which_steps(front, back):
            return (FRONT if front else []) + (BACK if back else [])

        N_W = 11
        block = ctx.enter_context(nc.Block())

        @block.sync
        def _(sp):
            for dst, src in (
                (win, i_["in_proj"]), (wxp, i_["x_proj"]), (wdt, i_["dt_proj"]), (wout, i_["out_proj"]),
                (wq, i_["wq"]), (wk0, i_["wk"][0:P]), (wk1, i_["wk"][P:CTX]),
                (wf0, wf_d[0:P, 0:2 * D]), (wf1, wf_d[P:CTX + 1, 0:2 * D]), (vec, i_["vec"]),
                (gb, i_["wide"][0:1, 0:2 * D].to_broadcast([P, 2 * D])),
            ):
                sp.dma_start(dst, src).then_inc(w_ld, 16)

            def load_xT(i):
                sp.dma_start(xT, i_["xT"][:, :, bass.ts(i, T)]).then_inc(S["ld_xT"], 16)

            def load_back(i):
                need(sp, "st_x1", i - 1, 16)
                need(sp, "xt_mm", i - 1, 2)
                need(sp, "xn0", i - 1, 4)
                sp.dma_start(x1, i_["x"][:, bass.ts(i, G), :]).then_inc(S["ld_x"], 16)
                need(sp, "k_mm", i - 1, 1)
                sp.dma_start(ctxT0, i_["ctxT"][0:P, bass.ts(i, T)]).then_inc(S["ld_ctxT"], 16)
                sp.dma_start(ctxT1, i_["ctxT"][P:CTX, bass.ts(i, T)]).then_inc(S["ld_ctxT"], 16)
                need(sp, "maskb", i - 1, 1)
                need(sp, "tmb", i - 1, 1)
                sp.dma_start(tmask8, i_["tmask"][:, bass.ts(i, G)]).then_inc(S["ld_mask"], 16)
                sp.dma_start(mask8, i_["vmask"][0:1, bass.ts(i, T)].to_broadcast([P, T])).then_inc(S["ld_mask"], 16)
                need(sp, "xa_mm", i - 1, 2)
                sp.dma_start(ctxn, i_["ctx"][:, bass.ts(i, G), :]).then_inc(S["ld_ctx"], 16)

            def store_x1(i):
                need(sp, "x1", i, 4)
                sp.dma_start(x1_d[:, bass.ts(i, G), :], x1).then_inc(S["st_x1"], 16)

            def store_rest(i):
                need(sp, "xaT0", i, 1)
                sp.dma_start(xa_d[0:P, bass.ts(i, T)], xa0).then_inc(S["st_xa"], 16)
                need(sp, "xaT1", i, 1)
                sp.dma_start(xa_d[P:CTX, bass.ts(i, T)], xa1[0:CT2]).then_inc(S["st_xa"], 16)

            def store_xin(i):
                need(sp, "film", i, G)
                for h in range(DH):
                    sp.dma_start(xin_d[h][:, bass.ts(i, G), :], xn[:, :, h * P:(h + 1) * P]).then_inc(S["st_xin"], 16)

            def iteration(i, ahead, back):
                if ahead:
                    need(sp, "in_mm", i + 1, 8)
                    load_xT(i + 2)
                if back:
                    store_x1(i - 1)
                if back:
                    store_rest(i - 1)
                load_back(i)
                if back:
                    store_xin(i - 1)

            load_xT(0)
            need(sp, "in_mm", 0, 8)
            load_xT(1)
            iteration(0, NB > 2, False)
            if NB > 2:
                iteration(1, True, True)
                if NB > 4:
                    with sp.Fori(2, NB - 2, 1) as i:
                        iteration(i, True, True)
                iteration(NB - 2, False, True)
            iteration(NB - 1, False, True)
            store_x1(NB - 1)
            store_rest(NB - 1)
            store_xin(NB - 1)
            for n in ("st_x1", "st_xa", "st_xin"):
                sp.wait_ge(S[n], NB * PER[n])

        @block.tensor
        def _(pe):
            def take_bank(name, i, i_other, which):
                prev = bank_before(name, which)
                if prev is not None:
                    j = i if is_front(prev) == is_front(name) else i_other
                    need(pe, LAST_READ[prev][0], j, LAST_READ[prev][1])
                    if prev == "xp":
                        need(pe, "dtr", j, 1)
                else:
                    f = i if is_front(name) else i_other
                    b = i_other if is_front(name) else i
                    need(pe, "vrelu", f - 1, C)
                    need(pe, "film", b - 1, G)

            def step(name, i, par, other, which):
                def bank(tile):
                    take_bank(tile, i, other, which)
                    return tile_ps(tile)

                if name[:2] == "xc" or name[0] == "z":
                    c = int(name[-1])
                    e0 = c * P + (DI if name[0] == "z" else 0)
                    ps = bank(name)
                    if name == "xc0":
                        need(pe, "ld_xT", i, 16)
                    for k in range(DH):
                        mm = pe.matmul(ps, win[:, k, e0:e0 + P], xT[:, k], start=k == 0, stop=k == DH - 1)
                    mm.then_inc(S["in_mm"], 1)
                elif name == "xp":
                    ps = bank(name)
                    need(pe, "xs", i, C)
                    for c in range(C):
                        mm = pe.matmul(ps[0:96], wxp[:, c], xs[par][:, c], start=c == 0, stop=c == C - 1)
                    mm.then_inc(S["xp_mm"], 1)
                elif name[:2] == "dt":
                    c = int(name[-1])
                    ps = bank(name)
                    if c == 0:
                        need(pe, "dtr", i, 1)
                    pe.matmul(ps, wdt[:, c * P:(c + 1) * P], dtr, start=True, stop=True).then_inc(S["dt_mm"], 1)
                elif name == "oproj":
                    for o in range(2):
                        ps = bank(f"o{o}")
                        if o == 0:
                            need(pe, "yg", i, C)
                        for bb in range(2):
                            b = 2 * o + bb
                            for c in range(C):
                                mm = pe.matmul(ps[:, bb * D:(bb + 1) * D], yg[:, c, b * L:(b + 1) * L],
                                               wout[:, c], start=c == 0, stop=c == C - 1)
                        mm.then_inc(S["o_mm"], 1)
                elif name == "x1T":
                    for k in range(DH):
                        ps = bank(f"t{k}")
                        if k == 0:
                            need(pe, "x1", i, G)
                        for b in range(G):
                            mm = pe.transpose(ps[:, b * L:(b + 1) * L], x1[:, b, k * P:(k + 1) * P], ident)
                        mm.then_inc(S["xt_mm"], 1)
                elif name == "qk":
                    ps = bank("q")
                    need(pe, "x1T", i, DH)
                    for k in range(DH):
                        mm = pe.matmul(ps, wq[:, k], x1T[:, k], start=k == 0, stop=k == DH - 1)
                    mm.then_inc(S["q_mm"], 1)
                    ps = bank("k")
                    need(pe, "ld_ctxT", i, 32)
                    pe.matmul(ps, wk0, ctxT0, start=True, stop=False)
                    pe.matmul(ps, wk1, ctxT1, start=False, stop=True).then_inc(S["k_mm"], 1)
                elif name[:2] == "sc":
                    b = int(name[-1])
                    ps = bank(f"s{b}")
                    if b == 0:
                        need(pe, "qT", i, 1)
                        need(pe, "kT", i, 1)
                    for h in range(H):
                        rows = slice(h * HD, (h + 1) * HD)
                        if h:
                            need(pe, "s_mm", i, b * H + h)
                        pe.matmul(ps[:, h * P:(h + 1) * P], qT[rows, b * L:(b + 1) * L],
                                  kT[rows, b * L:(b + 1) * L], start=True, stop=True).then_inc(S["s_mm"], 1)
                elif name[:2] == "at":
                    b = int(name[-1])
                    ps = bank(f"a{b}")
                    need(pe, "em", i, b + 1)
                    need(pe, "diag", i, b + 1)
                    for h in range(H):
                        mm = pe.matmul(ps[:, 0:L], sc[:, h], diag[:, h], start=h == 0, stop=h == H - 1)
                    mm.then_inc(S["at_mm"], 1)
                elif name == "xa":
                    for n, (lo, hi) in enumerate(((0, P), (P, CTX))):
                        ps = bank(f"xa{n}")
                        if n == 0:
                            need(pe, "atT", i, G)
                            need(pe, "ld_ctx", i, 16)
                        for b in range(G):
                            mm = pe.matmul(ps[0:hi - lo, b * L:(b + 1) * L], ctxn[:, b, lo:hi], at[:, b],
                                           start=True, stop=True)
                        mm.then_inc(S["xa_mm"], 1)
                elif name[:4] == "film":
                    b = int(name[-1])
                    ps = bank(f"f{b}")
                    if b == 0:
                        need(pe, "xaT0", i, 1)
                        need(pe, "xaT1", i, 1)
                    pe.matmul(ps, xa0[:, b * L:(b + 1) * L], wf0, start=True, stop=False)
                    pe.matmul(ps, xa1[0:CT2 + 1, b * L:(b + 1) * L], wf1, start=False, stop=True)\
                        .then_inc(S["film_mm"], 1)

            def spread_b(n, i, par):
                if n == 0:
                    need(pe, "bcp", i, 1)
                else:
                    need(pe, "bb_sb", i, n)
                pe.matmul(bb_ps, sel3[0:96, n:n + 1].to_broadcast([96, P]), bcp[par], start=True, stop=True)\
                    .then_inc(S["bb_mm"], 1)

            def sum_states(i, u):
                need(pe, "hc", i, u + 1)
                if u == 0:
                    need(pe, "y", i - 1, C)
                elif u % NS == 0:
                    need(pe, "y", i, u // NS)
                pe.matmul(y_ps, ident, ring[:, u % RING], start=u % NS == 0, stop=u % NS == NS - 1)\
                    .then_inc(S["nsum"], 1)

            def iteration(i, par, front, back):
                which = ([True] if front else []) + ([False] if back else [])
                names = which_steps(front, back)
                for n in range(3):
                    if n == 0:
                        need(pe, "bb_sb", i - 1, NS)
                    spread_b(n, i, par)
                for u in range(C * NS):
                    if 3 + u < NS:
                        spread_b(3 + u, i, par)
                    if u >= 2:
                        need(pe, "hc", i, u - 1)
                    else:
                        need(pe, "hc", i - 1, C * NS - 1 + u)
                    n = NS + u % NS
                    pe.matmul(cb_ps[:, u % 2], sel3[0:96, n:n + 1].to_broadcast([96, P]), bcp[par],
                              start=True, stop=True).then_inc(S["cb_mm"], 1)
                    if u >= 1:
                        sum_states(i, u - 1)
                    for s in steps_at(PE_AT, u, names):
                        if s in FRONT:
                            step(s, i + 1, 1 - par, i - 1, which)
                        else:
                            step(s, i - 1, 1 - par, i + 1, which)
                sum_states(i, C * NS - 1)

            pe.wait_ge(pool_step, 7)
            pe.wait_ge(bias_one, 1)
            pe.wait_ge(w_ld, 16 * N_W)
            for s in [s for s in PE_AT if s in FRONT]:
                step(s, 0, 0, 0, [True])
            all_blocks(pe, iteration, NB)
            for s in [s for s in PE_AT if s in BACK]:
                step(s, NB - 1, 1, NB, [False])

        @block.scalar
        def _(act):
            def step(name, i, par):
                c = int(name[-1]) if name[-1].isdigit() else 0
                if name[:2] == "xc":
                    need(act, "in_mm", i, c + 1)
                    if c == 0:
                        need(act, "y", i - 2, C)
                    act.activation(xs[par][:, c], tile_ps(name), ACT.Identity, bias=half_w[:, 16 + c:17 + c],
                                   scale=half_w[:, 4 * c + 3:4 * c + 4]).then_inc(S["conv0"], 1)
                elif name[0] == "z":
                    tanh_x(i, par, c)
                    need(act, "in_mm", i, C + c + 1)
                    if c == 0:
                        need(act, "yg", i - 2, C)
                    act.activation(zs[par][:, c], tile_ps(name), ACT.Identity, scale=0.5).then_inc(S["zhalf"], 1)
                    if c == 0:
                        need(act, "dt", i - 1, C)
                    act.activation(tmpA[:, c], tile_ps(name), ACT.Tanh, scale=0.5).then_inc(S["zth"], 1)
                elif name == "xp":
                    need(act, "xp_mm", i, 1)
                    need(act, "dt_mm", i - 1, C)
                    act.copy(dtr, tile_ps("xp")[0:R]).then_inc(S["dtr"], 1)
                elif name[:2] == "dt":
                    need(act, "dt_mm", i, c + 1)
                    need(act, "zs", i, c + 1)
                    act.activation(tmpA[:, c], tile_ps(name), ACT.Abs, bias=vec[:, V_DTB + c:V_DTB + c + 1])\
                        .then_inc(S["vabs"], 1)
                    act.activation(dt[par][:, c], tile_ps(name), ACT.Relu, bias=vec[:, V_DTB + c:V_DTB + c + 1])\
                        .then_inc(S["vrelu"], 1)
                    need(act, "vabs", i, c + 1)
                    act.activation(tmpA[:, c], tmpA[:, c], ACT.Exp, scale=-1.0).then_inc(S["vexp"], 1)
                elif name == "ln":
                    for c in range(C):
                        need(act, "vexp", i, c + 1)
                        need(act, "xs", i, c + 1)
                        act.activation(tmpB[:, c], tmpA[:, c], ACT.Ln, bias=1.0).then_inc(S["vln"], 1)
                elif name == "x1T":
                    for k in range(DH):
                        need(act, "xt_mm", i, k + 1)
                        if k == 0:
                            need(act, "q_mm", i - 1, 1)
                        act.copy(x1T[:, k], tile_ps(f"t{k}")).then_inc(S["x1T"], 1)
                elif name == "qk":
                    need(act, "q_mm", i, 1)
                    need(act, "s_mm", i - 1, G * H)
                    act.copy(qT, tile_ps("q")).then_inc(S["qT"], 1)
                    need(act, "k_mm", i, 1)
                    act.copy(kT, tile_ps("k")).then_inc(S["kT"], 1)
                elif name[:2] == "sm":
                    need(act, "nmax", i, c + 1)
                    need(act, "took", i, c * KR + 1)
                    for h in range(H):
                        a = act.activation(sc[:, h], sc[:, h], ACT.Exp, bias=nmax[:, h:h + 1], scale=HD ** -0.5)
                    a.then_inc(S["ex"], 1)
                elif name[:2] == "at":
                    need(act, "at_mm", i, c + 1)
                    if c == 0:
                        need(act, "xa_mm", i - 1, 2)
                    act.copy(at[:, c], tile_ps(f"a{c}")[:, 0:L]).then_inc(S["atT"], 1)
                elif name == "xa":
                    need(act, "xa_mm", i, 1)
                    need(act, "film_mm", i - 1, G)
                    need(act, "st_xa", i - 1, 32)
                    act.copy(xa0, tile_ps("xa0")).then_inc(S["xaT0"], 1)
                    need(act, "xa_mm", i, 2)
                    act.copy(xa1[0:CT2], tile_ps("xa1")[0:CT2]).then_inc(S["xaT1"], 1)

            def tanh_x(i, par, c):
                need(act, "conv", i, c + 1)
                if c == 0:
                    need(act, "dt", i - 1, C)
                act.activation(tmpB[:, c], xs[par][:, c], ACT.Tanh).then_inc(S["xth"], 1)

            def copy_b(n, i):
                need(act, "bb_mm", i, n + 1)
                if n == 0:
                    need(act, "bx", i - 1, C * NS)
                act.copy(Bb[:, n], bb_ps).then_inc(S["bb_sb"], 1)

            def iteration(i, par, front, back):
                names = which_steps(front, back)
                for n in range(3):
                    copy_b(n, i)
                for u in range(C * NS):
                    if 3 + u < NS:
                        copy_b(3 + u, i)
                    c, n = u // NS, u % NS
                    if n == 0:
                        need(act, "dt", i, c + 1)
                    if u >= 2:
                        need(act, "scan", i, u - 1)
                    else:
                        need(act, "scan", i - 1, C * NS - 1 + u)
                    act.activation(seqs(decay_ps[:, u % 2])[:, :, 1:L], seqs(dt[par][:, c])[:, :, 1:L],
                                   ACT.Exp, scale=negA[:, c, n:n + 1]).then_inc(S["decay"], 1)
                    for s in steps_at(ACT_AT, u, names):
                        if s in FRONT:
                            step(s, i + 1, 1 - par)
                        else:
                            step(s, i - 1, 1 - par)

            act.wait_ge(w_ld, 16 * N_W)
            act.activation(negA, vec[:, V_ALOG:V_ALOG + C * NS].rearrange("p (c n) -> p c n", c=C), ACT.Exp)\
                .then_inc(alog_exp, 1)
            act.wait_ge(alog_exp, 1)
            act.mul(negA, negA, -1.0).then_inc(alog_exp, 1)
            act.mul(half_w, vec[:, 0:20], 0.5).then_inc(halved, 1)
            act.wait_ge(alog_exp, 2)
            act.wait_ge(halved, 1)
            act.wait_ge(zeroed, 2)
            for s in [s for s in ACT_AT if s in FRONT]:
                step(s, 0, 0)
            all_blocks(act, iteration, NB)
            for s in [s for s in ACT_AT if s in BACK]:
                step(s, NB - 1, 1)

        @block.vector
        def _(dve):
            def norm_stats(i, src, st, mvn):
                for b in range(G):
                    dve.bn_stats(stats[:, b], src[:, b]).then_inc(S[st], 1)
                need_apart(dve, (st, i, G))
                for b in range(G):
                    a = dve.bn_aggr(mv[:, b], stats[:, b])
                a.then_inc(S[mvn], 1)

            def read_y(i, par, c):
                need(dve, "nsum", i, (c + 1) * NS)
                if c == 0:
                    need(dve, "o_mm", i - 1, 2)
                dve.scalar_tensor_tensor(out=yg[:, c], in0=xs[par][:, c], scalar=vec[:, V_D + c:V_D + c + 1],
                                         in1=y_ps, op0=ALU.mult, op1=ALU.add).then_inc(S["y"], 1)

            def step(name, i, par):
                c = int(name[-1]) if name[-1].isdigit() else 0
                if name[:2] == "xc":
                    need(dve, "conv0", i, c + 1)
                    for s in (1, 2, 3):
                        if s > 1:
                            need(dve, "tap", i, 2 * c + s - 1)
                        o = seqs(xs[par][:, c])[:, :, s:L]
                        dve.scalar_tensor_tensor(out=o, in0=seqs(tile_ps(name))[:, :, 0:L - s],
                                                 scalar=half_w[:, 4 * c + 3 - s:4 * c + 4 - s], in1=o,
                                                 op0=ALU.mult, op1=ALU.add)\
                           .then_inc(S["tap" if s < 3 else "conv"], 1)
                elif name[0] == "z":
                    need(dve, "xth", i, c + 1)
                    dve.scalar_tensor_tensor(out=xs[par][:, c], in0=tmpB[:, c], scalar=1.0, in1=xs[par][:, c],
                                             op0=ALU.add, op1=ALU.mult).then_inc(S["xs"], 1)
                    need(dve, "zth", i, c + 1)
                    dve.scalar_tensor_tensor(out=zs[par][:, c], in0=tmpA[:, c], scalar=1.0, in1=zs[par][:, c],
                                             op0=ALU.add, op1=ALU.mult).then_inc(S["zs"], 1)
                elif name == "xp":
                    rows = slice(R, R + 2 * NS)
                    ps = tile_ps("xp")[rows]
                    need(dve, "xp_mm", i, 1)
                    need(dve, "cb_mm", i - 2, C * NS)
                    dve.tensor_copy(bcp[par][rows], ps).then_inc(S["bc_hi"], 1)
                    need(dve, "bc_hi", i, 1)
                    dve.tensor_tensor(r1, ps, bcp[par][rows], ALU.subtract).then_inc(S["bc_r1"], 1)
                    need(dve, "bc_r1", i, 1)
                    dve.tensor_copy(mid, r1).then_inc(S["bc_mid"], 1)
                    dve.tensor_copy(bcp[par][NS * 2:NS * 4], r1).then_inc(S["bc_cp"], 1)
                    need(dve, "bc_mid", i, 1)
                    need(dve, "bc_cp", i, 1)
                    dve.tensor_tensor(bcp[par][0:NS * 2], r1, mid, ALU.subtract).then_inc(S["bcp"], 1)
                elif name == "y3":
                    read_y(i, par, C - 1)
                elif name == "ln1":
                    need(dve, "ld_x", i, 16)
                    for o in range(2):
                        need(dve, "o_mm", i, o + 1)
                        pair = x1[:, 2 * o:2 * o + 2]
                        dve.tensor_tensor(pair, tile_ps(f"o{o}").rearrange("p (b d) -> p b d", b=2), pair,
                                          ALU.add).then_inc(S["res"], 1)
                    need(dve, "res", i, 2)
                    need(dve, "ve2", i - 1, 1)
                    need(dve, "xn0", i - 1, G)
                    norm_stats(i, x1, "st1", "mv1")
                elif name == "x1":
                    need(dve, "rs1", i, 1)
                    need(dve, "mv1", i, 1)
                    for b in range(G):
                        dve.tensor_scalar(x1[:, b], x1[:, b], mv[:, b, 0:1], rs[:, b:b + 1],
                                          ALU.subtract, ALU.mult).then_inc(S["x1"], 1)
                    need(dve, "x1", i, G)
                    norm_stats(i, x1, "st2", "mv2")
                elif name == "xn":
                    need(dve, "rs2", i, 1)
                    need(dve, "mv2", i, 1)
                    need(dve, "st_xin", i - 1, 32)
                    for b in range(G):
                        dve.tensor_scalar(xn[:, b], x1[:, b], mv[:, b, 0:1], rs[:, b:b + 1],
                                          ALU.subtract, ALU.mult).then_inc(S["xn0"], 1)
                elif name[:2] == "sc":
                    b = c
                    need(dve, "s_mm", i, (b + 1) * H)
                    if b == 0:
                        need(dve, "maskb", i, 1)
                        need(dve, "at_mm", i - 1, G)
                    else:
                        need(dve, "at_mm", i, b)
                    dve.tensor_tensor(sc, tile_ps(f"s{b}").rearrange("p (h g) -> p h g", h=H),
                                      maskb[:, b:b + 1].to_broadcast([P, H, P]), ALU.add).then_inc(S["smask"], 1)
                elif name[:2] == "tk":
                    b, r = c, "abcd".index(name[2])
                    src = left if r else sc
                    n = b * KR + r
                    if r:
                        need_apart(dve, ("took", i, n))
                    else:
                        need_apart(dve, ("smask", i, b + 1))
                    for h in range(H):
                        a = dve.max(v8[:, r, h], src[:, h])
                    a.then_inc(S["v8"], 1)
                    need_apart(dve, ("v8", i, n + 1))
                    for h in range(H):
                        a = dve.match_replace(left[:, h], v8[:, r, h], src[:, h], NEG)
                    a.then_inc(S["took"], 1)
                    if r == 0:
                        if b:
                            need(dve, "ex", i, b)
                        dve.tensor_scalar(nmax, v8[:, 0, :, 0], -HD ** -0.5, None, ALU.mult).then_inc(S["nmax"], 1)
                elif name[:2] == "sm":
                    b = c
                    need(dve, "ex", i, b + 1)
                    need(dve, "took", i, (b + 1) * KR)
                    for h in range(H):
                        a = dve.scalar_tensor_tensor(out=sc[:, h], in0=left[:, h], scalar=NEG / 2, in1=sc[:, h],
                                                     op0=ALU.is_lt, op1=ALU.mult, accum_out=esum[:, h:h + 1])
                    a.then_inc(S["em"], 1)
                    need(dve, "em", i, b + 1)
                    dve.reciprocal(rinv, esum).then_inc(S["rinv"], 1)
                    need(dve, "rinv", i, b + 1)
                    need(dve, "tmb", i, 1)
                    if b:
                        need(dve, "diag", i, b)
                    dve.tensor_scalar(rq, rinv, tmb[:, b:b + 1], None, ALU.mult).then_inc(S["rq"], 1)
                elif name[:4] == "film":
                    b, ps = c, tile_ps(f"f{c}")
                    need(dve, "film_mm", i, b + 1)
                    if b == 0:
                        need(dve, "xn2", i, 1)
                    dve.tensor_tensor(xn[:, b], xn[:, b], ps[:, 0:D], ALU.mult).then_inc(S["film_mul"], 1)
                    need(dve, "film_mul", i, b + 1)
                    dve.tensor_tensor(xn[:, b], xn[:, b], ps[:, D:2 * D], ALU.add).then_inc(S["film"], 1)

            def times_c(i, u):
                need(dve, "scan", i, u + 1)
                need(dve, "cb_mm", i, u + 1)
                h = ring[:, u % RING]
                dve.tensor_tensor(h, h, cb_ps[:, u % 2], ALU.mult).then_inc(S["hc"], 1)

            def iteration(i, par, front, back):
                names = which_steps(front, back)
                for u in range(C * NS):
                    need(dve, "decay", i, u + 1)
                    need(dve, "bx", i, u + 1)
                    s = ring[:, u % RING]
                    dve.tensor_tensor_scan(s, decay_ps[:, u % 2], s, 0.0, ALU.mult, ALU.add).then_inc(S["scan"], 1)
                    if u:
                        times_c(i, u - 1)
                    if u > 1 and u % NS == 1:
                        read_y(i, par, u // NS - 1)
                    for st in steps_at(DVE_AT, u, names):
                        if st in FRONT:
                            step(st, i + 1, 1 - par)
                        else:
                            step(st, i - 1, 1 - par)
                times_c(i, C * NS - 1)

            dve.memset(xa1[CT2:CT2 + 1], 1.0).then_inc(bias_one, 1)
            for k in range(2):
                dve.memset(seqs(decay_ps[:, k])[:, :, 0:1], 0.0).then_inc(zeroed, 1)
            dve.wait_ge(w_ld, 16 * N_W)
            dve.wait_ge(halved, 1)
            for s in [s for s in DVE_AT if s in FRONT]:
                step(s, 0, 0)
            all_blocks(dve, iteration, NB)
            for s in [s for s in DVE_AT if s in BACK]:
                step(s, NB - 1, 1)

        @block.gpsimd
        def _(pool):
            def inverse_deviation(i, mvn, ven, rsn, *used):
                need_apart(pool, (mvn, i, 1), *used)
                pool.tensor_scalar(ve, mv[:, :, 1], EPS, None, ALU.add).then_inc(S[ven], 1)
                need(pool, ven, i, 1)
                pool.tensor_tensor(rs, ve, nhalf, ALU.pow).then_inc(S[rsn], 1)

            def gate(i, par, c):
                need(pool, "y", i, c + 1)
                need(pool, "zs", i, c + 1)
                pool.tensor_tensor(yg[:, c], yg[:, c], zs[par][:, c], ALU.mult).then_inc(S["yg"], 1)

            def step(name, i, par):
                c = int(name[-1]) if name[-1].isdigit() else 0
                if name == "y3":
                    gate(i, par, C - 1)
                elif name == "ln1":
                    inverse_deviation(i, "mv1", "ve1", "rs1")
                elif name == "x1":
                    inverse_deviation(i, "mv2", "ve2", "rs2", ("x1", i, G))
                elif name == "mask":
                    need_apart(pool, ("ld_mask", i, 32), ("smask", i - 1, G))
                    pool.tensor_scalar(maskb.rearrange("p b g -> p (b g)"), mask8, -1.0, -OFF, ALU.add, ALU.mult)\
                        .then_inc(S["maskb"], 1)
                    need_apart(pool, ("rq", i - 1, G))
                    pool.tensor_scalar(tmb, tmask8, 1.0 / H, None, ALU.mult).then_inc(S["tmb"], 1)
                elif name == "xn":
                    need(pool, "xn0", i, G)
                    g, b = gb[:, 0:D], gb[:, D:2 * D]
                    pool.tensor_tensor(xn, xn, g[:, None, :].to_broadcast([P, G, D]), ALU.mult).then_inc(S["xn1"], 1)
                    need(pool, "xn1", i, 1)
                    pool.tensor_tensor(xn, xn, b[:, None, :].to_broadcast([P, G, D]), ALU.add).then_inc(S["xn2"], 1)
                elif name[:2] == "sm":
                    b = c
                    need_apart(pool, ("rq", i, b + 1), ("at_mm", i, b) if b else ("at_mm", i - 1, G))
                    for h in range(H):
                        a = pool.tensor_scalar(diag[:, h], ident, rq[:, h:h + 1], None, ALU.mult)
                    a.then_inc(S["diag"], 1)
                elif name[:2] == "sp":
                    need_apart(pool, ("vexp", i, c + 1))
                    t = uu[par][:, c]
                    pool.tensor_scalar(t, tmpA[:, c], 1.0, -1.0, ALU.add, ALU.add).then_inc(S["cor1"], 1)
                    need(pool, "vln", i, c + 1)
                    need(pool, "cor1", i, c + 1)
                    pool.tensor_tensor(tmpA[:, c], tmpA[:, c], t, ALU.subtract).then_inc(S["cor2"], 1)
                    need(pool, "cor2", i, c + 1)
                    pool.tensor_tensor(tmpB[:, c], tmpB[:, c], tmpA[:, c], ALU.add).then_inc(S["cor3"], 1)
                    need(pool, "cor3", i, c + 1)
                    need(pool, "vrelu", i, c + 1)
                    d = dt[par][:, c]
                    pool.tensor_tensor(d, d, tmpB[:, c], ALU.add).then_inc(S["dt"], 1)
                    need(pool, "dt", i, c + 1)
                    need(pool, "xs", i, c + 1)
                    pool.tensor_tensor(t, d, xs[par][:, c], ALU.mult).then_inc(S["u"], 1)

            def iteration(i, par, front, back):
                names = which_steps(front, back)
                for u in range(C * NS):
                    c, n = u // NS, u % NS
                    if n == 0:
                        need(pool, "u", i, c + 1)
                    if c == 0:
                        need(pool, "bb_sb", i, n + 1)
                    if u >= RING:
                        need(pool, "nsum", i, u - RING + 1)
                    else:
                        need(pool, "nsum", i - 1, C * NS - RING + u + 1)
                    pool.tensor_tensor(ring[:, u % RING], uu[par][:, c], Bb[:, n], ALU.mult).then_inc(S["bx"], 1)
                    if u > NS and u % NS == 4:
                        gate(i, par, u // NS - 1)
                    for s in steps_at(POOL_AT, u, names):
                        if s in FRONT:
                            step(s, i + 1, 1 - par)
                        else:
                            step(s, i - 1, 1 - par)

            identity(nc, pool, ident, pool_step)
            pool.memset(sel3[0:96], 0.0).then_inc(pool_step, 1)
            for k in range(3):
                pool.wait_ge(pool_step, 3 + k)
                pool.affine_select(out=sel3[0:96], in_=sel3[0:96], compare_op=ALU.not_equal, fill=1.0,
                                   base=-2 * NS * k, pattern=[[-1, 2 * NS]], channel_multiplier=1)\
                    .then_inc(pool_step, 1)
            pool.memset(nhalf, -0.5).then_inc(pool_step, 1)
            pool.wait_ge(pool_step, 7)
            pool.wait_ge(w_ld, 16 * N_W)
            for s in [s for s in POOL_AT if s in FRONT]:
                step(s, 0, 0)
            all_blocks(pool, iteration, NB)
            for s in [s for s in POOL_AT if s in BACK]:
                step(s, NB - 1, 1)


def pass2(nc, sems, arena, psum, xin_d, y_d, kr_d, B):
    GD = 8
    NB_ = 4
    LOOPS = P // (GD * NB_)
    with ExitStack() as ctx:
        def sem(n):
            return sems.named(n)
        x_ld = [sem(f"x_ld{h}") for h in range(DH)]
        t_ld = [sem(f"toeplitz_ld{k}") for k in range(NB_)]
        turned = [sem(f"turned{k}") for k in range(NB_)]
        conv_mm, out_v, out_s, y_st = sem("conv_mm"), sem("out_vector"), sem("out_scalar"), sem("y_stored")
        cv = Carve(arena)
        x2 = [cv.f32(B * P).rearrange("p (b d) -> p b d", b=B) for _ in range(DH)]
        rev, tz = ([cv.f32(GD * L).rearrange("p (d j) -> p d j", d=GD) for _ in range(NB_)] for _ in range(2))
        block = ctx.enter_context(nc.Block())
        NQ = 4

        @block.sync
        def _(sp):
            def load_toeplitz(q, first):
                for k in range(NB_):
                    if not first:
                        sp.wait_ge(turned[k], q)
                    row = kr_d[bass.ds(q * (NB_ * GD) + k * GD, GD), :]
                    src = bass.AP(row.tensor, row.offset, [[1, P], [2 * L, GD], [1, L]])
                    sp.dma_start(rev[k], src).then_inc(t_ld[k], 16)

            for h in range(DH):
                for q in range(NQ):
                    w = B // NQ
                    sp.dma_start(x2[h][:, q * w:(q + 1) * w], xin_d[h][:, q * w:(q + 1) * w]).then_inc(x_ld[h], 16)
            for h in range(DH):
                if h == 0:
                    load_toeplitz(0, True)
                with sp.Fori(1 if h == 0 else LOOPS, (h + 1) * LOOPS, 1) as q:
                    load_toeplitz(q, False)
            for h in range(DH):
                sp.wait_ge(out_v, (h + 1) * P // 8)
                sp.wait_ge(out_s, (h + 1) * P // 8)
                for q in range(NQ):
                    w = B // NQ
                    sp.dma_start(y_d[:, q * w:(q + 1) * w, h * P:(h + 1) * P], x2[h][:, q * w:(q + 1) * w])\
                      .then_inc(y_st, 16)
            sp.wait_ge(y_st, 16 * NQ * DH)

        @block.tensor
        def _(pe):
            def products(h, q, first):
                for k in range(NB_):
                    pe.wait_ge(turned[k], q + 1)
                    for j in range(2):
                        n = 2 * k + j
                        if not first:
                            pe.wait_ge(out_s if n % 2 else out_v, q * NB_)
                        for dd in range(4):
                            d = k * GD + j * 4 + dd
                            col = x2[h][:, :, bass.ds(q * (NB_ * GD) + (d - h * P), 1)]
                            pe.matmul(psum[:, n, dd * B:(dd + 1) * B], tz[k][:, j * 4 + dd],
                                      col.rearrange("p b o -> p (b o)"), start=True, stop=True)\
                              .then_inc(conv_mm, 1)

            for h in range(DH):
                pe.wait_ge(x_ld[h], 16 * NQ)
                if h == 0:
                    products(0, 0, True)
                with pe.Fori(h * LOOPS + (h == 0), (h + 1) * LOOPS, 1) as q:
                    products(h, q, False)

        @block.gpsimd
        def _(pool):
            def turn(q, first):
                for k in range(NB_):
                    loaded, used = q * 16 + 16, NB_ * GD * q + (GD * (k + 1) - NB_ * GD)
                    if not first:
                        loaded, used = pool.to_reg(loaded), pool.to_reg(used)
                    pool.wait_ge(t_ld[k], 16)
                    pool.wait_ge(t_ld[k], loaded)
                    if not first:
                        pool.wait_ge(conv_mm, used)
                    pool.tensor_copy(tz[k], rev[k][:, :, ::-1]).then_inc(turned[k], 1)

            turn(0, True)
            with pool.Fori(1, DH * LOOPS, 1) as q:
                turn(q, False)

        def read_out(eng, h, odd, sem_, copy):
            with eng.Fori(h * LOOPS, (h + 1) * LOOPS, 1) as q:
                for n in range(odd, 2 * NB_, 2):
                    eng.wait_ge(conv_mm, q * (NB_ * GD) + 4 * (n + 1))
                    dst = x2[h][:, :, bass.ds(q * (NB_ * GD) + (4 * n - h * P), 4)]
                    copy(dst.rearrange("p b d -> p d b"),
                         psum[:, n, 0:4 * B].rearrange("p (d b) -> p d b", d=4)).then_inc(sem_, 1)

        @block.vector
        def _(dve):
            for h in range(DH):
                read_out(dve, h, 0, out_v, dve.tensor_copy)

        @block.scalar
        def _(act):
            for h in range(DH):
                read_out(act, h, 1, out_s, act.copy)


PER3 = dict(
    g_y=16, g_x1=16, g_xa=32, st_out=16,
    fo_mm=4, fo_mul=4, fo_add=4, xt=1, hn0=4, hn1=1, hn2=1, ht_mm=2, hT=2,
    f1_mm=8, gelu=8, f2_mm=2, d_res=2, d_b2=1, xo=4, xo1=1, xo2=1, xo3=1, x2=4,
    x2t_mm=2, mix0=2, mix1=2, mix=2, wo1_mm=1, tanh=1, h_mm=5, hb=5, wo2_mm=1,
    best=1, ties=1, ranks=1, first=1, onehot=1, m_mm=5, hm=5, w2_mm=2, r3=2,
    xf=4, xf1=1, xf2=1, xf3=1, x3=4,
    st_a=4, mv_a=1, ve_a=1, rs_a=1, st_o=4, mv_o=1, ve_o=1, rs_o=1, st_r=4, mv_r=1, ve_r=1, rs_r=1,
    st_f=4, mv_f=1, ve_f=1, rs_f=1, st_z=4, mv_z=1, ve_z=1, rs_z=1,
)
QC = 5


def pass3(nc, sems, i_, arena, psum, x1_d, xa_d, y_d, wf_d, out, NB):
    with ExitStack() as ctx:
        S = {n: sems.named("p3_" + n) for n in PER3}
        w_ld, consts = sems.named("p3_w_ld"), sems.named("p3_consts")
        ident_made = sems.named("p3_ident")
        cv = Carve(arena)
        fo0, fo1 = cv.f32(2 * D), cv.f32(2 * D, CT2 + 1)
        w1 = cv.f32(DH * HID).rearrange("p (k e) -> p k e", k=DH)
        w2 = cv.f32(8 * D).rearrange("p (m d) -> p m d", m=8)
        wo1 = cv.f32(DH * DM).rearrange("p (k e) -> p k e", k=DH)
        wo2 = cv.f32(NP_, DM + 1)
        w1c = cv.f32(DH * NP_ * DM).rearrange("p (k e) -> p k e", k=DH)
        w2c = cv.f32(QC * D).rearrange("p (q d) -> p q d", q=QC)
        vec = cv.f32(NV)
        wide = cv.f32(9 * D)
        ident = cv.f32(P)
        ident_b = cv.bf16(P)
        rank = cv.f32(NP_)
        nhalf = cv.f32(G)

        def blocks(n=1):
            return [cv.f32(G * D).rearrange("p (b d) -> p b d", b=G) for _ in range(n)]

        y = blocks()[0]
        x1, xt, x2 = blocks(2), blocks(2), blocks(2)
        hn, xo, xf = blocks()[0], blocks()[0], blocks()[0]
        xa0, xa1 = cv.f32(T), cv.f32(T, CT2 + 1)
        hT = cv.f32(DH * T).rearrange("p (k t) -> p k t", k=DH)
        gT = cv.f32(8 * T).rearrange("p (m t) -> p m t", m=8)
        xm = cv.f32(DH * T).rearrange("p (k t) -> p k t", k=DH)
        th = cv.f32(T, DM + 1)
        hb = cv.f32(QC * T).rearrange("p (q t) -> p q t", q=QC)
        hm = cv.f32(QC * T).rearrange("p (q t) -> p q t", q=QC)
        score = cv.f32(G * NP_).rearrange("p (b n) -> p b n", b=G)
        tied = cv.f32(G * NP_).rearrange("p (b n) -> p b n", b=G)
        best, lead = cv.f32(G), cv.f32(G)
        onehot = cv.bf16(G * NP_ + 1)[:, 0:G * NP_].rearrange("p (b n) -> p b n", b=G)
        st = {k: cv.f32(G * 6).rearrange("p (b s) -> p b s", b=G) for k in "aorfz"}
        mv = {k: cv.f32(G * 2).rearrange("p (b s) -> p b s", b=G) for k in "aorfz"}
        ve = {k: cv.f32(G) for k in "aorfz"}
        rs = {k: cv.f32(G) for k in "aorfz"}
        N_CONST = 6
        N_W = 11
        REST = DM + NP_

        def need(eng, name, i, k):
            count = i * PER3[name] + k
            if not isinstance(count, int) or count > 0:
                eng.wait_ge(S[name], count)

        def need_apart(eng, *what):
            counts = [(name, i * PER3[name] + k) for name, i, k in what]
            counts = [(name, n if isinstance(n, int) else eng.to_reg(n)) for name, n in counts]
            eng.wait_ge(w_ld, 16 * N_W)
            for name, count in counts:
                if not isinstance(count, int) or count > 0:
                    eng.wait_ge(S[name], count)

        def following(i):
            return i if isinstance(i, int) and i == NB - 1 else i + 1

        def seqs(v):
            return v.rearrange("p (b t) -> p b t", b=G)

        def over_seqs(n):
            return wide[:, n * D:(n + 1) * D][:, None, :].to_broadcast([P, G, D])

        def run(eng, step, order):
            def iteration(i, par, ahead, behind):
                for name, off in order:
                    if (off == 1 and not ahead) or (off == -1 and not behind):
                        continue
                    step(name, i + off, (par + off) % 2)

            for name, off in order:
                if off == 1:
                    step(name, 0, 0)
            all_blocks(eng, iteration, NB)
            for name, off in order:
                if off == -1:
                    step(name, NB - 1, 1)

        block = ctx.enter_context(nc.Block())

        @block.sync
        def _(sp):
            for dst, src in (
                (fo0, wf_d[0:P, 2 * D:MOD]), (fo1, wf_d[P:CTX + 1, 2 * D:MOD]), (w1, i_["w1"]), (w2, i_["w2"]),
                (wo1, i_["wo1"]), (wo2, i_["wo2"]), (w1c, i_["w1c"]), (w2c[:, 0:4], i_["w2c"][:, 0:4]),
                (w2c[0:REST, 4], i_["w2c"][0:REST, 4]), (vec, i_["vec"]),
                (wide, i_["wide"][0:1, 0:9 * D].to_broadcast([P, 9 * D])),
            ):
                sp.dma_start(dst, src).then_inc(w_ld, 16)

            def step(name, i, par):
                if name == "load":
                    need(sp, "xt", i - 1, 1)
                    sp.dma_start(y, y_d[:, bass.ts(i, G), :]).then_inc(S["g_y"], 16)
                    need(sp, "xo3", i - 2, 1)
                    sp.dma_start(x1[par], x1_d[:, bass.ts(i, G), :]).then_inc(S["g_x1"], 16)
                    need(sp, "fo_mm", i - 1, G)
                    sp.dma_start(xa0, xa_d[0:P, bass.ts(i, T)]).then_inc(S["g_xa"], 16)
                    sp.dma_start(xa1[0:CT2], xa_d[P:CTX, bass.ts(i, T)]).then_inc(S["g_xa"], 16)
                elif name == "store":
                    need(sp, "x3", i, G)
                    sp.dma_start(out[:, bass.ts(i, G), :], xf).then_inc(S["st_out"], 16)

            run(sp, step, [("load", 1), ("store", -1)])
            sp.wait_ge(S["st_out"], NB * 16)

        @block.tensor
        def _(pe):
            def step(name, i, par):
                if name == "film":
                    need(pe, "g_xa", i, 32)
                    for b in range(G):
                        if b >= 2:
                            need(pe, "fo_add", i, b - 1)
                        else:
                            need(pe, "hT", i - 1, DH)
                        ps = psum[:, 4 + b % 2]
                        pe.matmul(ps, xa0[:, b * L:(b + 1) * L], fo0, start=True, stop=False)
                        pe.matmul(ps, xa1[0:CT2 + 1, b * L:(b + 1) * L], fo1, start=False, stop=True)\
                          .then_inc(S["fo_mm"], 1)
                elif name == "hT":
                    need(pe, "hn2", i, 1)
                    need(pe, "fo_add", i, G)
                    for k in range(DH):
                        for b in range(G):
                            mm = pe.transpose(psum[:, 4 + k, b * L:(b + 1) * L], hn[:, b, k * P:(k + 1) * P], ident)
                        mm.then_inc(S["ht_mm"], 1)
                elif name == "f1":
                    need(pe, "hT", i, DH)
                    need(pe, "hb", i - 2, QC)
                    for m in range(8):
                        if m >= 2:
                            need(pe, "gelu", i, m - 1)
                        for k in range(DH):
                            mm = pe.matmul(psum[:, m % 2], w1[:, k, m * P:(m + 1) * P], hT[:, k],
                                           start=k == 0, stop=k == DH - 1)
                        mm.then_inc(S["f1_mm"], 1)
                elif name == "f2":
                    need(pe, "gelu", i, 8)
                    need(pe, "r3", i - 2, 2)
                    for o in range(2):
                        for bb in range(2):
                            b = 2 * o + bb
                            for m in range(8):
                                mm = pe.matmul(psum[:, 2 + o, bb * D:(bb + 1) * D], gT[:, m, b * L:(b + 1) * L],
                                               w2[:, m], start=m == 0, stop=m == 7)
                        mm.then_inc(S["f2_mm"], 1)
                elif name == "x2T":
                    need(pe, "x2", i, G)
                    need(pe, "hm", i - 1, QC)
                    for k in range(DH):
                        for b in range(G):
                            mm = pe.transpose(psum[:, 6 + k, b * L:(b + 1) * L], x2[par][:, b, k * P:(k + 1) * P],
                                              ident)
                        mm.then_inc(S["x2t_mm"], 1)
                elif name == "wo1":
                    need(pe, "mix", i, DH)
                    for k in range(DH):
                        mm = pe.matmul(psum[0:DM, 6], wo1[:, k], xm[:, k], start=k == 0, stop=k == DH - 1)
                    mm.then_inc(S["wo1_mm"], 1)
                elif name == "h9":
                    need(pe, "gelu", following(i), 8)
                    for q in range(QC):
                        if q >= 2:
                            need(pe, "hb", i, q - 1)
                        rows = P if q < 4 else DM
                        for k in range(DH):
                            mm = pe.matmul(psum[0:rows, q % 2], w1c[:, k, q * P:q * P + rows], xm[:, k],
                                           start=k == 0, stop=k == DH - 1)
                        mm.then_inc(S["h_mm"], 1)
                elif name == "wo2":
                    need(pe, "tanh", i, 1)
                    for b in range(G):
                        mm = pe.matmul(psum[:, 7, b * NP_:(b + 1) * NP_], th[:, b * L:(b + 1) * L], wo2,
                                       start=True, stop=True)
                    mm.then_inc(S["wo2_mm"], 1)
                elif name == "mask":
                    need(pe, "onehot", i, 1)
                    for q in range(QC):
                        if q >= 2:
                            need(pe, "hm", i, q - 1)
                        for b in range(G):
                            o = psum[:, 6 + q % 2, b * L:(b + 1) * L]
                            if q < 4:
                                for k in range(2):
                                    path = onehot[:, b, 2 * q + k:2 * q + k + 1].to_broadcast([P, DM])
                                    mm = pe.matmul(o[k * DM:(k + 1) * DM], path, ident_b, start=True, stop=True)
                            else:
                                pe.matmul(o[0:DM], onehot[:, b, 8:9].to_broadcast([P, DM]), ident_b,
                                          start=True, stop=True)
                                mm = pe.matmul(o[DM:REST], onehot[:, b], ident_b, start=True, stop=True)
                        mm.then_inc(S["m_mm"], 1)
                elif name == "w2":
                    need(pe, "hm", i, QC)
                    need(pe, "d_res", following(i), 2)
                    for o in range(2):
                        for bb in range(2):
                            b = 2 * o + bb
                            for q in range(QC):
                                rows = P if q < 4 else REST
                                mm = pe.matmul(psum[:, 2 + o, bb * D:(bb + 1) * D], hm[0:rows, q, b * L:(b + 1) * L],
                                               w2c[0:rows, q], start=q == 0, stop=q == QC - 1)
                        mm.then_inc(S["w2_mm"], 1)

            pe.wait_ge(consts, N_CONST)
            pe.wait_ge(w_ld, 16 * N_W)
            run(pe, step, [("f1", 0), ("x2T", -1), ("film", 1), ("f2", 0), ("wo1", -1), ("h9", -1), ("wo2", -1),
                           ("mask", -1), ("hT", 1), ("w2", -1)])

        @block.scalar
        def _(act):
            def step(name, i, par):
                if name == "hT":
                    need(act, "f1_mm", i - 1, 8)
                    for k in range(DH):
                        need(act, "ht_mm", i, k + 1)
                        act.copy(hT[:, k], psum[:, 4 + k]).then_inc(S["hT"], 1)
                elif name == "f1":
                    need(act, "f2_mm", i - 1, 2)
                    for m in range(8):
                        need(act, "f1_mm", i, m + 1)
                        act.activation(gT[:, m], psum[:, m % 2], ACT.Gelu, bias=vec[:, V_B1 + m:V_B1 + m + 1])\
                            .then_inc(S["gelu"], 1)
                elif name == "mix":
                    need(act, "h_mm", i - 1, QC)
                    for k in range(DH):
                        need(act, "x2t_mm", i, k + 1)
                        act.activation(xm[:, k], psum[:, 6 + k], ACT.Identity,
                                       scale=vec[:, V_MIX + 3 * k + 1:V_MIX + 3 * k + 2]).then_inc(S["mix0"], 1)
                elif name == "tanh":
                    need(act, "wo1_mm", i, 1)
                    need(act, "wo2_mm", i - 1, 1)
                    act.activation(th[0:DM], psum[0:DM, 6], ACT.Tanh, bias=vec[0:DM, V_BO1:V_BO1 + 1])\
                        .then_inc(S["tanh"], 1)
                elif name == "hb":
                    need(act, "hm", i - 1, QC)
                    for q in range(QC):
                        rows = P if q < 4 else DM
                        need(act, "h_mm", i, q + 1)
                        act.activation(hb[0:rows, q], psum[0:rows, q % 2], ACT.Identity,
                                       bias=vec[0:rows, V_FB1 + q:V_FB1 + q + 1]).then_inc(S["hb"], 1)

            act.wait_ge(w_ld, 16 * N_W)
            act.wait_ge(consts, N_CONST)
            run(act, step, [("f1", 0), ("mix", -1), ("tanh", -1), ("hb", -1), ("hT", 1)])

        @block.vector
        def _(dve):
            def stats(i, src, k):
                need(dve, "ve_" + k, i - 1, 1)
                need(dve, "rs_" + k, i - 1, 1)
                for b in range(G):
                    dve.bn_stats(st[k][:, b], src[:, b]).then_inc(S["st_" + k], 1)
                need_apart(dve, ("st_" + k, i, G))
                for b in range(G):
                    a = dve.bn_aggr(mv[k][:, b], st[k][:, b])
                a.then_inc(S["mv_" + k], 1)

            def normed(i, dst, src, k, sem):
                need(dve, "rs_" + k, i, 1)
                need(dve, "mv_" + k, i, 1)
                for b in range(G):
                    dve.tensor_scalar(dst[:, b], src[:, b], mv[k][:, b, 0:1], rs[k][:, b:b + 1],
                                      ALU.subtract, ALU.mult).then_inc(S[sem], 1)

            def pair(v, o):
                return v[:, 2 * o:2 * o + 2]

            def halves(ps):
                return ps.rearrange("p (b d) -> p b d", b=2)

            def step(name, i, par):
                if name == "film":
                    need(dve, "g_y", i, 16)
                    for b in range(G):
                        ps = psum[:, 4 + b % 2]
                        need(dve, "fo_mm", i, b + 1)
                        dve.tensor_tensor(y[:, b], y[:, b], ps[:, 0:D], ALU.mult).then_inc(S["fo_mul"], 1)
                        need(dve, "fo_mul", i, b + 1)
                        dve.tensor_tensor(y[:, b], y[:, b], ps[:, D:2 * D], ALU.add).then_inc(S["fo_add"], 1)
                elif name == "stA":
                    need(dve, "xt", i, 1)
                    stats(i, xt[par], "a")
                elif name == "nA":
                    need(dve, "ht_mm", i - 1, DH)
                    normed(i, hn, xt[par], "a", "hn0")
                elif name == "d1":
                    for o in range(2):
                        need(dve, "f2_mm", i, o + 1)
                        dve.tensor_tensor(pair(xt[par], o), halves(psum[:, 2 + o]), pair(xt[par], o), ALU.add)\
                           .then_inc(S["d_res"], 1)
                elif name == "stO":
                    need(dve, "d_b2", i, 1)
                    stats(i, xt[par], "o")
                elif name == "nO":
                    need(dve, "x2", i - 1, G)
                    normed(i, xo, xt[par], "o", "xo")
                elif name == "stR":
                    need(dve, "xo3", i, 1)
                    stats(i, xo, "r")
                elif name == "nR":
                    normed(i, x2[par], xo, "r", "x2")
                elif name == "mix":
                    for k in range(DH):
                        need(dve, "mix0", i, k + 1)
                        src, dst = seqs(psum[:, 6 + k]), seqs(xm[:, k])
                        w = V_MIX + 3 * k
                        dve.scalar_tensor_tensor(out=dst[:, :, 1:L], in0=src[:, :, 0:L - 1], scalar=vec[:, w:w + 1],
                                                 in1=dst[:, :, 1:L], op0=ALU.mult, op1=ALU.add).then_inc(S["mix1"], 1)
                    for k in range(DH):
                        need(dve, "mix1", i, k + 1)
                        src, dst = seqs(psum[:, 6 + k]), seqs(xm[:, k])
                        w = V_MIX + 3 * k
                        dve.scalar_tensor_tensor(out=dst[:, :, 0:L - 1], in0=src[:, :, 1:L],
                                                 scalar=vec[:, w + 2:w + 3], in1=dst[:, :, 0:L - 1],
                                                 op0=ALU.mult, op1=ALU.add).then_inc(S["mix"], 1)
                elif name == "argmax":
                    ps = psum[:, 7, 0:G * NP_].rearrange("p (b n) -> p b n", b=G)
                    need(dve, "wo2_mm", i, 1)
                    dve.tensor_reduce(best, ps, AX.X, ALU.max).then_inc(S["best"], 1)
                    need(dve, "best", i, 1)
                    dve.tensor_tensor(tied, ps, best[:, :, None].to_broadcast([P, G, NP_]), ALU.is_equal)\
                       .then_inc(S["ties"], 1)
                    need(dve, "ties", i, 1)
                    dve.tensor_tensor(tied, tied, rank[:, None, :].to_broadcast([P, G, NP_]), ALU.mult)\
                       .then_inc(S["ranks"], 1)
                    need(dve, "ranks", i, 1)
                    dve.tensor_reduce(lead, tied, AX.X, ALU.max).then_inc(S["first"], 1)
                    need(dve, "first", i, 1)
                    need(dve, "m_mm", i - 1, QC)
                    dve.tensor_tensor(onehot, tied, lead[:, :, None].to_broadcast([P, G, NP_]), ALU.is_equal)\
                       .then_inc(S["onehot"], 1)
                elif name == "hm":
                    need(dve, "w2_mm", i - 1, 2)
                    for q in range(QC):
                        rows = P if q < 4 else REST
                        need(dve, "hb", i, q + 1)
                        need(dve, "m_mm", i, q + 1)
                        dve.tensor_tensor(hm[0:rows, q], hb[0:rows, q], psum[0:rows, 6 + q % 2], ALU.mult)\
                           .then_inc(S["hm"], 1)
                elif name == "r3":
                    need(dve, "st_out", i - 1, 16)
                    for o in range(2):
                        need(dve, "w2_mm", i, o + 1)
                        dve.tensor_tensor(pair(xf, o), halves(psum[:, 2 + o]), pair(x2[par], o), ALU.add)\
                           .then_inc(S["r3"], 1)
                    need(dve, "r3", i, 2)
                    stats(i, xf, "f")
                elif name == "nF":
                    normed(i, xf, xf, "f", "xf")
                elif name == "stZ":
                    need(dve, "xf3", i, 1)
                    stats(i, xf, "z")
                elif name == "nZ":
                    normed(i, xf, xf, "z", "x3")

            dve.memset(xa1[CT2:CT2 + 1], 1.0).then_inc(consts, 1)
            dve.memset(th[DM:DM + 1], 1.0).then_inc(consts, 1)
            dve.memset(hb[DM:P, 4], 1.0).then_inc(consts, 1)
            dve.wait_ge(w_ld, 16 * N_W)
            dve.wait_ge(consts, N_CONST)
            run(dve, step, [("stO", -1), ("nO", -1), ("stR", -1), ("nR", -1), ("mix", -1), ("film", 1), ("stA", 1),
                            ("nA", 1), ("d1", 0), ("argmax", -1), ("hm", -1), ("r3", -1), ("nF", -1), ("stZ", -1),
                            ("nZ", -1)])

        @block.gpsimd
        def _(pool):
            def deviation(i, k):
                need_apart(pool, ("mv_" + k, i, 1))
                pool.tensor_scalar(ve[k], mv[k][:, :, 1], EPS, None, ALU.add).then_inc(S["ve_" + k], 1)
                need(pool, "ve_" + k, i, 1)
                pool.tensor_tensor(rs[k], ve[k], nhalf, ALU.pow).then_inc(S["rs_" + k], 1)

            def affine(i, v, ready, g, b, s1, s2):
                need(pool, ready, i, G)
                pool.tensor_tensor(v, v, over_seqs(g), ALU.mult).then_inc(S[s1], 1)
                need(pool, s1, i, 1)
                pool.tensor_tensor(v, v, over_seqs(b), ALU.add).then_inc(S[s2], 1)

            def step(name, i, par):
                if name == "xt":
                    need(pool, "fo_add", i, G)
                    need(pool, "g_x1", i, 16)
                    need(pool, "xo", i - 2, G)
                    pool.tensor_tensor(xt[par], y, x1[par], ALU.add).then_inc(S["xt"], 1)
                elif name == "dA":
                    deviation(i, "a")
                elif name == "hn":
                    affine(i, hn, "hn0", W_GFFN, W_BFFN, "hn1", "hn2")
                elif name == "b2":
                    need(pool, "d_res", i, 2)
                    pool.tensor_tensor(xt[par], xt[par], over_seqs(W_B2), ALU.add).then_inc(S["d_b2"], 1)
                elif name == "dO":
                    deviation(i, "o")
                elif name == "xo":
                    affine(i, xo, "xo", W_GOUT, W_BOUT, "xo1", "xo2")
                    need(pool, "xo2", i, 1)
                    pool.tensor_tensor(xo, xo, x1[par], ALU.add).then_inc(S["xo3"], 1)
                elif name == "dR":
                    deviation(i, "r")
                elif name == "dF":
                    deviation(i, "f")
                elif name == "xf":
                    affine(i, xf, "xf", W_GAM, W_BET, "xf1", "xf2")
                    need(pool, "xf2", i, 1)
                    pool.tensor_tensor(xf, xf, x2[par], ALU.add).then_inc(S["xf3"], 1)
                elif name == "dZ":
                    deviation(i, "z")

            identity(nc, pool, ident, ident_made)
            pool.wait_ge(ident_made, 2)
            pool.tensor_copy(ident_b, ident).then_inc(consts, 1)
            pool.iota(rank, [[-1, NP_]], base=NP_, channel_multiplier=0,
                      allow_small_or_imprecise_dtypes=True).then_inc(consts, 1)
            pool.memset(nhalf, -0.5).then_inc(consts, 1)
            pool.wait_ge(w_ld, 16 * N_W)
            pool.wait_ge(consts, N_CONST)
            run(pool, step, [("dO", -1), ("xo", -1), ("dR", -1), ("xt", 1), ("dA", 1), ("hn", 1), ("b2", 0),
                             ("dF", -1), ("xf", -1), ("dZ", -1)])


_OUT = "out_0_dram"


def lay_out(inputs, B):
    import numpy as np
    a = {k: np.asarray(v) for k, v in inputs.items()}
    f = {k[len("L0_"):]: v for k, v in a.items() if k.startswith("L0_")}

    def chunks(v, rows=P):
        return np.ascontiguousarray(v.reshape(-1, rows, v.shape[-1]).transpose(1, 0, 2))

    x, c = a["x"][:B], a["ctx_768"][:B]
    conv_w = f["attn_conv_w"].reshape(C, P, 4).transpose(1, 0, 2).reshape(P, 16)

    def cols(v):
        return v.reshape(-1, P).T

    fb1 = np.zeros((P, 5), np.float32)
    fb1[:, 0:4] = f["ffn_b1"].reshape(-1)[0:512].reshape(4, P).T
    fb1[0:DM, 4] = f["ffn_b1"].reshape(-1)[512:]
    bo1 = np.zeros((P, 1), np.float32)
    bo1[0:DM, 0] = f["ffn_bo1"]
    vec = np.concatenate([
        conv_w, cols(f["attn_conv_b"]), cols(f["attn_dt_proj_b"]), cols(f["attn_D"]),
        f["attn_A_log"].reshape(C, P, NS).transpose(1, 0, 2).reshape(P, C * NS), cols(f["xattn_b1"]),
        f["ffn_mix_kernel"].reshape(3, DH, P).transpose(2, 1, 0).reshape(P, 6), fb1, bo1], axis=1)
    assert vec.shape == (P, NV)
    wide = np.concatenate([f["xattn_g_norm_in"], f["xattn_b_norm_in"], f["xattn_g_ffn"], f["xattn_b_ffn"],
                           f["xattn_b2"], f["xattn_g_norm_out"], f["xattn_b_norm_out"], f["ffn_gamma"],
                           f["ffn_beta"], f["xattn_mod_gate"].reshape(1)])[None]
    w2c = np.zeros((P, QC, D), np.float32)
    flat = f["ffn_W2"].reshape(NP_ * DM, D)
    w2c[:, 0:4] = flat[0:512].reshape(4, P, D).transpose(1, 0, 2)
    w2c[0:DM, 4] = flat[512:]
    w2c[DM:DM + NP_, 4] = f["ffn_b2"]
    w1c = f["ffn_W1"].transpose(1, 0, 2).reshape(D, NP_ * DM)
    r = {
        "x": x.transpose(1, 0, 2), "xT": x.reshape(B * L, DH, P).transpose(2, 1, 0),
        "ctx": c.transpose(1, 0, 2), "ctxT": c.reshape(B * L, CTX).T,
        "vmask": a["mask_BxS2_bf1"][:B].reshape(1, B * L).view(np.uint8),
        "tmask": np.ascontiguousarray(a["mask_BxS_bf1"][:B].T).view(np.uint8),
        "in_proj": chunks(f["attn_in_proj_w"].T), "x_proj": chunks(f["attn_x_proj_w"].T),
        "dt_proj": f["attn_dt_proj_w"].T, "out_proj": chunks(f["attn_out_proj_w"].T),
        "wq": chunks(f["xattn_Wq"]), "wk": f["xattn_Wk"], "wv": chunks(f["xattn_Wv"].T),
        "wf": chunks(np.concatenate([f["xattn_W_film_in"], f["xattn_W_film_out"]], axis=1)),
        "film_b": np.concatenate([f["xattn_b_film_in"], f["xattn_b_film_out"]])[None],
        "s4": np.stack([f["xattn_A_re"].T, f["xattn_A_im"].T, f["xattn_C_re"].T, f["xattn_C_im"].T], axis=1),
        "log_dt": f["xattn_log_dt"][None], "d_skip": f["xattn_D_skip"][None],
        "w1": chunks(f["xattn_W1"]), "w2": chunks(f["xattn_W2"]), "wo1": chunks(f["ffn_Wo1"]),
        "wo2": np.concatenate([f["ffn_Wo2"], f["ffn_bo2"][None]]), "w1c": chunks(w1c), "w2c": w2c,
        "vec": vec, "wide": wide,
    }
    return {k: np.ascontiguousarray(v) for k, v in r.items()}


def kernel(**inputs):
    import concourse.bacc as bacc
    import numpy as np
    from concourse.bass_utils import run_bass_kernel_spmd

    B = inputs["x"].shape[0]
    arrays = lay_out(inputs, B)
    nc = bacc.Bacc("TRN2", target_bir_lowering=False, num_devices=1)
    i_ = {k: nc.dram_tensor(f"in_{k}_dram", v.shape, mybir.dt.from_np(v.dtype), kind="ExternalInput").ap()
          for k, v in arrays.items()}
    out = nc.dram_tensor(_OUT, (L, B, D), F32, kind="ExternalOutput").ap()
    decoder_layer(nc, i_, out, B // G)
    r = run_bass_kernel_spmd(nc, [{f"in_{k}_dram": v for k, v in arrays.items()}], core_ids=[0])
    return np.ascontiguousarray(r.results[0][_OUT].transpose(1, 0, 2))
```

```python
from contextlib import ExitStack

import concourse.bass as bass
from concourse import mybir

ALU = mybir.AluOpType
ACT = mybir.ActivationFunctionType
AX = mybir.AxisListType
F32 = mybir.dt.float32
BF16 = mybir.dt.bfloat16
U8 = mybir.dt.uint8

P = 128
L = 128
D = 256
DH = D // P
DI = 512
C = DI // P
NS = 16
R = 64
G = 4
T = G * L
CTX = 192
CT2 = CTX - P
H = 4
HD = 32
TOPK = 32
KR = TOPK // 8
MOD = 1024
EPS = 1e-5
SM = 64
HID = 1024
NP_ = 9
DM = D // 4
RING = 8
SUM_LAG = 3
Y_AT = 4
GATE_AT = 9
NEG = -3.0e38
OFF = -1.0e30

V_CONVW, V_CONVB, V_DTB, V_D, V_ALOG = 0, 16, 20, 24, 28
V_B1, V_MIX, V_FB1, V_BO1, NV = 92, 100, 106, 111, 112
W_GIN, W_BIN, W_GFFN, W_BFFN, W_B2, W_GOUT, W_BOUT, W_GAM, W_BET = range(9)
NW = 9 * D + 1

PER = dict(
    ld_xT=16, ld_x=16, ld_ctxT=32, ld_ctx=16, ld_mask=32, st_x1=16, st_xa=32, st_xin=32,
    in_mm=8, xp_mm=1, dt_mm=4, conv0=4, tap=8, conv=4, xth=4, xt1=4, xs=4, zhalf=4, zth=4, zt1=4, zs=4,
    dtr=1, bc_hi=1, bc_r1=1, bc_mid=1, bc_cp=1, bcp=1, vabs=4, vrelu=4, vexp=4, vln=4, w1=4,
    cor1=4, cor2=4, cor3=4, dt=4, u=4,
    bb_mm=16, bb_sb=16, cb_mm=64, decay=64, bx=64, scan=64, hc=64, nsum=64, y=4, yg=4,
    o_mm=2, res=2, st1=4, mv1=1, ve1=1, rs1=1, x1=4, st2=4, mv2=1, ve2=1, rs2=1, tmb=1,
    xt_mm=2, x1T=2, q_mm=1, k_mm=1, qT=1, kT=1, maskb=1, s_mm=16, smask=4,
    v8=4 * KR, took=4 * KR, nmax=4, ex=4, em=4, rinv=4, rq=4, diag=4, at_mm=4, atT=4,
    xa_mm=2, xaT0=1, xaT1=1, film_mm=4, film_mul=4, film=4,
)

FRONT = ["xc0", "xc1", "xc2", "xc3", "z0", "z1", "z2", "z3", "xp", "xq", "dt0", "dt1", "dt2", "dt3", "ln",
         "sp0", "sp1", "sp2", "sp3"]
BACK = (["y3", "op0", "op1", "op2", "op3", "ln1", "mask", "rs1", "x1", "rs2", "x1T", "qk"]
        + [s + str(b) for b in range(G) for s in ("sc", "tka", "tkb", "tkc", "tkd", "sm", "dg", "at")]
        + ["xa", "film0", "film1", "film2", "film3"])
PE_AT = dict(xc0=0, xc1=2, xc2=3, xc3=4, op0=6, op1=8, z0=10, op2=11, op3=11, z1=12, z2=12, x1T=14, z3=15,
             qk=16, sc0=18, xp=20, dt0=23, sc1=28, at0=31, dt1=33, dt2=33, dt3=33, sc2=37, at1=42, sc3=45,
             at2=49, at3=57, xa=58, film0=59, film1=60, film2=61, film3=61)
ACT_AT = dict(xc0=2, y3=2, xc1=3, xc2=4, xc3=7, z0=11, z1=13, z2=13, x1T=13, z3=14, qk=17, sc0=20, sm0=22,
              xp=24, dt0=27, dg0=31, at0=34, sc1=34, dt1=35, dt2=36, sm1=37, dt3=40, dg1=42, sc2=43, ln=45,
              at1=45, sm2=47, dg2=50, at2=51, sc3=51, sm3=52, xq=55, dg3=57, at3=58, xa=60)
DVE_AT = dict(xc0=2, xc1=3, xc2=5, xc3=9, ln1=11, x1=13, tka0=20, tkb0=20, tkc0=21, xp=26, tkd0=26, sm0=29,
              tka1=33, tkb1=34, tkc1=35, tkd1=36, sm1=38, tka2=43, tkb2=43, tkc2=44, tkd2=45, sm2=47, tka3=51,
              tkb3=52, tkc3=53, tkd3=54, sm3=55, xq=58, film0=59, film1=60, film2=62, film3=63)
POOL_AT = dict(y3=6, z0=13, rs1=15, z1=15, z2=18, mask=18, z3=21, rs2=31, sp0=54, sp1=58, sp2=63, sp3=63)


def steps_at(table, u, which):
    return [s for s, at in table.items() if at == u and s in which]


LAST_READ = dict(
    xc0=("conv", 1), xc1=("conv", 2), xc2=("conv", 3), xc3=("conv", 4),
    z0=("zth", 1), z1=("zth", 2), z2=("zth", 3), z3=("zth", 4), xp=("bc_r1", 1),
    dt0=("vrelu", 1), dt1=("vrelu", 2), dt2=("vrelu", 3), dt3=("vrelu", 4),
    o0=("res", 1), o1=("res", 2), t0=("x1T", 1), t1=("x1T", 2), q=("qT", 1), k=("kT", 1),
    s0=("smask", 1), s1=("smask", 2), s2=("smask", 3), s3=("smask", 4),
    a0=("atT", 1), a1=("atT", 2), a2=("atT", 3), a3=("atT", 4), xa0=("xaT0", 1), xa1=("xaT1", 1),
    f0=("film", 1), f1=("film", 2), f2=("film", 3), f3=("film", 4),
)
TILES = dict(op0=["o0"], op1=[], op2=["o1"], op3=[], x1T=["t0", "t1"], qk=["q", "k"], xa=["xa0", "xa1"],
             **{f"sc{b}": [f"s{b}"] for b in range(G)}, **{f"at{b}": [f"a{b}"] for b in range(G)},
             **{f"film{b}": [f"f{b}"] for b in range(G)})
ORDER = [t for s in PE_AT for t in TILES.get(s, [s])]
BANK = {t: n % 2 for n, t in enumerate(ORDER)}


def is_front(tile):
    return tile in FRONT


def bank_before(tile, which):
    held = None
    for t in ORDER:
        if t == tile:
            return held
        if BANK[t] == BANK[tile] and is_front(t) in which:
            held = t
    return None


B_AHEAD = 3
SPREAD = [("b", n) for n in range(B_AHEAD)]
for unit in range(C * NS):
    SPREAD += [("b", B_AHEAD + unit)] * (B_AHEAD + unit < NS) + [("c", unit)]
SPREAD_BANK = {t: n % 3 for n, t in enumerate(SPREAD)}


def spread_before(tile):
    n = SPREAD.index(tile)
    if n >= 3:
        return SPREAD[n - 3], 0
    return [t for t in SPREAD if SPREAD_BANK[t] == SPREAD_BANK[tile]][-1], 1


class Carve:

    def __init__(self, arena, start=0):
        self.arena, self.at = arena, start

    def f32(self, cols, rows=P):
        v = self.arena[0:rows, self.at:self.at + cols]
        self.at += cols
        assert self.at <= self.arena.shape[1], self.at
        return v

    def bf16(self, cols, rows=P):
        return self.f32((cols + 1) // 2, rows).bitcast(BF16)

    def u8(self, cols, rows=P):
        return self.f32((cols + 3) // 4, rows).bitcast(U8)


class Semaphores:

    def __init__(self, nc):
        self.nc, self.held = nc, []

    def named(self, name):
        self.held.append(self.nc.alloc_semaphore(name))
        return self.held[-1]

    def clear(self):
        self.nc.all_engine_barrier()
        self.nc.clear_and_free_semaphores(self.held)
        self.nc.all_engine_barrier()
        self.held = []


def decoder_layer(nc, i_, out, NB):
    B = NB * G
    x1_d = nc.dram_tensor("x1_scratch", [L, B, D], F32).ap()
    xa_d = nc.dram_tensor("xa_scratch", [CTX, B * L], F32).ap()
    xin_d = nc.dram_tensor("xin_scratch", [DH, L, B, P], F32).ap()
    y_d = nc.dram_tensor("y_scratch", [L, B, D], F32).ap()
    kr_d = nc.dram_tensor("kernel_scratch", [D, 2 * L], F32).ap()
    wf_d = nc.dram_tensor("film_scratch", [CTX + 1, MOD], F32).ap()
    with ExitStack() as ctx:
        arena = ctx.enter_context(nc.sbuf_tensor("arena", [P, 53200], F32))
        psum = ctx.enter_context(nc.psum_tensor("psum", [P, 8, 512], F32))
        sems = Semaphores(nc)
        setup(nc, sems, i_, arena, psum, kr_d, wf_d)
        sems.clear()
        pass1(nc, sems, i_, arena, psum, x1_d, xa_d, xin_d, wf_d, NB)
        sems.clear()
        pass2(nc, sems, arena, psum, xin_d, y_d, kr_d, B)
        sems.clear()
        pass3(nc, sems, i_, arena, psum, x1_d, xa_d, y_d, wf_d, out, NB)


def all_blocks(eng, iteration, NB):
    iteration(0, 0, True, False)
    if NB > 2:
        iteration(1, 1, True, True)
        if NB > 4:
            with eng.Fori(0, (NB - 4) // 2, 1) as q:
                iteration(q * 2 + 2, 0, True, True)
                iteration(q * 2 + 3, 1, True, True)
        iteration(NB - 2, 0, True, True)
    iteration(NB - 1, 1, False, True)


def identity(nc, eng, ident, sem):
    eng.memset(ident, 0.0).then_inc(sem, 1)
    eng.wait_ge(sem, 1)
    eng.affine_select(out=ident, in_=ident, compare_op=ALU.not_equal, fill=1.0, base=0,
                      pattern=[[-1, P]], channel_multiplier=1).then_inc(sem, 1)


def setup(nc, sems, i_, arena, psum, kr_d, wf_d):
    NE, NR, NG = 35, 16, 8
    TWO_PI = 6.283185307179586
    MAGIC = 12582912.0
    C1 = 6.28125
    C2 = 0.0019340515136718750
    C3 = TWO_PI - C1 - C2
    PI = 3.1415925
    with ExitStack() as ctx:
        def sem(n):
            return sems.named(n)
        loaded, film_mm, film_sb, film_st = sem("loaded"), sem("film_folded"), sem("film_gated"), sem("film_stored")
        consts, dve_step, dt_ready, mag_a = sem("s_consts"), sem("dve_step"), sem("dt_ready"), sem("mag_a")
        angles, sines, mags, tables, kmm, ksb, kst = (sem(n) for n in (
            "angles", "sines", "mags", "tables", "kernel_mm", "kernel_sb", "kernel_stored"))
        zero_st, bias_row, tanh_a = sem("zeros_ready"), sem("bias_row"), sem("tanh_a")
        gained = sem("gained")
        cv = Carve(arena)
        wv = cv.f32(DH * CTX).rearrange("p (k c) -> p k c", k=DH)
        wf = cv.f32(DH * MOD).rearrange("p (k c) -> p k c", k=DH)
        fold0, fold1 = cv.f32(MOD), cv.f32(MOD, CT2)
        brow = cv.f32(MOD, 1)
        gate = cv.f32(1)
        s4 = cv.f32(4 * D).rearrange("p (a d) -> p a d", a=4)
        are, aim, cre, cim = (s4[:, k] for k in range(4))
        dt = cv.f32(D)
        a, b = cv.f32(D), cv.f32(D)
        tab = cv.f32(NE * D).rearrange("p (e d) -> p e d", e=NE)
        turns = cv.f32(NE * D).rearrange("p (e d) -> p e d", e=NE)
        mag = cv.f32((NR + NG) * D).rearrange("p (e d) -> p e d", e=NR + NG)
        tmp = [cv.f32(D) for _ in range(8)]
        ph = cv.f32(5)
        gb = cv.f32(2 * D)
        drow = cv.f32(16 * D, 1).rearrange("p (d j) -> p d j", j=16)
        last8 = cv.f32(8, 1)
        ksbuf = cv.f32(16 * D, 8)
        zeros = cv.f32(2 * L)
        dsk = cv.f32(D, 1)
        block = ctx.enter_context(nc.Block())

        @block.sync
        def _(sp):
            for dst, src in (
                (wv, i_["wv"]), (wf, i_["wf"]), (brow, i_["film_b"]),
                (gate, i_["wide"][0:1, NW - 1:NW].to_broadcast([P, 1])),
                (s4[0:SM], i_["s4"]), (s4[SM:P], i_["s4"]), (dt, i_["log_dt"].to_broadcast([P, D])), (dsk, i_["d_skip"]),
                (gb, i_["wide"][0:1, 0:2 * D].to_broadcast([P, 2 * D])),
            ):
                sp.dma_start(dst, src).then_inc(loaded, 16)
            sp.wait_ge(gained, 3)
            sp.dma_start(wf_d[0:P], fold0).then_inc(film_st, 16)
            sp.dma_start(wf_d[P:CTX], fold1).then_inc(film_st, 16)
            sp.dma_start(wf_d[CTX:CTX + 1], brow).then_inc(film_st, 16)
            sp.wait_ge(zero_st, 1)
            sp.dma_start(kr_d.rearrange("(h p) j -> p h j", p=P)[:, :, L:2 * L],
                         zeros.rearrange("p (h j) -> p h j", h=DH)).then_inc(kst, 16)
            sp.wait_ge(ksb, 8)
            for k in range(NG):
                sp.dma_start(kr_d[:, 16 * k:16 * k + 16][None], ksbuf[k:k + 1].rearrange("p (d j) -> p d j", j=16))\
                  .then_inc(kst, 16)
            sp.wait_ge(film_st, 48)
            sp.wait_ge(kst, 16 * (NG + 1))

        @block.gpsimd
        def _(pool):
            pool.memset(zeros, 0.0).then_inc(zero_st, 1)
        @block.tensor
        def _(pe):
            pe.wait_ge(loaded, 16 * 9)
            for n, (lo, hi) in enumerate(((0, P), (P, CTX))):
                for half in range(2):
                    for k in range(DH):
                        mm = pe.matmul(psum[0:hi - lo, 2 * n + half], wv[:, k, lo:hi],
                                       wf[:, k, half * 512:(half + 1) * 512], start=k == 0, stop=k == DH - 1)
                    mm.then_inc(film_mm, 1)
            pe.wait_ge(film_sb, 4)
            pe.wait_ge(consts, 14)
            pe.wait_ge(tables, 1)
            for q in range(8):
                for dd in range(32):
                    d = 32 * q + dd
                    o = psum[0:8, q, 16 * dd:16 * dd + 16]
                    pe.matmul(o, tab[:, NR:NR + NG, d], tab[:, 0:NR, d], start=True, stop=False)
                    mm = pe.matmul(o, last8, drow[:, d], start=False, stop=True)
                mm.then_inc(kmm, 1)

        @block.scalar
        def _(act):
            act.wait_ge(loaded, 16 * 9)
            act.activation(dt, dt, ACT.Exp).then_inc(dt_ready, 1)
            act.wait_ge(mag_a, 1)
            for e in range(NR):
                act.activation(mag[:, e], a, ACT.Exp, scale=float(NR - 1 - e)).then_inc(mags, 1)
            for e in range(NG):
                act.activation(mag[:, NR + e], a, ACT.Exp, scale=float(16 * (NG - 1 - e))).then_inc(mags, 1)
            act.activation(tmp[0], a, ACT.Tanh, scale=0.5).then_inc(tanh_a, 1)
            for n in range(4):
                rows, dst = (P, fold0) if n < 2 else (CT2, fold1)
                act.wait_ge(film_mm, n + 1)
                act.activation(dst[0:rows, (n % 2) * 512:(n % 2) * 512 + 512], psum[0:rows, n], ACT.Identity,
                               scale=gate[0:rows]).then_inc(film_sb, 1)
            act.activation(brow, brow, ACT.Identity, scale=gate[0:1]).then_inc(bias_row, 1)
            for half in range(2):
                act.wait_ge(bias_row, half + 1)
                act.activation(brow[:, half * 512:half * 512 + D], brow[:, half * 512:half * 512 + D],
                               ACT.Identity, bias=1.0).then_inc(bias_row, 1)
            act.wait_ge(angles, 1)
            act.activation(tab, tab, ACT.Sin).then_inc(sines, 1)
            for q in range(8):
                act.wait_ge(kmm, q + 1)
                act.copy(ksbuf[:, 512 * q:512 * q + 512], psum[0:8, q]).then_inc(ksb, 1)

        @block.vector
        def _(dve):
            count = [0]

            def link(ins):
                ins.then_inc(dve_step, 1)
                count[0] += 1
                dve.wait_ge(dve_step, count[0])

            def tt(o, x, y, op):
                link(dve.tensor_tensor(o, x, y, op))

            dve.memset(ph[0:SM, 0:1], TWO_PI / 4).then_inc(consts, 1)
            dve.memset(ph[SM:P, 0:1], 0.0).then_inc(consts, 1)
            dve.memset(ph[0:SM, 1:2], 0.0).then_inc(consts, 1)
            dve.memset(ph[SM:P, 1:2], TWO_PI / 4).then_inc(consts, 1)
            dve.memset(ph[0:SM, 2:3], 0.25).then_inc(consts, 1)
            dve.memset(ph[SM:P, 2:3], 0.0).then_inc(consts, 1)
            dve.memset(ph[0:SM, 3:4], 0.0).then_inc(consts, 1)
            dve.memset(ph[SM:P, 3:4], 0.25).then_inc(consts, 1)
            dve.memset(ph[0:SM, 4:5], 2.0).then_inc(consts, 1)
            dve.memset(ph[SM:P, 4:5], -2.0).then_inc(consts, 1)
            dve.memset(drow, 0.0).then_inc(consts, 1)
            dve.memset(last8, 0.0).then_inc(consts, 1)
            dve.wait_ge(consts, 12)
            dve.memset(last8[:, 7:8], 1.0).then_inc(consts, 1)
            dve.wait_ge(loaded, 16 * 9)
            dve.tensor_copy(drow[:, :, 15], dsk).then_inc(consts, 1)
            dve.wait_ge(dt_ready, 1)
            dve.tensor_tensor(a, are, dt, ALU.mult).then_inc(mag_a, 1)
            tt(b, aim, dt, ALU.mult)
            exps = [NR - 1 - e for e in range(NR)] + [16 * (NG - 1 - e) for e in range(NG)] * 2 + [1, 1, 0.5]
            for e, x in enumerate(exps):
                last = dve.tensor_scalar(tab[:, e], b, float(x), None, ALU.mult)
            link(last)
            dve.wait_ge(consts, 14)
            groups = ((0, NR + NG, ph[:, 2:3], ph[:, 0:1]), (NR + NG, NR + 2 * NG, ph[:, 3:4], ph[:, 1:2]),
                      (NE - 3, NE - 2, 0.25, TWO_PI / 4), (NE - 2, NE, 0.0, 0.0))
            for lo, hi, turn, _ in groups:
                last = dve.tensor_scalar(turns[:, lo:hi], tab[:, lo:hi], 1 / TWO_PI, turn, ALU.mult, ALU.add)
            link(last)
            link(dve.tensor_scalar(turns, turns, MAGIC, -MAGIC, ALU.add, ALU.add))
            for part in (C1, C2, C3):
                flat = tab.rearrange("p e d -> p (e d)")
                link(dve.scalar_tensor_tensor(out=flat, in0=turns.rearrange("p e d -> p (e d)"), scalar=-part,
                                              in1=flat, op0=ALU.mult, op1=ALU.add))
            for lo, hi, _, phase in groups:
                last = dve.tensor_scalar(tab[:, lo:hi], tab[:, lo:hi], phase, PI, ALU.add, ALU.min)
            link(last)
            dve.tensor_scalar(tab, tab, -PI, None, ALU.max).then_inc(angles, 1)
            t, em, den, er, ei, x, qr, qi = tmp
            dve.wait_ge(tanh_a, 1)
            link(dve.tensor_scalar(em, t, -0.5, 0.5, ALU.mult, ALU.add))
            link(dve.reciprocal(em, em))
            tt(em, em, t, ALU.mult)
            tt(den, are, are, ALU.mult)
            tt(x, aim, aim, ALU.mult)
            tt(den, den, x, ALU.add)
            link(dve.reciprocal(den, den))
            dve.wait_ge(film_sb, 4)
            dve.wait_ge(bias_row, 3)
            for rows, v in ((P, fold0), (CT2, fold1), (1, brow)):
                scale, shift = v[0:rows, 0:D], v[0:rows, D:2 * D]
                tt(x[0:rows], scale, gb[0:rows, D:2 * D], ALU.mult)
                tt(shift, shift, x[0:rows], ALU.add)
                dve.tensor_tensor(scale, scale, gb[0:rows, 0:D], ALU.mult).then_inc(gained, 1)
            dve.wait_ge(sines, 1)
            tt(x, tab[:, NE - 1], tab[:, NE - 1], ALU.mult)
            tt(er, em, tab[:, NE - 3], ALU.mult)
            link(dve.scalar_tensor_tensor(out=er, in0=x, scalar=-2.0, in1=er, op0=ALU.mult, op1=ALU.add))
            link(dve.scalar_tensor_tensor(out=ei, in0=em, scalar=1.0, in1=tab[:, NE - 2], op0=ALU.add, op1=ALU.mult))
            tt(qr, er, are, ALU.mult)
            tt(x, ei, aim, ALU.mult)
            tt(qr, qr, x, ALU.add)
            tt(qr, qr, den, ALU.mult)
            tt(qi, ei, are, ALU.mult)
            tt(x, er, aim, ALU.mult)
            tt(qi, qi, x, ALU.subtract)
            tt(qi, qi, den, ALU.mult)
            tt(er, cre, qr, ALU.mult)
            tt(x, cim, qi, ALU.mult)
            tt(er, er, x, ALU.subtract)
            tt(ei, cre, qi, ALU.mult)
            tt(x, cim, qr, ALU.mult)
            tt(ei, ei, x, ALU.add)
            link(dve.tensor_scalar(er, er, ph[:, 4:5], None, ALU.mult))
            link(dve.tensor_scalar(ei, ei, -2.0, None, ALU.mult))
            g0, g1 = tab[:, NR:NR + NG], tab[:, NR + NG:NR + 2 * NG]
            tt(g0, g0, er[:, None, :].to_broadcast([P, NG, D]), ALU.mult)
            tt(g1, g1, ei[:, None, :].to_broadcast([P, NG, D]), ALU.mult)
            tt(g0, g0, g1, ALU.add)
            dve.wait_ge(mags, NR + NG)
            tt(tab[:, 0:NR + NG], tab[:, 0:NR + NG], mag, ALU.mult)
            dve.memset(turns[:, 0, 0:1], 0.0).then_inc(tables, 1)

def pass1(nc, sems, i_, arena, psum, x1_d, xa_d, xin_d, wf_d, NB):
    with ExitStack() as ctx:
        S = {n: sems.named(n) for n in PER}
        w_ld = sems.named("w_ld")
        pool_step = sems.named("pool_step")
        bias_one = sems.named("bias_one")
        zeroed = sems.named("zeroed")
        alog_exp = sems.named("alog_exp")
        halved = sems.named("halved")
        diag_made = sems.named("diag_made")

        cv = Carve(arena)
        win = cv.f32(DH * 2 * DI).rearrange("p (k e) -> p k e", k=DH)
        wxp = cv.f32(C * 96).rearrange("p (c r) -> p c r", c=C)
        wdt = cv.f32(DI, R)
        wout = cv.f32(C * D).rearrange("p (c d) -> p c d", c=C)
        wq = cv.f32(DH * P).rearrange("p (k e) -> p k e", k=DH)
        wk0, wk1 = cv.f32(P), cv.f32(P, CT2)
        wf0, wf1 = cv.f32(2 * D), cv.f32(2 * D, CT2 + 1)
        vec = cv.f32(NV)
        ident = cv.f32(P)
        sel3 = cv.bf16(2 * NS)
        negA = cv.f32(C * NS).rearrange("p (c n) -> p c n", c=C)
        half_w = cv.f32(20)
        diag_d = cv.f32(C * P).rearrange("p (c q) -> p c q", c=C)

        xT = cv.f32(DH * T).rearrange("p (k t) -> p k t", k=DH)
        x1 = cv.f32(G * D).rearrange("p (b d) -> p b d", b=G)
        ctxT0, ctxT1 = cv.f32(T), cv.f32(T, CT2)
        ctxn = cv.f32(G * CTX).rearrange("p (b d) -> p b d", b=G)
        mask8, maskb, ones = cv.u8(T), cv.bf16(T), cv.bf16(P)
        tmask8, tmb = cv.u8(G), cv.f32(G)
        xs = [cv.f32(C * T).rearrange("p (c t) -> p c t", c=C) for _ in range(2)]
        zs = [cv.f32(C * T).rearrange("p (c t) -> p c t", c=C) for _ in range(2)]
        dt = [cv.f32(C * T).rearrange("p (c t) -> p c t", c=C) for _ in range(2)]
        uu = [cv.f32(C * T).rearrange("p (c t) -> p c t", c=C) for _ in range(2)]
        tmpA = cv.f32(C * T).rearrange("p (c t) -> p c t", c=C)
        tmpB = cv.f32(C * T).rearrange("p (c t) -> p c t", c=C)
        dtr_r1 = cv.f32(T)
        dtr, r1 = dtr_r1[0:R], dtr_r1[R:R + 2 * NS]
        mid = cv.bf16(T)[R:R + 2 * NS]
        bcp = [cv.bf16(T, 96) for _ in range(2)]
        Bb = cv.f32(NS * T).rearrange("p (n t) -> p n t", n=NS)
        ring = cv.f32(RING * T).rearrange("p (s t) -> p s t", s=RING)
        yg = cv.f32(C * T).rearrange("p (c t) -> p c t", c=C)
        xn = cv.f32(G * D).rearrange("p (b d) -> p b d", b=G)
        x1T = cv.f32(DH * T).rearrange("p (k t) -> p k t", k=DH)
        qT, kT = cv.f32(T), cv.f32(T)
        sc = cv.f32(H * P).rearrange("p (h g) -> p h g", h=H)
        left = cv.f32(H * P).rearrange("p (h g) -> p h g", h=H)
        diag = cv.f32(H * P).rearrange("p (h g) -> p h g", h=H)
        at = cv.f32(T).rearrange("p (b t) -> p b t", b=G)
        xa0, xa1 = cv.f32(T), cv.f32(T, CT2 + 1)
        stats = cv.f32(G * 6).rearrange("p (b s) -> p b s", b=G)
        mv = cv.f32(G * 2).rearrange("p (b s) -> p b s", b=G)
        ve, rs, eps, nhalf = cv.f32(G), cv.f32(G), cv.f32(G), cv.f32(G)
        v8 = cv.f32(KR * H * 8).rearrange("p (r h s) -> p r h s", r=KR, h=H)
        nmax, esum, rinv, rq = cv.f32(H), cv.f32(H), cv.f32(H), cv.f32(H)

        decay_ps, spread, y_ps, side = psum[:, 0:2], psum[:, 2:5], psum[:, 5], psum[:, 6:8]

        def tile_ps(name):
            return side[:, BANK[name]]

        def seqs(v):
            return v.rearrange("p (b t) -> p b t", b=G)

        def need(eng, name, i, k):
            count = i * PER[name] + k
            if not isinstance(count, int) or count > 0:
                eng.wait_ge(S[name], count)

        def need_apart(eng, *what):
            counts = [(name, i * PER[name] + k) for name, i, k in what]
            counts = [(name, n if isinstance(n, int) else eng.to_reg(n)) for name, n in counts]
            eng.wait_ge(w_ld, 16 * N_W)
            for name, count in counts:
                if not isinstance(count, int) or count > 0:
                    eng.wait_ge(S[name], count)

        def which_steps(front, back):
            return (FRONT if front else []) + (BACK if back else [])

        N_W = 10
        block = ctx.enter_context(nc.Block())

        @block.sync
        def _(sp):
            for dst, src in (
                (win, i_["in_proj"]), (wxp, i_["x_proj"]), (wdt, i_["dt_proj"]), (wout, i_["out_proj"]),
                (wq, i_["wq"]), (wk0, i_["wk"][0:P]), (wk1, i_["wk"][P:CTX]),
                (wf0, wf_d[0:P, 0:2 * D]), (wf1, wf_d[P:CTX + 1, 0:2 * D]), (vec, i_["vec"]),
            ):
                sp.dma_start(dst, src).then_inc(w_ld, 16)

            def load_xT(i):
                sp.dma_start(xT, i_["xT"][:, :, bass.ts(i, T)]).then_inc(S["ld_xT"], 16)

            def load_back(i):
                need(sp, "st_x1", i - 1, 16)
                need(sp, "xt_mm", i - 1, 2)
                need(sp, "film_mul", i - 1, G)
                sp.dma_start(x1, i_["x"][:, bass.ts(i, G), :]).then_inc(S["ld_x"], 16)
                need(sp, "k_mm", i - 1, 1)
                sp.dma_start(ctxT0, i_["ctxT"][0:P, bass.ts(i, T)]).then_inc(S["ld_ctxT"], 16)
                sp.dma_start(ctxT1, i_["ctxT"][P:CTX, bass.ts(i, T)]).then_inc(S["ld_ctxT"], 16)
                need(sp, "maskb", i - 1, 1)
                need(sp, "tmb", i - 1, 1)
                sp.dma_start(tmask8, i_["tmask"][:, bass.ts(i, G)]).then_inc(S["ld_mask"], 16)
                sp.dma_start(mask8, i_["vmask"][0:1, bass.ts(i, T)].to_broadcast([P, T])).then_inc(S["ld_mask"], 16)
                need(sp, "xa_mm", i - 1, 2)
                sp.dma_start(ctxn, i_["ctx"][:, bass.ts(i, G), :]).then_inc(S["ld_ctx"], 16)

            def store_x1(i):
                need(sp, "x1", i, 4)
                sp.dma_start(x1_d[:, bass.ts(i, G), :], x1).then_inc(S["st_x1"], 16)

            def store_rest(i):
                need(sp, "xaT0", i, 1)
                sp.dma_start(xa_d[0:P, bass.ts(i, T)], xa0).then_inc(S["st_xa"], 16)
                need(sp, "xaT1", i, 1)
                sp.dma_start(xa_d[P:CTX, bass.ts(i, T)], xa1[0:CT2]).then_inc(S["st_xa"], 16)

            def store_xin(i):
                need(sp, "film", i, G)
                for h in range(DH):
                    sp.dma_start(xin_d[h][:, bass.ts(i, G), :], xn[:, :, h * P:(h + 1) * P]).then_inc(S["st_xin"], 16)

            def iteration(i, ahead, back):
                if ahead:
                    need(sp, "in_mm", i + 1, 8)
                    load_xT(i + 2)
                if back:
                    store_x1(i - 1)
                    store_rest(i - 1)
                load_back(i)
                if back:
                    store_xin(i - 1)

            load_xT(0)
            need(sp, "in_mm", 0, 8)
            load_xT(1)
            iteration(0, NB > 2, False)
            if NB > 2:
                iteration(1, True, True)
                if NB > 4:
                    with sp.Fori(2, NB - 2, 1) as i:
                        iteration(i, True, True)
                iteration(NB - 2, False, True)
            iteration(NB - 1, False, True)
            store_x1(NB - 1)
            store_rest(NB - 1)
            store_xin(NB - 1)
            for n in ("st_x1", "st_xa", "st_xin"):
                sp.wait_ge(S[n], NB * PER[n])

        @block.tensor
        def _(pe):
            def take_bank(name, i, i_other, which):
                prev = bank_before(name, which)
                if prev is not None:
                    j = i if is_front(prev) == is_front(name) else i_other
                    need(pe, LAST_READ[prev][0], j, LAST_READ[prev][1])
                    if prev == "xp":
                        need(pe, "dtr", j, 1)
                else:
                    f = i if is_front(name) else i_other
                    b = i_other if is_front(name) else i
                    need(pe, "vrelu", f - 1, C)
                    need(pe, "film", b - 1, G)

            def step(name, i, par, other, which):
                def bank(tile):
                    take_bank(tile, i, other, which)
                    return tile_ps(tile)

                if name[:2] == "xc" or name[0] == "z":
                    c = int(name[-1])
                    e0 = c * P + (DI if name[0] == "z" else 0)
                    ps = bank(name)
                    if name == "xc0":
                        need(pe, "ld_xT", i, 16)
                    for k in range(DH):
                        mm = pe.matmul(ps, win[:, k, e0:e0 + P], xT[:, k], start=k == 0, stop=k == DH - 1)
                    mm.then_inc(S["in_mm"], 1)
                elif name == "xp":
                    ps = bank(name)
                    need(pe, "xs", i, C)
                    for c in range(C):
                        mm = pe.matmul(ps[0:96], wxp[:, c], xs[par][:, c], start=c == 0, stop=c == C - 1)
                    mm.then_inc(S["xp_mm"], 1)
                elif name[:2] == "dt":
                    c = int(name[-1])
                    ps = bank(name)
                    if c == 0:
                        need(pe, "dtr", i, 1)
                    pe.matmul(ps, wdt[:, c * P:(c + 1) * P], dtr, start=True, stop=True).then_inc(S["dt_mm"], 1)
                elif name[:2] == "op":
                    b = int(name[-1])
                    ps = tile_ps(f"o{b // 2}") if b % 2 else bank(f"o{b // 2}")
                    if b == 0:
                        need(pe, "yg", i, C)
                    for c in range(C):
                        mm = pe.matmul(ps[:, b % 2 * D:(b % 2 + 1) * D], yg[:, c, b * L:(b + 1) * L],
                                       wout[:, c], start=c == 0, stop=c == C - 1)
                    if b % 2:
                        mm.then_inc(S["o_mm"], 1)
                elif name == "x1T":
                    for k in range(DH):
                        ps = bank(f"t{k}")
                        if k == 0:
                            need(pe, "x1", i, G)
                        for b in range(G):
                            mm = pe.transpose(ps[:, b * L:(b + 1) * L], x1[:, b, k * P:(k + 1) * P], ident)
                        mm.then_inc(S["xt_mm"], 1)
                elif name == "qk":
                    ps = bank("q")
                    need(pe, "x1T", i, DH)
                    for k in range(DH):
                        mm = pe.matmul(ps, wq[:, k], x1T[:, k], start=k == 0, stop=k == DH - 1)
                    mm.then_inc(S["q_mm"], 1)
                    ps = bank("k")
                    need(pe, "ld_ctxT", i, 32)
                    pe.matmul(ps, wk0, ctxT0, start=True, stop=False)
                    pe.matmul(ps, wk1, ctxT1, start=False, stop=True).then_inc(S["k_mm"], 1)
                elif name[:2] == "sc":
                    b = int(name[-1])
                    ps = bank(f"s{b}")
                    if b == 0:
                        need(pe, "qT", i, 1)
                        need(pe, "kT", i, 1)
                        need(pe, "maskb", i, 1)
                    for h in range(H):
                        rows = slice(h * HD, (h + 1) * HD)
                        if h:
                            need(pe, "s_mm", i, b * H + h)
                        o, row = ps[:, h * P:(h + 1) * P], slice(h * HD, h * HD + 1)
                        pe.matmul(o, ones[row], maskb[row, b * L:(b + 1) * L], start=True, stop=False)
                        pe.matmul(o, qT[rows, b * L:(b + 1) * L], kT[rows, b * L:(b + 1) * L],
                                  start=False, stop=True).then_inc(S["s_mm"], 1)
                elif name[:2] == "at":
                    b = int(name[-1])
                    ps = bank(f"a{b}")
                    need(pe, "em", i, b + 1)
                    need(pe, "diag", i, b + 1)
                    for h in range(H):
                        mm = pe.matmul(ps[:, 0:L], sc[:, h], diag[:, h], start=h == 0, stop=h == H - 1)
                    mm.then_inc(S["at_mm"], 1)
                elif name == "xa":
                    for n, (lo, hi) in enumerate(((0, P), (P, CTX))):
                        ps = bank(f"xa{n}")
                        if n == 0:
                            need(pe, "atT", i, G)
                            need(pe, "ld_ctx", i, 16)
                        for b in range(G):
                            mm = pe.matmul(ps[0:hi - lo, b * L:(b + 1) * L], ctxn[:, b, lo:hi], at[:, b],
                                           start=True, stop=True)
                        mm.then_inc(S["xa_mm"], 1)
                elif name[:4] == "film":
                    b = int(name[-1])
                    ps = bank(f"f{b}")
                    if b == 0:
                        need(pe, "xaT0", i, 1)
                        need(pe, "xaT1", i, 1)
                    pe.matmul(ps, xa0[:, b * L:(b + 1) * L], wf0, start=True, stop=False)
                    pe.matmul(ps, xa1[0:CT2 + 1, b * L:(b + 1) * L], wf1, start=False, stop=True)\
                        .then_inc(S["film_mm"], 1)

            def spread_out(kind, n, i, par):
                if kind == "b" and n == 0:
                    need(pe, "bcp", i, 1)
                (held, m), ago = spread_before((kind, n))
                if held == "b":
                    need(pe, "bb_sb", i - ago, m + 1)
                else:
                    need(pe, "hc", i - ago, m + 1)
                row = n if kind == "b" else NS + n % NS
                pe.matmul(spread[:, SPREAD_BANK[kind, n]], sel3[0:96, row:row + 1].to_broadcast([96, P]), bcp[par],
                          start=True, stop=True).then_inc(S["bb_mm" if kind == "b" else "cb_mm"], 1)

            def sum_states(i, par, u):
                if u < 0:
                    i, par, u = i - 1, 1 - par, C * NS + u
                need(pe, "hc", i, u + 1)
                c, n = u // NS, u % NS
                if n == 0:
                    if c == 0:
                        need(pe, "y", i - 1, C)
                    else:
                        need(pe, "y", i, c)
                    pe.matmul(y_ps, diag_d[:, c], xs[par][:, c], start=True, stop=False)
                pe.matmul(y_ps, ident, ring[:, u % RING], start=False, stop=n == NS - 1).then_inc(S["nsum"], 1)

            def iteration(i, par, front, back):
                which = ([True] if front else []) + ([False] if back else [])
                names = which_steps(front, back)
                for n in range(B_AHEAD):
                    spread_out("b", n, i, par)
                for u in range(C * NS):
                    if B_AHEAD + u < NS:
                        spread_out("b", B_AHEAD + u, i, par)
                    spread_out("c", u, i, par)
                    if u >= SUM_LAG or back:
                        sum_states(i, par, u - SUM_LAG)
                    for s in steps_at(PE_AT, u, names):
                        if s in FRONT:
                            step(s, i + 1, 1 - par, i - 1, which)
                        else:
                            step(s, i - 1, 1 - par, i + 1, which)

            pe.wait_ge(pool_step, 8)
            pe.wait_ge(bias_one, 2)
            pe.wait_ge(diag_made, C)
            pe.wait_ge(w_ld, 16 * N_W)
            for s in [s for s in PE_AT if s in FRONT]:
                step(s, 0, 0, 0, [True])
            all_blocks(pe, iteration, NB)
            for u in range(SUM_LAG):
                sum_states(NB, 0, u - SUM_LAG)
            for s in [s for s in PE_AT if s in BACK]:
                step(s, NB - 1, 1, NB, [False])

        @block.scalar
        def _(act):
            def step(name, i, par):
                c = int(name[-1]) if name[-1].isdigit() else 0
                if name[:2] == "xc":
                    need(act, "in_mm", i, c + 1)
                    if c == 0:
                        need(act, "nsum", i - 2, C * NS)
                    act.activation(xs[par][:, c], tile_ps(name), ACT.Identity, bias=half_w[:, 16 + c:17 + c],
                                   scale=half_w[:, 4 * c + 3:4 * c + 4]).then_inc(S["conv0"], 1)
                elif name[0] == "z":
                    tanh_x(i, par, c)
                    need(act, "in_mm", i, C + c + 1)
                    if c == 0:
                        need(act, "yg", i - 2, C)
                    act.activation(zs[par][:, c], tile_ps(name), ACT.Identity, scale=0.5).then_inc(S["zhalf"], 1)
                    if c == 0:
                        need(act, "dt", i - 1, C)
                    act.activation(tmpA[:, c], tile_ps(name), ACT.Tanh, scale=0.5).then_inc(S["zth"], 1)
                    need(act, "xth", i, c + 1)
                    act.activation(tmpB[:, c], tmpB[:, c], ACT.Identity, bias=1.0).then_inc(S["xt1"], 1)
                    need(act, "zth", i, c + 1)
                    act.activation(tmpA[:, c], tmpA[:, c], ACT.Identity, bias=1.0).then_inc(S["zt1"], 1)
                elif name == "xp":
                    need(act, "xp_mm", i, 1)
                    need(act, "dt_mm", i - 1, C)
                    act.copy(dtr, tile_ps("xp")[0:R]).then_inc(S["dtr"], 1)
                    need(act, "cb_mm", i - 2, C * NS)
                    act.copy(bcp[par][R:R + 2 * NS], tile_ps("xp")[R:R + 2 * NS]).then_inc(S["bc_hi"], 1)
                elif name == "xq":
                    need(act, "bc_r1", i, 1)
                    act.copy(mid, r1).then_inc(S["bc_mid"], 1)
                    act.copy(bcp[par][NS * 2:NS * 4], r1).then_inc(S["bc_cp"], 1)
                elif name[:2] == "dt":
                    need(act, "dt_mm", i, c + 1)
                    need(act, "zs", i, c + 1)
                    act.activation(tmpA[:, c], tile_ps(name), ACT.Abs, bias=vec[:, V_DTB + c:V_DTB + c + 1])\
                        .then_inc(S["vabs"], 1)
                    act.activation(dt[par][:, c], tile_ps(name), ACT.Relu, bias=vec[:, V_DTB + c:V_DTB + c + 1])\
                        .then_inc(S["vrelu"], 1)
                    need(act, "vabs", i, c + 1)
                    act.activation(tmpA[:, c], tmpA[:, c], ACT.Exp, scale=-1.0).then_inc(S["vexp"], 1)
                    if c == 0:
                        need(act, "bx", i - 2, C * NS)
                    need(act, "vexp", i, c + 1)
                    act.activation(uu[par][:, c], tmpA[:, c], ACT.Identity, bias=1.0).then_inc(S["w1"], 1)
                    need(act, "w1", i, c + 1)
                    act.activation(uu[par][:, c], uu[par][:, c], ACT.Identity, scale=-1.0, bias=1.0)\
                        .then_inc(S["cor1"], 1)
                elif name == "ln":
                    for c in range(C):
                        need(act, "vexp", i, c + 1)
                        need(act, "xs", i, c + 1)
                        act.activation(tmpB[:, c], tmpA[:, c], ACT.Ln, bias=1.0).then_inc(S["vln"], 1)
                elif name == "x1T":
                    for k in range(DH):
                        need(act, "xt_mm", i, k + 1)
                        if k == 0:
                            need(act, "q_mm", i - 1, 1)
                        act.copy(x1T[:, k], tile_ps(f"t{k}")).then_inc(S["x1T"], 1)
                elif name == "qk":
                    need(act, "q_mm", i, 1)
                    need(act, "s_mm", i - 1, G * H)
                    act.copy(qT, tile_ps("q")).then_inc(S["qT"], 1)
                    need(act, "k_mm", i, 1)
                    act.copy(kT, tile_ps("k")).then_inc(S["kT"], 1)
                elif name == "y3":
                    read_y(i, C - 1)
                elif name[:2] == "sc":
                    need(act, "s_mm", i, (c + 1) * H)
                    if c == 0:
                        need(act, "at_mm", i - 1, G)
                    else:
                        need(act, "at_mm", i, c)
                    act.copy(sc, tile_ps(name[0] + name[-1]).rearrange("p (h g) -> p h g", h=H))\
                        .then_inc(S["smask"], 1)
                elif name[:2] == "sm":
                    need(act, "nmax", i, c + 1)
                    need(act, "took", i, c * KR + 1)
                    for h in range(H):
                        a = act.activation(sc[:, h], sc[:, h], ACT.Exp, bias=nmax[:, h:h + 1], scale=HD ** -0.5)
                    a.then_inc(S["ex"], 1)
                elif name[:2] == "dg":
                    need(act, "rq", i, c + 1)
                    if c:
                        need(act, "at_mm", i, c)
                    else:
                        need(act, "at_mm", i - 1, G)
                    for h in range(H):
                        a = act.activation(diag[:, h], ident, ACT.Identity, scale=rq[:, h:h + 1])
                    a.then_inc(S["diag"], 1)
                elif name[:2] == "at":
                    need(act, "at_mm", i, c + 1)
                    if c == 0:
                        need(act, "xa_mm", i - 1, 2)
                    act.copy(at[:, c], tile_ps(f"a{c}")[:, 0:L]).then_inc(S["atT"], 1)
                elif name == "xa":
                    need(act, "xa_mm", i, 1)
                    need(act, "film_mm", i - 1, G)
                    need(act, "st_xa", i - 1, 32)
                    act.copy(xa0, tile_ps("xa0")).then_inc(S["xaT0"], 1)
                    need(act, "xa_mm", i, 2)
                    act.copy(xa1[0:CT2], tile_ps("xa1")[0:CT2]).then_inc(S["xaT1"], 1)

            def tanh_x(i, par, c):
                need(act, "conv", i, c + 1)
                if c == 0:
                    need(act, "dt", i - 1, C)
                act.activation(tmpB[:, c], xs[par][:, c], ACT.Tanh).then_inc(S["xth"], 1)

            def read_y(i, c):
                need(act, "nsum", i, (c + 1) * NS)
                if c == 0:
                    need(act, "o_mm", i - 1, 2)
                act.copy(yg[:, c], y_ps).then_inc(S["y"], 1)

            def copy_b(n, i):
                need(act, "bb_mm", i, n + 1)
                if n == 0:
                    need(act, "bx", i - 1, C * NS)
                act.copy(Bb[:, n], spread[:, SPREAD_BANK["b", n]]).then_inc(S["bb_sb"], 1)

            def iteration(i, par, front, back):
                names = which_steps(front, back)
                for n in range(B_AHEAD):
                    copy_b(n, i)
                for u in range(C * NS):
                    c, n = u // NS, u % NS
                    if n == 0:
                        need(act, "dt", i, c + 1)
                    if u >= 2:
                        need(act, "scan", i, u - 1)
                    else:
                        need(act, "scan", i - 1, C * NS - 1 + u)
                    act.activation(seqs(decay_ps[:, u % 2])[:, :, 1:L], seqs(dt[par][:, c])[:, :, 1:L],
                                   ACT.Exp, scale=negA[:, c, n:n + 1]).then_inc(S["decay"], 1)
                    if B_AHEAD + u < NS:
                        copy_b(B_AHEAD + u, i)
                    if u > NS and n == Y_AT:
                        read_y(i, c - 1)
                    for s in steps_at(ACT_AT, u, names):
                        if s in FRONT:
                            step(s, i + 1, 1 - par)
                        else:
                            step(s, i - 1, 1 - par)

            act.wait_ge(w_ld, 16 * N_W)
            act.activation(negA, vec[:, V_ALOG:V_ALOG + C * NS].rearrange("p (c n) -> p c n", c=C), ACT.Exp)\
                .then_inc(alog_exp, 1)
            act.wait_ge(alog_exp, 1)
            act.mul(negA, negA, -1.0).then_inc(alog_exp, 1)
            act.mul(half_w, vec[:, 0:20], 0.5).then_inc(halved, 1)
            act.wait_ge(alog_exp, 2)
            act.wait_ge(halved, 1)
            act.wait_ge(pool_step, 8)
            for c in range(C):
                act.activation(diag_d[:, c], ident, ACT.Identity, scale=vec[:, V_D + c:V_D + c + 1])\
                    .then_inc(diag_made, 1)
            act.wait_ge(zeroed, 2)
            for s in [s for s in ACT_AT if s in FRONT]:
                step(s, 0, 0)
            all_blocks(act, iteration, NB)
            for s in [s for s in ACT_AT if s in BACK]:
                step(s, NB - 1, 1)

        @block.vector
        def _(dve):
            def norm_stats(i, src, st, mvn):
                for b in range(G):
                    dve.bn_stats(stats[:, b], src[:, b]).then_inc(S[st], 1)
                need_apart(dve, (st, i, G))
                for b in range(G):
                    a = dve.bn_aggr(mv[:, b], stats[:, b])
                a.then_inc(S[mvn], 1)

            def step(name, i, par):
                c = int(name[-1]) if name[-1].isdigit() else 0
                if name[:2] == "xc":
                    need(dve, "conv0", i, c + 1)
                    for s in (1, 2, 3):
                        if s > 1:
                            need(dve, "tap", i, 2 * c + s - 1)
                        o = seqs(xs[par][:, c])[:, :, s:L]
                        dve.scalar_tensor_tensor(out=o, in0=seqs(tile_ps(name))[:, :, 0:L - s],
                                                 scalar=half_w[:, 4 * c + 3 - s:4 * c + 4 - s], in1=o,
                                                 op0=ALU.mult, op1=ALU.add)\
                           .then_inc(S["tap" if s < 3 else "conv"], 1)
                elif name == "xp":
                    need(dve, "bc_hi", i, 1)
                    dve.tensor_tensor(r1, tile_ps("xp")[R:R + 2 * NS], bcp[par][R:R + 2 * NS], ALU.subtract)\
                        .then_inc(S["bc_r1"], 1)
                elif name == "xq":
                    need(dve, "bc_mid", i, 1)
                    need(dve, "bc_cp", i, 1)
                    dve.tensor_tensor(bcp[par][0:NS * 2], r1, mid, ALU.subtract).then_inc(S["bcp"], 1)
                elif name == "ln1":
                    need(dve, "ld_x", i, 16)
                    for o in range(2):
                        need(dve, "o_mm", i, o + 1)
                        pair = x1[:, 2 * o:2 * o + 2]
                        dve.tensor_tensor(pair, tile_ps(f"o{o}").rearrange("p (b d) -> p b d", b=2), pair,
                                          ALU.add).then_inc(S["res"], 1)
                    need(dve, "res", i, 2)
                    need(dve, "film", i - 1, G)
                    norm_stats(i, x1, "st1", "mv1")
                elif name == "x1":
                    need(dve, "rs1", i, 1)
                    for b in range(G):
                        dve.tensor_scalar(x1[:, b], x1[:, b], mv[:, b, 0:1], rs[:, b:b + 1],
                                          ALU.subtract, ALU.mult).then_inc(S["x1"], 1)
                    need(dve, "x1", i, G)
                    norm_stats(i, x1, "st2", "mv2")
                elif name[:2] == "tk":
                    b, r = c, "abcd".index(name[2])
                    src = left if r else sc
                    n = b * KR + r
                    if r:
                        need_apart(dve, ("took", i, n))
                    else:
                        need_apart(dve, ("smask", i, b + 1))
                    for h in range(H):
                        a = dve.max(v8[:, r, h], src[:, h])
                    a.then_inc(S["v8"], 1)
                    need_apart(dve, ("v8", i, n + 1))
                    for h in range(H):
                        a = dve.match_replace(left[:, h], v8[:, r, h], src[:, h], NEG)
                    a.then_inc(S["took"], 1)
                    if r == 0:
                        if b:
                            need(dve, "ex", i, b)
                        dve.tensor_scalar(nmax, v8[:, 0, :, 0], -HD ** -0.5, None, ALU.mult).then_inc(S["nmax"], 1)
                elif name[:2] == "sm":
                    b = c
                    need(dve, "ex", i, b + 1)
                    need(dve, "took", i, (b + 1) * KR)
                    for h in range(H):
                        a = dve.scalar_tensor_tensor(out=sc[:, h], in0=left[:, h], scalar=NEG / 2, in1=sc[:, h],
                                                     op0=ALU.is_lt, op1=ALU.mult, accum_out=esum[:, h:h + 1])
                    a.then_inc(S["em"], 1)
                    need(dve, "em", i, b + 1)
                    dve.reciprocal(rinv, esum).then_inc(S["rinv"], 1)
                    need(dve, "rinv", i, b + 1)
                    need(dve, "tmb", i, 1)
                    if b:
                        need(dve, "diag", i, b)
                    dve.tensor_scalar(rq, rinv, tmb[:, b:b + 1], None, ALU.mult).then_inc(S["rq"], 1)
                elif name[:4] == "film":
                    b, ps = c, tile_ps(f"f{c}")
                    need(dve, "film_mm", i, b + 1)
                    if b == 0:
                        need(dve, "rs2", i, 1)
                        need(dve, "st_xin", i - 1, 32)
                    dve.scalar_tensor_tensor(out=xn[:, b], in0=x1[:, b], scalar=mv[:, b, 0:1], in1=ps[:, 0:D],
                                             op0=ALU.subtract, op1=ALU.mult).then_inc(S["film_mul"], 1)
                    need(dve, "film_mul", i, b + 1)
                    dve.scalar_tensor_tensor(out=xn[:, b], in0=xn[:, b], scalar=rs[:, b:b + 1], in1=ps[:, D:2 * D],
                                             op0=ALU.mult, op1=ALU.add).then_inc(S["film"], 1)

            def times_c(i, u):
                need(dve, "scan", i, u + 1)
                need(dve, "cb_mm", i, u + 1)
                h = ring[:, u % RING]
                dve.tensor_tensor(h, h, spread[:, SPREAD_BANK["c", u]], ALU.mult).then_inc(S["hc"], 1)

            def iteration(i, par, front, back):
                names = which_steps(front, back)
                for u in range(C * NS):
                    need(dve, "decay", i, u + 1)
                    need(dve, "bx", i, u + 1)
                    s = ring[:, u % RING]
                    dve.tensor_tensor_scan(s, decay_ps[:, u % 2], s, 0.0, ALU.mult, ALU.add).then_inc(S["scan"], 1)
                    if u:
                        times_c(i, u - 1)
                    for st in steps_at(DVE_AT, u, names):
                        if st in FRONT:
                            step(st, i + 1, 1 - par)
                        else:
                            step(st, i - 1, 1 - par)
                times_c(i, C * NS - 1)

            dve.memset(xa1[CT2:CT2 + 1], 1.0).then_inc(bias_one, 1)
            dve.memset(ones, 1.0).then_inc(bias_one, 1)
            for k in range(2):
                dve.memset(seqs(decay_ps[:, k])[:, :, 0:1], 0.0).then_inc(zeroed, 1)
            dve.wait_ge(w_ld, 16 * N_W)
            dve.wait_ge(halved, 1)
            for s in [s for s in DVE_AT if s in FRONT]:
                step(s, 0, 0)
            all_blocks(dve, iteration, NB)
            for s in [s for s in DVE_AT if s in BACK]:
                step(s, NB - 1, 1)

        @block.gpsimd
        def _(pool):
            def inverse_deviation(i, mvn, ven, rsn):
                need(pool, mvn, i, 1)
                pool.tensor_tensor(ve, mv[:, :, 1], eps, ALU.add).then_inc(S[ven], 1)
                need(pool, ven, i, 1)
                pool.tensor_tensor(rs, ve, nhalf, ALU.pow).then_inc(S[rsn], 1)

            def gate(i, par, c):
                need(pool, "y", i, c + 1)
                need(pool, "zs", i, c + 1)
                pool.tensor_tensor(yg[:, c], yg[:, c], zs[par][:, c], ALU.mult).then_inc(S["yg"], 1)

            def step(name, i, par):
                c = int(name[-1]) if name[-1].isdigit() else 0
                if name == "y3":
                    gate(i, par, C - 1)
                elif name[0] == "z":
                    need(pool, "xt1", i, c + 1)
                    pool.tensor_tensor(xs[par][:, c], xs[par][:, c], tmpB[:, c], ALU.mult).then_inc(S["xs"], 1)
                    need(pool, "zt1", i, c + 1)
                    pool.tensor_tensor(zs[par][:, c], zs[par][:, c], tmpA[:, c], ALU.mult).then_inc(S["zs"], 1)
                elif name == "rs1":
                    inverse_deviation(i, "mv1", "ve1", "rs1")
                elif name == "rs2":
                    need(pool, "x1", i, G)
                    inverse_deviation(i, "mv2", "ve2", "rs2")
                elif name == "mask":
                    need_apart(pool, ("ld_mask", i, 32), ("s_mm", i - 1, G * H))
                    pool.tensor_scalar(maskb, mask8, -1.0, -OFF, ALU.add, ALU.mult)\
                        .then_inc(S["maskb"], 1)
                    need_apart(pool, ("rq", i - 1, G))
                    pool.tensor_scalar(tmb, tmask8, 1.0 / H, None, ALU.mult).then_inc(S["tmb"], 1)
                elif name[:2] == "sp":
                    t = uu[par][:, c]
                    need(pool, "vln", i, c + 1)
                    need(pool, "cor1", i, c + 1)
                    pool.tensor_tensor(tmpA[:, c], tmpA[:, c], t, ALU.add).then_inc(S["cor2"], 1)
                    need(pool, "cor2", i, c + 1)
                    pool.tensor_tensor(tmpB[:, c], tmpB[:, c], tmpA[:, c], ALU.add).then_inc(S["cor3"], 1)
                    need(pool, "cor3", i, c + 1)
                    need(pool, "vrelu", i, c + 1)
                    d = dt[par][:, c]
                    pool.tensor_tensor(d, d, tmpB[:, c], ALU.add).then_inc(S["dt"], 1)
                    need(pool, "dt", i, c + 1)
                    need(pool, "xs", i, c + 1)
                    pool.tensor_tensor(t, d, xs[par][:, c], ALU.mult).then_inc(S["u"], 1)

            def iteration(i, par, front, back):
                names = which_steps(front, back)
                for u in range(C * NS):
                    c, n = u // NS, u % NS
                    if n == 0:
                        need(pool, "u", i, c + 1)
                    if c == 0:
                        need(pool, "bb_sb", i, n + 1)
                    if u >= RING:
                        need(pool, "nsum", i, u - RING + 1)
                    else:
                        need(pool, "nsum", i - 1, C * NS - RING + u + 1)
                    pool.tensor_tensor(ring[:, u % RING], uu[par][:, c], Bb[:, n], ALU.mult).then_inc(S["bx"], 1)
                    if u > NS and u % NS == GATE_AT:
                        gate(i, par, u // NS - 1)
                    for s in steps_at(POOL_AT, u, names):
                        if s in FRONT:
                            step(s, i + 1, 1 - par)
                        else:
                            step(s, i - 1, 1 - par)

            identity(nc, pool, ident, pool_step)
            pool.memset(sel3[0:96], 0.0).then_inc(pool_step, 1)
            for k in range(3):
                pool.wait_ge(pool_step, 3 + k)
                pool.affine_select(out=sel3[0:96], in_=sel3[0:96], compare_op=ALU.not_equal, fill=1.0,
                                   base=-2 * NS * k, pattern=[[-1, 2 * NS]], channel_multiplier=1)\
                    .then_inc(pool_step, 1)
            pool.memset(eps, EPS).then_inc(pool_step, 1)
            pool.memset(nhalf, -0.5).then_inc(pool_step, 1)
            pool.wait_ge(pool_step, 8)
            pool.wait_ge(w_ld, 16 * N_W)
            for s in [s for s in POOL_AT if s in FRONT]:
                step(s, 0, 0)
            all_blocks(pool, iteration, NB)
            for s in [s for s in POOL_AT if s in BACK]:
                step(s, NB - 1, 1)


def pass2(nc, sems, arena, psum, xin_d, y_d, kr_d, B):
    GD = 8
    NB_ = 4
    LOOPS = P // (GD * NB_)
    with ExitStack() as ctx:
        def sem(n):
            return sems.named(n)
        x_ld = [sem(f"x_ld{h}") for h in range(DH)]
        t_ld = [sem(f"toeplitz_ld{k}") for k in range(NB_)]
        turned = [sem(f"turned{k}") for k in range(NB_)]
        conv_mm, out_v, out_s, y_st = sem("conv_mm"), sem("out_vector"), sem("out_scalar"), sem("y_stored")
        cv = Carve(arena)
        x2 = [cv.f32(B * P).rearrange("p (b d) -> p b d", b=B) for _ in range(DH)]
        rev, tz = ([cv.f32(GD * L).rearrange("p (d j) -> p d j", d=GD) for _ in range(NB_)] for _ in range(2))
        block = ctx.enter_context(nc.Block())
        NQ = 4

        def load_x(eng, h, first):
            for q in range(first, NQ, 2):
                w = B // NQ
                eng.dma_start(x2[h][:, q * w:(q + 1) * w], xin_d[h][:, q * w:(q + 1) * w]).then_inc(x_ld[h], 16)

        def store_y(eng, h, first):
            for q in range(first, NQ, 2):
                w = B // NQ
                eng.dma_start(y_d[:, q * w:(q + 1) * w, h * P:(h + 1) * P], x2[h][:, q * w:(q + 1) * w])\
                   .then_inc(y_st, 16)

        @block.sync
        def _(sp):
            def load_toeplitz(q, first):
                for k in range(NB_):
                    if not first:
                        sp.wait_ge(turned[k], q)
                    row = kr_d[bass.ds(q * (NB_ * GD) + k * GD, GD), :]
                    src = bass.AP(row.tensor, row.offset, [[1, P], [2 * L, GD], [1, L]])
                    sp.dma_start(rev[k], src).then_inc(t_ld[k], 16)

            load_toeplitz(0, True)
            for h in range(DH):
                load_x(sp, h, 0)
            for h in range(DH):
                with sp.Fori(1 if h == 0 else LOOPS, (h + 1) * LOOPS, 1) as q:
                    load_toeplitz(q, False)
            for h in range(DH):
                sp.wait_ge(out_v, (h + 1) * P // 8)
                sp.wait_ge(out_s, (h + 1) * P // 8)
                store_y(sp, h, 0)
            sp.wait_ge(y_st, 16 * NQ * DH)

        @block.tensor
        def _(pe):
            def products(h, q, first):
                for k in range(NB_):
                    pe.wait_ge(turned[k], q + 1)
                    for j in range(2):
                        n = 2 * k + j
                        if not first:
                            pe.wait_ge(out_s if n % 2 else out_v, q * NB_)
                        for dd in range(4):
                            d = k * GD + j * 4 + dd
                            col = x2[h][:, :, bass.ds(q * (NB_ * GD) + (d - h * P), 1)]
                            pe.matmul(psum[:, n, dd * B:(dd + 1) * B], tz[k][:, j * 4 + dd],
                                      col.rearrange("p b o -> p (b o)"), start=True, stop=True)\
                              .then_inc(conv_mm, 1)

            for h in range(DH):
                pe.wait_ge(x_ld[h], 16 * NQ)
                if h == 0:
                    products(0, 0, True)
                with pe.Fori(h * LOOPS + (h == 0), (h + 1) * LOOPS, 1) as q:
                    products(h, q, False)

        def turn(eng, copy, k, q, first):
            loaded, used = q * 16 + 16, NB_ * GD * q + (GD * (k + 1) - NB_ * GD)
            if not first:
                loaded, used = eng.to_reg(loaded), eng.to_reg(used)
            eng.wait_ge(t_ld[k], 16)
            eng.wait_ge(t_ld[k], loaded)
            if not first:
                eng.wait_ge(conv_mm, used)
            copy(tz[k], rev[k][:, :, ::-1]).then_inc(turned[k], 1)

        @block.gpsimd
        def _(pool):
            turn(pool, pool.tensor_copy, 0, 0, True)
            with pool.Fori(1, DH * LOOPS, 1) as q:
                turn(pool, pool.tensor_copy, 0, q, False)

        def read_out(eng, odd, sem_, copy, turns):
            def one_round(h, q, ahead):
                for n in range(odd, 2 * NB_, 2):
                    eng.wait_ge(conv_mm, q * (NB_ * GD) + 4 * (n + 1))
                    dst = x2[h][:, :, bass.ds(q * (NB_ * GD) + (4 * n - h * P), 4)]
                    copy(dst.rearrange("p b d -> p d b"),
                         psum[:, n, 0:4 * B].rearrange("p (d b) -> p d b", d=4)).then_inc(sem_, 1)
                    if ahead and n // 2 in turns:
                        turn(eng, copy, n // 2, q + 1, False)

            for k in turns:
                turn(eng, copy, k, 0, True)
            for h in range(DH):
                last = h == DH - 1
                with eng.Fori(h * LOOPS, (h + 1) * LOOPS - last, 1) as q:
                    one_round(h, q, True)
                if last:
                    one_round(h, DH * LOOPS - 1, False)

        @block.vector
        def _(dve):
            read_out(dve, 0, out_v, dve.tensor_copy, (1, 3))

        @block.scalar
        def _(act):
            for h in range(DH):
                load_x(act, h, 1)
            read_out(act, 1, out_s, act.copy, (2,))
            for h in range(DH):
                act.wait_ge(out_v, (h + 1) * P // 8)
                act.wait_ge(out_s, (h + 1) * P // 8)
                store_y(act, h, 1)


PER3 = dict(
    g_y=16, g_x1=16, g_xa=32, st_out=16,
    fo_mm=4, fo_mul=4, fo_add=4, xt=1, hn0=4, hn1=4, ht_mm=2, hT=2,
    f1_mm=8, gelu=8, f2_mm=2, d_res=2, d_b2=1, xo=4, xo1=4, xo3=1, x2=4,
    x2t_mm=2, mix0=2, mix1=2, mix=2, wo1_mm=1, tanh=1, h_mm=5, hb=5, wo2_mm=1,
    best=1, ties=1, ranks=1, first=1, onehot=1, m_mm=5, hm=5, w2_mm=2, r3=2,
    xf=4, xf1=4, xf3=1, x3=4,
    st_a=4, mv_a=1, ve_a=1, rs_a=1, st_o=4, mv_o=1, ve_o=1, rs_o=1, st_r=4, mv_r=1, ve_r=1, rs_r=1,
    st_f=4, mv_f=1, ve_f=1, rs_f=1, st_z=4, mv_z=1, ve_z=1, rs_z=1,
)
QC = 5

PE_STEPS = [("f1_0", 0), ("f1_1", 0), ("f2_0", 0), ("f2_1", 0), ("x2T", -1), ("film", 1), ("wo1", -1),
            ("h9_0", -1), ("wo2", -1), ("h9_1", -1), ("mask", -1), ("hT", 1), ("w2_0", -1), ("w2_1", -1)]
ACT_STEPS = [("f1_0", 0), ("f1_1", 0), ("mix", -1), ("tanh", -1), ("h9_0", -1), ("h9_1", -1), ("hT", 1)]
DVE_STEPS = [("stO", -1), ("nO", -1), ("stR", -1), ("nR", -1), ("d1_0", 0), ("mix", -1), ("film", 1),
             ("d1_1", 0), ("stA", 1), ("nA", 1), ("argmax", -1), ("hm", -1), ("r3_0", -1), ("r3_1", -1),
             ("nF", -1), ("stZ", -1), ("nZ", -1)]
POOL_STEPS = [("dO", -1), ("dR", -1), ("xt", 1), ("b2", 0), ("dA", 1), ("dF", -1), ("dZ", -1)]
PART = {("f1", 0): range(0, 4), ("f1", 1): range(4, 8), ("h9", 0): range(0, 2), ("h9", 1): range(2, QC)}


def pass3(nc, sems, i_, arena, psum, x1_d, xa_d, y_d, wf_d, out, NB):
    with ExitStack() as ctx:
        S = {n: sems.named("p3_" + n) for n in PER3}
        w_ld, consts = sems.named("p3_w_ld"), sems.named("p3_consts")
        ident_made = sems.named("p3_ident")
        cv = Carve(arena)
        fo0, fo1 = cv.f32(2 * D), cv.f32(2 * D, CT2 + 1)
        w1 = cv.f32(DH * HID).rearrange("p (k e) -> p k e", k=DH)
        w2 = cv.f32(8 * D).rearrange("p (m d) -> p m d", m=8)
        wo1 = cv.f32(DH * DM).rearrange("p (k e) -> p k e", k=DH)
        wo2 = cv.f32(NP_, DM + 1)
        w1c = cv.f32(DH * NP_ * DM).rearrange("p (k e) -> p k e", k=DH)
        w2c = cv.f32(QC * D).rearrange("p (q d) -> p q d", q=QC)
        vec = cv.f32(NV)
        wide = cv.f32(9 * D)
        ident = cv.f32(P)
        ident_b = cv.bf16(P)
        rank = cv.f32(NP_)
        nhalf = cv.f32(G)

        def blocks(n=1):
            return [cv.f32(G * D).rearrange("p (b d) -> p b d", b=G) for _ in range(n)]

        y = blocks()[0]
        x1, xt, x2 = blocks(2), blocks(2), blocks(2)
        hn, xo, xf = blocks()[0], blocks()[0], blocks()[0]
        xa0, xa1 = cv.f32(T), cv.f32(T, CT2 + 1)
        hT = cv.f32(DH * T).rearrange("p (k t) -> p k t", k=DH)
        gT = cv.f32(8 * T).rearrange("p (m t) -> p m t", m=8)
        xm = cv.f32(DH * T).rearrange("p (k t) -> p k t", k=DH)
        th = cv.f32(T, DM + 1)
        hb = cv.f32(QC * T).rearrange("p (q t) -> p q t", q=QC)
        hm = cv.f32(QC * T).rearrange("p (q t) -> p q t", q=QC)
        tied = cv.f32(G * NP_).rearrange("p (b n) -> p b n", b=G)
        best, lead = cv.f32(G), cv.f32(G)
        onehot = cv.bf16(G * NP_ + 1)[:, 0:G * NP_].rearrange("p (b n) -> p b n", b=G)
        st = {k: cv.f32(G * 6).rearrange("p (b s) -> p b s", b=G) for k in "aorfz"}
        mv = {k: cv.f32(G * 2).rearrange("p (b s) -> p b s", b=G) for k in "aorfz"}
        ve = {k: cv.f32(G) for k in "aorfz"}
        rs = {k: cv.f32(G) for k in "aorfz"}
        N_CONST = 6
        N_W = 11
        REST = DM + NP_

        def need(eng, name, i, k):
            count = i * PER3[name] + k
            if not isinstance(count, int) or count > 0:
                eng.wait_ge(S[name], count)

        def need_apart(eng, *what):
            counts = [(name, i * PER3[name] + k) for name, i, k in what]
            counts = [(name, n if isinstance(n, int) else eng.to_reg(n)) for name, n in counts]
            eng.wait_ge(w_ld, 16 * N_W)
            for name, count in counts:
                if not isinstance(count, int) or count > 0:
                    eng.wait_ge(S[name], count)

        def following(i):
            return i if isinstance(i, int) and i == NB - 1 else i + 1

        def seqs(v):
            return v.rearrange("p (b t) -> p b t", b=G)

        def over_seqs(n):
            return wide[:, n * D:(n + 1) * D][:, None, :].to_broadcast([P, G, D])

        def run(eng, step, order):
            def iteration(i, par, ahead, behind):
                for name, off in order:
                    if (off == 1 and not ahead) or (off == -1 and not behind):
                        continue
                    step(name, i + off, (par + off) % 2)

            for name, off in order:
                if off == 1:
                    step(name, 0, 0)
            all_blocks(eng, iteration, NB)
            for name, off in order:
                if off == -1:
                    step(name, NB - 1, 1)

        block = ctx.enter_context(nc.Block())

        @block.sync
        def _(sp):
            for dst, src in (
                (fo0, wf_d[0:P, 2 * D:MOD]), (fo1, wf_d[P:CTX + 1, 2 * D:MOD]), (w1, i_["w1"]), (w2, i_["w2"]),
                (wo1, i_["wo1"]), (wo2, i_["wo2"]), (w1c, i_["w1c"]), (w2c[:, 0:4], i_["w2c"][:, 0:4]),
                (w2c[0:REST, 4], i_["w2c"][0:REST, 4]), (vec, i_["vec"]),
                (wide, i_["wide"][0:1, 0:9 * D].to_broadcast([P, 9 * D])),
            ):
                sp.dma_start(dst, src).then_inc(w_ld, 16)

            def step(name, i, par):
                if name == "load":
                    need(sp, "xt", i - 1, 1)
                    sp.dma_start(y, y_d[:, bass.ts(i, G), :]).then_inc(S["g_y"], 16)
                    need(sp, "xo3", i - 2, 1)
                    sp.dma_start(x1[par], x1_d[:, bass.ts(i, G), :]).then_inc(S["g_x1"], 16)
                    need(sp, "fo_mm", i - 1, G)
                    sp.dma_start(xa0, xa_d[0:P, bass.ts(i, T)]).then_inc(S["g_xa"], 16)
                    sp.dma_start(xa1[0:CT2], xa_d[P:CTX, bass.ts(i, T)]).then_inc(S["g_xa"], 16)
                elif name == "store":
                    need(sp, "x3", i, G)
                    sp.dma_start(out[:, bass.ts(i, G), :], xf).then_inc(S["st_out"], 16)

            run(sp, step, [("load", 1), ("store", -1)])
            sp.wait_ge(S["st_out"], NB * 16)

        @block.tensor
        def _(pe):
            def step(name, i, par):
                if name == "film":
                    need(pe, "g_xa", i, 32)
                    for b in range(G):
                        if b >= 2:
                            need(pe, "fo_add", i, b - 1)
                        else:
                            need(pe, "hT", i - 1, DH)
                        ps = psum[:, 4 + b % 2]
                        pe.matmul(ps, xa0[:, b * L:(b + 1) * L], fo0, start=True, stop=False)
                        pe.matmul(ps, xa1[0:CT2 + 1, b * L:(b + 1) * L], fo1, start=False, stop=True)\
                          .then_inc(S["fo_mm"], 1)
                elif name == "hT":
                    need(pe, "hn1", i, G)
                    need(pe, "fo_add", i, G)
                    for k in range(DH):
                        for b in range(G):
                            mm = pe.transpose(psum[:, 4 + k, b * L:(b + 1) * L], hn[:, b, k * P:(k + 1) * P], ident)
                        mm.then_inc(S["ht_mm"], 1)
                elif name[:2] == "f1":
                    if name == "f1_0":
                        need(pe, "hT", i, DH)
                        need(pe, "hb", i - 2, QC)
                    for m in PART["f1", int(name[-1])]:
                        if m >= 2:
                            need(pe, "gelu", i, m - 1)
                        for k in range(DH):
                            mm = pe.matmul(psum[:, m % 2], w1[:, k, m * P:(m + 1) * P], hT[:, k],
                                           start=k == 0, stop=k == DH - 1)
                        mm.then_inc(S["f1_mm"], 1)
                elif name[:2] == "f2":
                    o = int(name[-1])
                    if o == 0:
                        need(pe, "gelu", i, 8)
                    need(pe, "r3", i - 2, o + 1)
                    for bb in range(2):
                        b = 2 * o + bb
                        for m in range(8):
                            mm = pe.matmul(psum[:, 2 + o, bb * D:(bb + 1) * D], gT[:, m, b * L:(b + 1) * L],
                                           w2[:, m], start=m == 0, stop=m == 7)
                    mm.then_inc(S["f2_mm"], 1)
                elif name == "x2T":
                    need(pe, "x2", i, G)
                    need(pe, "hm", i - 1, QC)
                    for k in range(DH):
                        for b in range(G):
                            mm = pe.transpose(psum[:, 6 + k, b * L:(b + 1) * L], x2[par][:, b, k * P:(k + 1) * P],
                                              ident)
                        mm.then_inc(S["x2t_mm"], 1)
                elif name == "wo1":
                    need(pe, "mix", i, DH)
                    for k in range(DH):
                        mm = pe.matmul(psum[0:DM, 6], wo1[:, k], xm[:, k], start=k == 0, stop=k == DH - 1)
                    mm.then_inc(S["wo1_mm"], 1)
                elif name[:2] == "h9":
                    if name == "h9_0":
                        need(pe, "gelu", following(i), 8)
                    for q in PART["h9", int(name[-1])]:
                        if q >= 2:
                            need(pe, "hb", i, q - 1)
                        rows = P if q < 4 else DM
                        for k in range(DH):
                            mm = pe.matmul(psum[0:rows, q % 2], w1c[:, k, q * P:q * P + rows], xm[:, k],
                                           start=k == 0, stop=k == DH - 1)
                        mm.then_inc(S["h_mm"], 1)
                elif name == "wo2":
                    need(pe, "tanh", i, 1)
                    for b in range(G):
                        mm = pe.matmul(psum[:, 7, b * NP_:(b + 1) * NP_], th[:, b * L:(b + 1) * L], wo2,
                                       start=True, stop=True)
                    mm.then_inc(S["wo2_mm"], 1)
                elif name == "mask":
                    need(pe, "onehot", i, 1)
                    for q in range(QC):
                        if q >= 2:
                            need(pe, "hm", i, q - 1)
                        for b in range(G):
                            o = psum[:, 6 + q % 2, b * L:(b + 1) * L]
                            if q < 4:
                                for k in range(2):
                                    path = onehot[:, b, 2 * q + k:2 * q + k + 1].to_broadcast([P, DM])
                                    mm = pe.matmul(o[k * DM:(k + 1) * DM], path, ident_b, start=True, stop=True)
                            else:
                                pe.matmul(o[0:DM], onehot[:, b, 8:9].to_broadcast([P, DM]), ident_b,
                                          start=True, stop=True)
                                mm = pe.matmul(o[DM:REST], onehot[:, b], ident_b, start=True, stop=True)
                        mm.then_inc(S["m_mm"], 1)
                elif name[:2] == "w2":
                    o = int(name[-1])
                    if o == 0:
                        need(pe, "hm", i, QC)
                    need(pe, "d_res", following(i), o + 1)
                    for bb in range(2):
                        b = 2 * o + bb
                        for q in range(QC):
                            rows = P if q < 4 else REST
                            mm = pe.matmul(psum[:, 2 + o, bb * D:(bb + 1) * D], hm[0:rows, q, b * L:(b + 1) * L],
                                           w2c[0:rows, q], start=q == 0, stop=q == QC - 1)
                    mm.then_inc(S["w2_mm"], 1)

            pe.wait_ge(consts, N_CONST)
            pe.wait_ge(w_ld, 16 * N_W)
            run(pe, step, PE_STEPS)

        @block.scalar
        def _(act):
            def step(name, i, par):
                if name == "hT":
                    need(act, "f1_mm", i - 1, 8)
                    for k in range(DH):
                        need(act, "ht_mm", i, k + 1)
                        act.copy(hT[:, k], psum[:, 4 + k]).then_inc(S["hT"], 1)
                elif name[:2] == "f1":
                    if name == "f1_0":
                        need(act, "f2_mm", i - 1, 2)
                    for m in PART["f1", int(name[-1])]:
                        need(act, "f1_mm", i, m + 1)
                        act.activation(gT[:, m], psum[:, m % 2], ACT.Gelu, bias=vec[:, V_B1 + m:V_B1 + m + 1])\
                            .then_inc(S["gelu"], 1)
                elif name == "mix":
                    need(act, "h_mm", i - 1, QC)
                    for k in range(DH):
                        need(act, "x2t_mm", i, k + 1)
                        act.activation(xm[:, k], psum[:, 6 + k], ACT.Identity,
                                       scale=vec[:, V_MIX + 3 * k + 1:V_MIX + 3 * k + 2]).then_inc(S["mix0"], 1)
                elif name == "tanh":
                    need(act, "wo1_mm", i, 1)
                    need(act, "wo2_mm", i - 1, 1)
                    act.activation(th[0:DM], psum[0:DM, 6], ACT.Tanh, bias=vec[0:DM, V_BO1:V_BO1 + 1])\
                        .then_inc(S["tanh"], 1)
                elif name[:2] == "h9":
                    if name == "h9_0":
                        need(act, "hm", i - 1, QC)
                    for q in PART["h9", int(name[-1])]:
                        rows = P if q < 4 else DM
                        need(act, "h_mm", i, q + 1)
                        act.activation(hb[0:rows, q], psum[0:rows, q % 2], ACT.Identity,
                                       bias=vec[0:rows, V_FB1 + q:V_FB1 + q + 1]).then_inc(S["hb"], 1)

            act.wait_ge(w_ld, 16 * N_W)
            act.wait_ge(consts, N_CONST)
            run(act, step, ACT_STEPS)

        @block.vector
        def _(dve):
            def stats(i, src, k):
                need(dve, "ve_" + k, i - 1, 1)
                need(dve, "rs_" + k, i - 1, 1)
                for b in range(G):
                    dve.bn_stats(st[k][:, b], src[:, b]).then_inc(S["st_" + k], 1)
                need_apart(dve, ("st_" + k, i, G))
                for b in range(G):
                    a = dve.bn_aggr(mv[k][:, b], st[k][:, b])
                a.then_inc(S["mv_" + k], 1)

            def normed(i, dst, src, k, sem):
                need(dve, "rs_" + k, i, 1)
                need(dve, "mv_" + k, i, 1)
                for b in range(G):
                    dve.tensor_scalar(dst[:, b], src[:, b], mv[k][:, b, 0:1], rs[k][:, b:b + 1],
                                      ALU.subtract, ALU.mult).then_inc(S[sem], 1)

            def normed_affine(i, dst, src, k, first, second, gain, bias):
                def row(n):
                    return wide[:, n * D:(n + 1) * D]

                need(dve, "rs_" + k, i, 1)
                for b in range(G):
                    dve.scalar_tensor_tensor(out=dst[:, b], in0=src[:, b], scalar=mv[k][:, b, 0:1], in1=row(gain),
                                             op0=ALU.subtract, op1=ALU.mult).then_inc(S[first], 1)
                for b in range(G):
                    need(dve, first, i, b + 1)
                    dve.scalar_tensor_tensor(out=dst[:, b], in0=dst[:, b], scalar=rs[k][:, b:b + 1], in1=row(bias),
                                             op0=ALU.mult, op1=ALU.add).then_inc(S[second], 1)

            def pair(v, o):
                return v[:, 2 * o:2 * o + 2]

            def halves(ps):
                return ps.rearrange("p (b d) -> p b d", b=2)

            def step(name, i, par):
                if name == "film":
                    need(dve, "g_y", i, 16)
                    for b in range(G):
                        ps = psum[:, 4 + b % 2]
                        need(dve, "fo_mm", i, b + 1)
                        dve.tensor_tensor(y[:, b], y[:, b], ps[:, 0:D], ALU.mult).then_inc(S["fo_mul"], 1)
                        need(dve, "fo_mul", i, b + 1)
                        dve.tensor_tensor(y[:, b], y[:, b], ps[:, D:2 * D], ALU.add).then_inc(S["fo_add"], 1)
                elif name == "stA":
                    need(dve, "xt", i, 1)
                    stats(i, xt[par], "a")
                elif name == "nA":
                    need(dve, "ht_mm", i - 1, DH)
                    normed_affine(i, hn, xt[par], "a", "hn0", "hn1", W_GFFN, W_BFFN)
                elif name[:2] == "d1":
                    o = int(name[-1])
                    need(dve, "f2_mm", i, o + 1)
                    dve.tensor_tensor(pair(xt[par], o), halves(psum[:, 2 + o]), pair(xt[par], o), ALU.add)\
                       .then_inc(S["d_res"], 1)
                elif name == "stO":
                    need(dve, "d_b2", i, 1)
                    stats(i, xt[par], "o")
                elif name == "nO":
                    need(dve, "x2", i - 1, G)
                    normed_affine(i, xo, xt[par], "o", "xo", "xo1", W_GOUT, W_BOUT)
                    need(dve, "xo1", i, G)
                    dve.tensor_tensor(xo, xo, x1[par], ALU.add).then_inc(S["xo3"], 1)
                elif name == "stR":
                    need(dve, "xo3", i, 1)
                    stats(i, xo, "r")
                elif name == "nR":
                    normed(i, x2[par], xo, "r", "x2")
                elif name == "mix":
                    for k in range(DH):
                        need(dve, "mix0", i, k + 1)
                        src, dst = seqs(psum[:, 6 + k]), seqs(xm[:, k])
                        w = V_MIX + 3 * k
                        dve.scalar_tensor_tensor(out=dst[:, :, 1:L], in0=src[:, :, 0:L - 1], scalar=vec[:, w:w + 1],
                                                 in1=dst[:, :, 1:L], op0=ALU.mult, op1=ALU.add).then_inc(S["mix1"], 1)
                    for k in range(DH):
                        need(dve, "mix1", i, k + 1)
                        src, dst = seqs(psum[:, 6 + k]), seqs(xm[:, k])
                        w = V_MIX + 3 * k
                        dve.scalar_tensor_tensor(out=dst[:, :, 0:L - 1], in0=src[:, :, 1:L],
                                                 scalar=vec[:, w + 2:w + 3], in1=dst[:, :, 0:L - 1],
                                                 op0=ALU.mult, op1=ALU.add).then_inc(S["mix"], 1)
                elif name == "argmax":
                    ps = psum[:, 7, 0:G * NP_].rearrange("p (b n) -> p b n", b=G)
                    need(dve, "wo2_mm", i, 1)
                    dve.tensor_reduce(best, ps, AX.X, ALU.max).then_inc(S["best"], 1)
                    need(dve, "best", i, 1)
                    dve.tensor_tensor(tied, ps, best[:, :, None].to_broadcast([P, G, NP_]), ALU.is_equal)\
                       .then_inc(S["ties"], 1)
                    need(dve, "ties", i, 1)
                    dve.tensor_tensor(tied, tied, rank[:, None, :].to_broadcast([P, G, NP_]), ALU.mult)\
                       .then_inc(S["ranks"], 1)
                    need(dve, "ranks", i, 1)
                    dve.tensor_reduce(lead, tied, AX.X, ALU.max).then_inc(S["first"], 1)
                    need(dve, "first", i, 1)
                    need(dve, "m_mm", i - 1, QC)
                    dve.tensor_tensor(onehot, tied, lead[:, :, None].to_broadcast([P, G, NP_]), ALU.is_equal)\
                       .then_inc(S["onehot"], 1)
                elif name == "hm":
                    need(dve, "w2_mm", i - 1, 2)
                    for q in range(QC):
                        rows = P if q < 4 else REST
                        need(dve, "hb", i, q + 1)
                        need(dve, "m_mm", i, q + 1)
                        dve.tensor_tensor(hm[0:rows, q], hb[0:rows, q], psum[0:rows, 6 + q % 2], ALU.mult)\
                           .then_inc(S["hm"], 1)
                elif name[:2] == "r3":
                    o = int(name[-1])
                    if o == 0:
                        need(dve, "st_out", i - 1, 16)
                    need(dve, "w2_mm", i, o + 1)
                    dve.tensor_tensor(pair(xf, o), halves(psum[:, 2 + o]), pair(x2[par], o), ALU.add)\
                       .then_inc(S["r3"], 1)
                    if o == 1:
                        need(dve, "r3", i, 2)
                        stats(i, xf, "f")
                elif name == "nF":
                    normed_affine(i, xf, xf, "f", "xf", "xf1", W_GAM, W_BET)
                    need(dve, "xf1", i, G)
                    dve.tensor_tensor(xf, xf, x2[par], ALU.add).then_inc(S["xf3"], 1)
                elif name == "stZ":
                    need(dve, "xf3", i, 1)
                    stats(i, xf, "z")
                elif name == "nZ":
                    normed(i, xf, xf, "z", "x3")

            dve.memset(xa1[CT2:CT2 + 1], 1.0).then_inc(consts, 1)
            dve.memset(th[DM:DM + 1], 1.0).then_inc(consts, 1)
            dve.memset(hb[DM:P, 4], 1.0).then_inc(consts, 1)
            dve.wait_ge(w_ld, 16 * N_W)
            dve.wait_ge(consts, N_CONST)
            run(dve, step, DVE_STEPS)

        @block.gpsimd
        def _(pool):
            def deviation(i, k):
                need_apart(pool, ("mv_" + k, i, 1))
                pool.tensor_scalar(ve[k], mv[k][:, :, 1], EPS, None, ALU.add).then_inc(S["ve_" + k], 1)
                need(pool, "ve_" + k, i, 1)
                pool.tensor_tensor(rs[k], ve[k], nhalf, ALU.pow).then_inc(S["rs_" + k], 1)

            def step(name, i, par):
                if name == "xt":
                    need(pool, "fo_add", i, G)
                    need(pool, "g_x1", i, 16)
                    need(pool, "xo", i - 2, G)
                    pool.tensor_tensor(xt[par], y, x1[par], ALU.add).then_inc(S["xt"], 1)
                elif name == "dA":
                    deviation(i, "a")
                elif name == "b2":
                    need(pool, "d_res", i, 2)
                    pool.tensor_tensor(xt[par], xt[par], over_seqs(W_B2), ALU.add).then_inc(S["d_b2"], 1)
                elif name == "dO":
                    deviation(i, "o")
                elif name == "dR":
                    deviation(i, "r")
                elif name == "dF":
                    deviation(i, "f")
                elif name == "dZ":
                    deviation(i, "z")

            identity(nc, pool, ident, ident_made)
            pool.wait_ge(ident_made, 2)
            pool.tensor_copy(ident_b, ident).then_inc(consts, 1)
            pool.iota(rank, [[-1, NP_]], base=NP_, channel_multiplier=0,
                      allow_small_or_imprecise_dtypes=True).then_inc(consts, 1)
            pool.memset(nhalf, -0.5).then_inc(consts, 1)
            pool.wait_ge(w_ld, 16 * N_W)
            pool.wait_ge(consts, N_CONST)
            run(pool, step, POOL_STEPS)


_OUT = "out_0_dram"


def lay_out(inputs, B):
    import numpy as np
    a = {k: np.asarray(v) for k, v in inputs.items()}
    f = {k[len("L0_"):]: v for k, v in a.items() if k.startswith("L0_")}

    def chunks(v, rows=P):
        return np.ascontiguousarray(v.reshape(-1, rows, v.shape[-1]).transpose(1, 0, 2))

    x, c = a["x"][:B], a["ctx_768"][:B]
    conv_w = f["attn_conv_w"].reshape(C, P, 4).transpose(1, 0, 2).reshape(P, 16)

    def cols(v):
        return v.reshape(-1, P).T

    fb1 = np.zeros((P, 5), np.float32)
    fb1[:, 0:4] = f["ffn_b1"].reshape(-1)[0:512].reshape(4, P).T
    fb1[0:DM, 4] = f["ffn_b1"].reshape(-1)[512:]
    bo1 = np.zeros((P, 1), np.float32)
    bo1[0:DM, 0] = f["ffn_bo1"]
    vec = np.concatenate([
        conv_w, cols(f["attn_conv_b"]), cols(f["attn_dt_proj_b"]), cols(f["attn_D"]),
        f["attn_A_log"].reshape(C, P, NS).transpose(1, 0, 2).reshape(P, C * NS), cols(f["xattn_b1"]),
        f["ffn_mix_kernel"].reshape(3, DH, P).transpose(2, 1, 0).reshape(P, 6), fb1, bo1], axis=1)
    assert vec.shape == (P, NV)
    wide = np.concatenate([f["xattn_g_norm_in"], f["xattn_b_norm_in"], f["xattn_g_ffn"], f["xattn_b_ffn"],
                           f["xattn_b2"], f["xattn_g_norm_out"], f["xattn_b_norm_out"], f["ffn_gamma"],
                           f["ffn_beta"], f["xattn_mod_gate"].reshape(1)])[None]
    w2c = np.zeros((P, QC, D), np.float32)
    flat = f["ffn_W2"].reshape(NP_ * DM, D)
    w2c[:, 0:4] = flat[0:512].reshape(4, P, D).transpose(1, 0, 2)
    w2c[0:DM, 4] = flat[512:]
    w2c[DM:DM + NP_, 4] = f["ffn_b2"]
    w1c = f["ffn_W1"].transpose(1, 0, 2).reshape(D, NP_ * DM)
    r = {
        "x": x.transpose(1, 0, 2), "xT": x.reshape(B * L, DH, P).transpose(2, 1, 0),
        "ctx": c.transpose(1, 0, 2), "ctxT": c.reshape(B * L, CTX).T,
        "vmask": a["mask_BxS2_bf1"][:B].reshape(1, B * L).view(np.uint8),
        "tmask": np.ascontiguousarray(a["mask_BxS_bf1"][:B].T).view(np.uint8),
        "in_proj": chunks(f["attn_in_proj_w"].T), "x_proj": chunks(f["attn_x_proj_w"].T),
        "dt_proj": f["attn_dt_proj_w"].T, "out_proj": chunks(f["attn_out_proj_w"].T),
        "wq": chunks(f["xattn_Wq"]), "wk": f["xattn_Wk"], "wv": chunks(f["xattn_Wv"].T),
        "wf": chunks(np.concatenate([f["xattn_W_film_in"], f["xattn_W_film_out"]], axis=1)),
        "film_b": np.concatenate([f["xattn_b_film_in"], f["xattn_b_film_out"]])[None],
        "s4": np.stack([f["xattn_A_re"].T, f["xattn_A_im"].T, f["xattn_C_re"].T, f["xattn_C_im"].T], axis=1),
        "log_dt": f["xattn_log_dt"][None], "d_skip": f["xattn_D_skip"][None],
        "w1": chunks(f["xattn_W1"]), "w2": chunks(f["xattn_W2"]), "wo1": chunks(f["ffn_Wo1"]),
        "wo2": np.concatenate([f["ffn_Wo2"], f["ffn_bo2"][None]]), "w1c": chunks(w1c), "w2c": w2c,
        "vec": vec, "wide": wide,
    }
    return {k: np.ascontiguousarray(v) for k, v in r.items()}


def kernel(**inputs):
    import concourse.bacc as bacc
    import numpy as np
    from concourse.bass_utils import run_bass_kernel_spmd

    B = inputs["x"].shape[0]
    arrays = lay_out(inputs, B)
    nc = bacc.Bacc("TRN2", target_bir_lowering=False, num_devices=1)
    i_ = {k: nc.dram_tensor(f"in_{k}_dram", v.shape, mybir.dt.from_np(v.dtype), kind="ExternalInput").ap()
          for k, v in arrays.items()}
    out = nc.dram_tensor(_OUT, (L, B, D), F32, kind="ExternalOutput").ap()
    decoder_layer(nc, i_, out, B // G)
    r = run_bass_kernel_spmd(nc, [{f"in_{k}_dram": v for k, v in arrays.items()}], core_ids=[0])
    return np.ascontiguousarray(r.results[0][_OUT].transpose(1, 0, 2))
```
